# Optimizing a Trainium2 kernel written in Bass

```python
import numpy as np
import jax
import jax.numpy as jnp

def _softmax(x, axis=-1):
    return jax.nn.softmax(x, axis=axis)

def _gelu(x):
    return jax.nn.gelu(x, approximate=True)

def _silu(x):
    return jax.nn.silu(x)

def _sigmoid(x):
    return jax.nn.sigmoid(x)

def _layernorm(x, axis=-1, eps=1e-05):
    m = jnp.mean(x, axis=axis, keepdims=True)
    v = jnp.var(x, axis=axis, keepdims=True)
    return (x - m) / jnp.sqrt(v + eps)

def _scatter_add(tgt, idx, src, axis=0):
    return tgt.at[idx].add(src)

def _segment_sum(src, seg, n):
    return jax.ops.segment_sum(src, seg, n)
kernel_name = 'mk_decoder_postln_d1_seqx_r8_2f1f39'

def setup_inputs(seed: int=0):
    np.random.seed(seed)
    _w = jnp.asarray

    def _rec_inputs():
        import jax
        import jax.numpy as jnp
        _rk = jax.random.key(seed)
        x = 7.22e-05 + 1 * jax.random.normal(jax.random.fold_in(_rk, 1), (16, 64, 512), jnp.float32)
        _lenS = 64 - jax.random.randint(jax.random.fold_in(_rk, 7), (16,), 0, max(1, 64 // 4) + 1, jnp.int32)
        _lenS2 = 64 - jax.random.randint(jax.random.fold_in(_rk, 8), (16,), 0, max(1, 64 // 4) + 1, jnp.int32)
        _ctx_4096P = jax.random.normal(jax.random.fold_in(_rk, 11), (16, 16, 512), jnp.float32)
        _ctx_4096c = jax.random.dirichlet(jax.random.fold_in(_rk, 511), 0.3 * jnp.ones((16,), jnp.float32), (16, 64))
        _ctx_4096t = jnp.einsum('bsk,bkd->bsd', _ctx_4096c, _ctx_4096P)
        _ctx_4096t = _ctx_4096t * jax.lax.rsqrt(jnp.mean(jnp.square(_ctx_4096t)) + 1e-12) * 0.953939
        ctx_4096 = 4.13588e-05 + 0.999923 * (_ctx_4096t + 0.3 * jax.random.normal(jax.random.fold_in(_rk, 611), (16, 64, 512), jnp.float32))
        return (x, ctx_4096)
    x, ctx_4096 = _rec_inputs()

    def _L0_attn_setup():
        import jax, jax.numpy as jnp
        import numpy as np
        K_FACTOR = 0.5
        key = jax.random.key(seed)
        k1, k2, k3, k4 = jax.random.split(key, 4)
        B, S, H, I = (1, 256, 512, 1376)
        x = jax.random.normal(k1, (B, S, H), dtype=jnp.float32)
        w_gate = jax.random.normal(k2, (I, H), dtype=jnp.float32) * 0.02
        w_up = jax.random.normal(k3, (I, H), dtype=jnp.float32) * 0.02
        w_down = jax.random.normal(k4, (H, I), dtype=jnp.float32) * 0.02
        return {'x': x, 'w_gate': w_gate, 'w_up': w_up, 'w_down': w_down}
    _L0_attn_all = _L0_attn_setup()
    _L0_attn_in = {k: v for k, v in _L0_attn_all.items() if k in ('w_gate', 'w_up', 'w_down')}
    del _L0_attn_all

    def _L0_xattn_setup():
        import jax, jax.numpy as jnp
        import numpy as np
        import math
        D_MODEL = 128
        NHEAD = 16
        MAX_SUP = 4
        DK = D_MODEL // NHEAD
        DM = D_MODEL * MAX_SUP
        B, S = (2, 128)
        key = jax.random.key(seed)
        ks = jax.random.split(key, 12)
        std = 0.02
        inp = {'q': jax.random.normal(ks[0], (B, S, DM), jnp.float32), 'k': jax.random.normal(ks[1], (B, S, DM), jnp.float32), 'v': jax.random.normal(ks[2], (B, S, DM), jnp.float32), 'Wq': jax.random.normal(ks[3], (DM, DM), jnp.float32) * std, 'bq': jnp.zeros((DM,), jnp.float32), 'Wk': jax.random.normal(ks[4], (DM, DM), jnp.float32) * std, 'bk': jnp.zeros((DM,), jnp.float32), 'Wv': jax.random.normal(ks[5], (DM, DM), jnp.float32) * std, 'bv': jnp.zeros((DM,), jnp.float32), 'interference': jax.random.normal(ks[6], (NHEAD, MAX_SUP, MAX_SUP), jnp.float32), 'amp': jnp.ones((1,), jnp.float32), 'Wo': jax.random.normal(ks[7], (DM, DM), jnp.float32) * std, 'bo': jnp.zeros((DM,), jnp.float32)}
        return inp
    _L0_xattn_all = _L0_xattn_setup()
    _L0_xattn_in = {k: v for k, v in _L0_xattn_all.items() if k in ('Wq', 'bq', 'Wk', 'bk', 'Wv', 'bv', 'interference', 'amp', 'Wo', 'bo')}
    del _L0_xattn_all

    def _L0_ffn_setup():
        import jax, jax.numpy as jnp
        import numpy as np
        B, S, D, O, E, R = (2, 512, 512, 512, 8, 16)
        TOP_K = 2
        SCALING = 32.0 / 16.0
        key = jax.random.key(seed)
        k = jax.random.split(key, 6)
        x = jax.random.normal(k[0], (B, S, D), dtype=jnp.float32)
        W_base = jax.random.normal(k[1], (O, D), dtype=jnp.float32) * 0.02
        b_base = jax.random.normal(k[2], (O,), dtype=jnp.float32) * 0.02
        W_router = jax.random.normal(k[3], (E, D), dtype=jnp.float32) * 0.01
        lora_A = jax.random.normal(k[4], (E, R, D), dtype=jnp.float32) * (1.0 / np.sqrt(D))
        lora_B = jax.random.normal(k[5], (E, O, R), dtype=jnp.float32) * 0.02
        return {'x': x, 'W_base': W_base, 'b_base': b_base, 'W_router': W_router, 'lora_A': lora_A, 'lora_B': lora_B}
    _L0_ffn_all = _L0_ffn_setup()
    _L0_ffn_in = {k: v for k, v in _L0_ffn_all.items() if k in ('W_base', 'b_base', 'W_router', 'lora_A', 'lora_B')}
    del _L0_ffn_all
    return {'x': x, 'ctx_4096': ctx_4096, 'L0_attn_w_gate': _L0_attn_in['w_gate'], 'L0_attn_w_up': _L0_attn_in['w_up'], 'L0_attn_w_down': _L0_attn_in['w_down'], 'L0_xattn_Wq': _L0_xattn_in['Wq'], 'L0_xattn_bq': _L0_xattn_in['bq'], 'L0_xattn_Wk': _L0_xattn_in['Wk'], 'L0_xattn_bk': _L0_xattn_in['bk'], 'L0_xattn_Wv': _L0_xattn_in['Wv'], 'L0_xattn_bv': _L0_xattn_in['bv'], 'L0_xattn_interference': _L0_xattn_in['interference'], 'L0_xattn_amp': _L0_xattn_in['amp'], 'L0_xattn_Wo': _L0_xattn_in['Wo'], 'L0_xattn_bo': _L0_xattn_in['bo'], 'L0_ffn_W_base': _L0_ffn_in['W_base'], 'L0_ffn_b_base': _L0_ffn_in['b_base'], 'L0_ffn_W_router': _L0_ffn_in['W_router'], 'L0_ffn_lora_A': _L0_ffn_in['lora_A'], 'L0_ffn_lora_B': _L0_ffn_in['lora_B']}

def reference(x, ctx_4096, L0_attn_w_gate, L0_attn_w_up, L0_attn_w_down, L0_xattn_Wq, L0_xattn_bq, L0_xattn_Wk, L0_xattn_bk, L0_xattn_Wv, L0_xattn_bv, L0_xattn_interference, L0_xattn_amp, L0_xattn_Wo, L0_xattn_bo, L0_ffn_W_base, L0_ffn_b_base, L0_ffn_W_router, L0_ffn_lora_A, L0_ffn_lora_B):
    import jax
    import jax.numpy as jnp

    def _L0_attn_ref(x, w_gate, w_up, w_down):
        import jax, jax.numpy as jnp
        import numpy as np
        K_FACTOR = 0.5
        s = jax.nn.silu(jnp.einsum('bsh,ih->bsi', x, w_gate))
        B, S, I = s.shape
        k = int(K_FACTOR * I)
        _, idx = jax.lax.top_k(-jnp.abs(s), k)
        flat = s.reshape(B * S, I)
        rows = jnp.arange(B * S)[:, None]
        flat = flat.at[rows, idx.reshape(B * S, k)].set(0.0)
        s = flat.reshape(B, S, I)
        s = s * jnp.einsum('bsh,ih->bsi', x, w_up)
        return jnp.einsum('bsi,hi->bsh', s, w_down)

    def _L0_xattn_ref(q, k, v, Wq, bq, Wk, bk, Wv, bv, interference, amp, Wo, bo):
        import jax, jax.numpy as jnp
        import numpy as np
        import math
        D_MODEL = 128
        NHEAD = 16
        MAX_SUP = 4
        DK = D_MODEL // NHEAD
        DM = D_MODEL * MAX_SUP
        B, S = (2, 128)
        b, s, dm = q.shape
        H, M = (interference.shape[0], interference.shape[1])
        dk = dm // (H * M)

        def proj(x, W, bias):
            y = x @ W.T + bias
            y = y.reshape(b, s, H, dk, M)
            return jnp.transpose(y, (0, 2, 1, 3, 4))
        qh = proj(q, Wq, bq)
        kh = proj(k, Wk, bk)
        vh = proj(v, Wv, bv)

        def interfere(x):
            return x + 0.1 * amp[0] * jnp.einsum('bhsdi,hij->bhsdj', x, interference)
        qh, kh, vh = (interfere(qh), interfere(kh), interfere(vh))
        scores = jnp.einsum('bhqdm,bhkdm->bhqkm', qh, kh) / math.sqrt(dk)
        weights = jax.nn.softmax(scores, axis=3)
        out = jnp.einsum('bhqkm,bhkdm->bhqdm', weights, vh)
        out = jnp.transpose(out, (0, 2, 1, 3, 4)).reshape(b, s, dm)
        return out @ Wo.T + bo

    def _L0_ffn_ref(x, W_base, b_base, W_router, lora_A, lora_B):
        import jax, jax.numpy as jnp
        import numpy as np
        B, S, D, O, E, R = (2, 512, 512, 512, 8, 16)
        TOP_K = 2
        SCALING = 32.0 / 16.0
        d = x.shape[-1]
        n_experts = W_router.shape[0]
        xf = x.reshape(-1, d)
        logits = xf @ W_router.T
        probs = jax.nn.softmax(logits, axis=-1)
        topk_p, topk_i = jax.lax.top_k(probs, TOP_K)
        topk_p = topk_p / jnp.sum(topk_p, axis=-1, keepdims=True)
        w = jnp.sum(jax.nn.one_hot(topk_i, n_experts, dtype=xf.dtype) * topk_p[..., None], axis=1)
        h = jnp.einsum('td,erd->ter', xf, lora_A)
        lora_out = jnp.einsum('ter,eor,te->to', h, lora_B, w) * SCALING
        base = x @ W_base.T + b_base
        return base + lora_out.reshape(x.shape[:-1] + (W_base.shape[0],))
    x = _layernorm(x + _L0_attn_ref(x, L0_attn_w_gate, L0_attn_w_up, L0_attn_w_down), axis=-1)
    x = _layernorm(x + _L0_xattn_ref(x, ctx_4096, ctx_4096, L0_xattn_Wq, L0_xattn_bq, L0_xattn_Wk, L0_xattn_bk, L0_xattn_Wv, L0_xattn_bv, L0_xattn_interference, L0_xattn_amp, L0_xattn_Wo, L0_xattn_bo), axis=-1)
    x = _layernorm(x + _L0_ffn_ref(x, L0_ffn_W_base, L0_ffn_b_base, L0_ffn_W_router, L0_ffn_lora_A, L0_ffn_lora_B), axis=-1)
    return x

_drawn_inputs = setup_inputs


def setup_inputs(seed=0):
    import zlib

    import numpy as np

    out = dict(_drawn_inputs(seed))
    spreads = {'L0_xattn_bq': (0.0, 0.8),
     'L0_xattn_bk': (0.0, 0.8),
     'L0_xattn_bv': (0.0, 0.1),
     'L0_xattn_bo': (0.0, 0.1)}
    factors = {'L0_xattn_Wq': 4.485, 'L0_xattn_Wk': 4.614, 'L0_ffn_b_base': 3.254}
    for name, (base, spread) in spreads.items():
        noise = np.random.default_rng([zlib.crc32(name.encode()), seed]).standard_normal(out[name].shape)
        drawn = base * np.exp(spread * noise) if base else spread * noise
        out[name] = jnp.asarray(drawn.astype(out[name].dtype))
    for name, factor in factors.items():
        out[name] = (out[name] * factor).astype(out[name].dtype)
    return out
```

```python
from contextlib import ExitStack

import concourse.bass as bass
from concourse import mybir

P = 128
F32 = mybir.dt.float32
BF16 = mybir.dt.bfloat16
I32 = mybir.dt.int32
ALU = mybir.AluOpType
ACT = mybir.ActivationFunctionType
AX = mybir.AxisListType
BIG = 1.0e38
EPS = 1e-5
LORA_SCALING = 2.0

GUESS, SLOPE = 0.78, 0.83
STEPS = (1.0, 1.0, 0.5)
COUNTS = len(STEPS) + 1
CANDIDATES = 16


def decoder_kernel(nc, x, ctx_in, w_gate, w_up, w_down, wq, bq, wk, bk, wv, bv, interference, amp, wo, bo,
                   w_base, b_base, w_router, lora_a, lora_b, out):
    B, S, D = x.shape
    I = w_gate.shape[0]
    NH, M, _ = interference.shape
    DK = D // (NH * M)
    E, R, _ = lora_a.shape
    T = B * S
    NT = T // P
    KC = D // P
    IC = (I + P - 1) // P
    IREM = I - (IC - 1) * P
    KEEP_OUT = I // 2
    AIM = KEEP_OUT - 5
    HC = NH // KC
    BT = P // S
    W33 = M * DK + 1
    ER = E * R
    assert S * 2 == P and M == 4 and DK == 8 and HC == 4 and ER == P and D == 512

    xf = x.rearrange("b s d -> (b s) d")
    cf = ctx_in.rearrange("b s d -> (b s) d")
    of = out.rearrange("b s d -> (b s) d")

    with ExitStack() as stack:
        def sb(name, shape, dt=F32):
            return stack.enter_context(nc.sbuf_tensor(name, shape, dt))

        def sem(name):
            return stack.enter_context(nc.semaphore(name))

        ident = sb("ident", [P, P])
        same_hd = sb("same_hd", [P, P])
        blk = sb("blk", [P, KC, P])
        int_hi = sb("int_hi", [M * NH, M])
        alpha = sb("alpha", [P, 1])
        mcol = sb("mcol", [P, M])
        ones = sb("ones", [P, P])
        half = sb("half", [P, 1])
        iota16 = sb("iota16", [P, CANDIDATES + 1])
        bits = sb("bits", [P, 32], I32)
        bcol = sb("bcol", [P, 3, KC])
        bk_f = sb("bk_f", [P, KC])
        bq_f = sb("bq_f", [P, KC])
        bv_f = sb("bv_f", [P, D])
        bo_f = sb("bo_f", [P, D])
        bb_f = sb("bb_f", [P, D])
        stage = sb("stage", [P, 3, 4 * D])
        wgT = sb("wgT", [P, KC, I])
        wuT = sb("wuT", [P, KC, I])
        wdT = sb("wdT", [P, IC, D])
        wqT = sb("wqT", [P, KC, D])
        wkT = sb("wkT", [P, KC, D])
        wvT = sb("wvT", [P, KC, D])
        woT = sb("woT", [P, KC, D])
        wbT = sb("wbT", [P, KC, D])
        arT = sb("arT", [P, KC, ER + E])
        lbT = sb("lbT", [P, D])
        xs = sb("xs", [P, NT, D])
        WORK = 5 * I + IC * P + 2 * D
        work = sb("work", [P, 11900])
        o = 0

        def carve(n, dt=F32, shape=None):
            nonlocal o
            v = work[:, o:o + n]
            o += n
            return v

        xT = [carve(D).rearrange("p (c t) -> p c t", c=KC) for _ in range(2)]
        act_s = carve(I)
        mag = [carve(I) for _ in range(2)]
        prod = [carve(I) for _ in range(2)]
        cand = carve(I)
        junk = carve(I // 2).bitcast(BF16)
        hT = carve(IC * P).rearrange("p (c t) -> p c t", c=IC)
        y1 = carve(D)
        o = 0
        spread = carve(D)[0:M * NH].rearrange("p (c n) -> p c n", c=KC)
        blk_tmp = carve(D).rearrange("p (c n) -> p c n", c=KC)
        bcol_bc = carve(D).rearrange("p (c n) -> p c n", c=KC)
        o = 0
        cnat = [carve(D) for _ in range(2)]
        x1T = carve(D).rearrange("p (c t) -> p c t", c=KC)
        cT = carve(D).rearrange("p (c t) -> p c t", c=KC)
        kqb = carve(D).rearrange("p (c t) -> p c t", c=KC)
        qb = carve(D).rearrange("p (c t) -> p c t", c=KC)
        attn_n = carve(BT * D // 2).rearrange("p (b f) -> p b f", b=BT)
        aT = carve(D).rearrange("p (a j t) -> p a j t", a=2, j=2)
        x2 = carve(D)
        x2T = carve(D).rearrange("p (c t) -> p c t", c=KC)
        sub = [carve(D) for _ in range(2)]
        pr = [carve(D) for _ in range(2)]
        pT = [carve(D) for _ in range(2)]
        hw = carve(ER)
        hwT = carve(ER)
        yb = carve(2 * D).rearrange("p (a n) -> p a n", a=2)
        xbias = carve(2 * D).rearrange("p (a n) -> p a n", a=2)
        assert o <= 11900, o
        stage_flat = stage[:].rearrange("p a n -> p (a n)")
        kx = stage_flat[:, 0:2048].rearrange("p (c b h k) -> p c b h k", c=KC, b=BT, h=HC)
        qx = stage_flat[:, 2048:4096].rearrange("p (c b m q) -> p c b m q", c=KC, b=BT, m=M)
        vx = stage_flat[:, 4096:4096 + BT * NH * W33].rearrange("p (b a h w) -> p b a h w", b=BT, a=NH // 2, h=2)
        msum = sb("msum", [P, 2])
        step = sb("step", [P, 4])
        tcol = sb("tcol", [P, COUNTS])
        ccol = sb("ccol", [P, COUNTS])
        okc = sb("okc", [P, COUNTS])
        okt = sb("okt", [P, COUNTS])
        lo = sb("lo", [P, 4])
        top = sb("top", [P, CANDIDATES + 1])
        pick = sb("pick", [P, CANDIDATES + 1])
        pick2 = sb("pick2", [P, CANDIDATES + 1])
        thr = sb("thr", [P, 2])
        flag = sb("flag", [P, 4])
        flag_all = sb("flag_all", [P, 1])
        stats = sb("stats", [P, 6])
        mv = sb("mv", [P, 2])
        veps = sb("veps", [P, 1])
        rstd = sb("rstd", [P, 1])
        smax = sb("smax", [P, 2, 8])
        rden = sb("rden", [P, 8])
        rt = sb("rt", [P, 8, 8])
        re = sb("re", [P, 8])
        rsum = sb("rsum", [P, 4])

        ps = stack.enter_context(nc.psum_tensor("ps", [P, 8, 512], F32))
        gate_ps = ps[:, 0:3, :].rearrange("p b n -> p (b n)")
        up_ps = ps[:, 3:6, :].rearrange("p b n -> p (b n)")
        M0, M1 = ps[:, 6, :], ps[:, 7, :]
        score_ps = [ps[:, 0, :], ps[:, 1, :]]
        ptr_ps = [ps[:, 2, :], ps[:, 3, :]]
        av_ps, base_ps = ps[:, 4, :], ps[:, 5, :]

        names = """x_first x_rest small_loaded pool_const ints_up ints_done blk_done bias_mm bias_done
            unit_mm unit_act unit_dve ctx_loaded0 ctx_loaded1 out_stored0 out_stored1
            xT_mm xT_done gate_mm silu_done mag_done up_mm prod_done masked bad_seen flag_summed
            hT_mm hT_done down_mm y1_done v1_done r1_done x1_done
            x1T_mm x1T_done cT_mm cT_done aT_mm aT_done o_mm y2_done v2_done r2_done x2_done xb1_done xb2_done
            k_mm kb_done kx_done q_mm qb_done qx_done v_mm vx_done
            x2T_mm x2T_done ar_mm base_mm rmax_done rexp_done hw_done hwT_mm hwT_done lora_mm y3_done v3_done r3_done
            x3_done score_mm sub_done exp_done ptr_mm pT_done av_mm av_done dve_step act_step pool_step vx_zero
            attn_read""".split()
        sm = {n: sem(n) for n in names}
        stage_sem = [sem(f"stage{i}") for i in range(3)]
        xs_free = sm["x1_done"]

        panels = []
        NP_ = 0

        def panel(loads, units):
            panels.append((loads, units))

        def slot_of():
            return stage[:, len(panels) % 3, :]

        def rows_panel(w, dstT, p0):
            st = slot_of().rearrange("p (r d) -> p r d", d=D)
            n = min(4, IC - p0)
            full = n if p0 + n < IC or IREM == P else n - 1
            loads = [(st[:, 0:full, :], w[p0 * P:(p0 + full) * P, :].rearrange("(r p) d -> p r d", p=P))]
            if full < n:
                loads.append((st[0:IREM, full, :], w[(p0 + full) * P:I, :]))
            cols = full * P + (IREM if full < n else 0)
            units = []
            for ic in range(KC):
                mms = []
                for r in range(n):
                    k = P if r < full else IREM
                    mms.append((slice(r * P, r * P + k), st[0:k, r, ic * P:(ic + 1) * P], ident[0:k, 0:k], P))
                units.append((mms, dstT[:, ic, p0 * P:p0 * P + cols], P, cols))
            panel(loads, units)

        def down_panel(p0):
            n = min(4, IC - p0)
            cols = min(I - p0 * P, n * P)
            st = slot_of().rearrange("p (r d) -> p r d", d=D)
            loads = [(st[:, :, 0:cols], w_down[:, p0 * P:p0 * P + cols].rearrange("(r p) i -> p r i", p=P))]
            units = []
            for c in range(n):
                m = min(P, cols - c * P)
                mms = [(slice(oc * P, oc * P + P), st[:, oc, c * P:c * P + m], ident[:, :], m) for oc in range(KC)]
                units.append((mms, wdT[0:m, p0 + c, :], m, D))
            panel(loads, units)

        def square_panel(w, dstT, kind):
            st = slot_of().rearrange("p (r d) -> p r d", d=D)
            loads = [(st[:, :, :], w.rearrange("(r p) d -> p r d", p=P))]
            units = []
            for ic in range(KC):
                mms = []
                for oc in range(KC):
                    if kind == "wo":
                        a = (ic // 2) * 2 * P + ic % 2
                        lhs = st[:, oc, a:a + 2 * P - 1:2]
                    else:
                        lhs = st[:, oc, ic * P:(ic + 1) * P]
                    rhs = blk[:, oc, :] if kind == "qkv" else ident[:, :]
                    mms.append((slice(oc * P, oc * P + P), lhs, rhs, P))
                units.append((mms, dstT[:, ic, :], P, D))
            panel(loads, units)

        for p0 in range(0, IC, 4):
            rows_panel(w_gate, wgT, p0)
        for p0 in range(0, IC, 4):
            rows_panel(w_up, wuT, p0)
        for p0 in range(0, IC, 4):
            down_panel(p0)
        square_panel(wk, wkT, "qkv")
        square_panel(wq, wqT, "qkv")
        square_panel(wv, wvT, "qkv")
        square_panel(wo, woT, "wo")
        square_panel(w_base, wbT, "plain")
        st = slot_of()
        loads = [(st[:, 0:D], lora_a.rearrange("e r d -> (e r) d")),
                 (st[0:E, 2 * D:3 * D], w_router)]
        for oc in range(KC):
            loads.append((st[:, D + oc * P:D + (oc + 1) * P].rearrange("p (e r) -> p e r", e=E),
                          lora_b[:, oc * P:(oc + 1) * P, :].rearrange("e p r -> p e r")))
        panel(loads, [
            ([(slice(ic * P, ic * P + P), st[:, ic * P:(ic + 1) * P], ident[:, :], P) for ic in range(KC)],
             arT[:, :, 0:ER], P, D),
            ([(slice(ic * E, ic * E + E), st[0:E, 2 * D + ic * P:2 * D + (ic + 1) * P], ident[0:E, 0:E], P) for ic in range(KC)],
             arT[:, :, ER:ER + E], P, KC * E),
            ([(slice(oc * P, oc * P + P), st[:, D + oc * P:D + (oc + 1) * P], ident[:, :], P) for oc in range(KC)],
             lbT[:, :], P, D)])

        unit_end = []
        total = 0
        for _, units in panels:
            total += len(units)
            unit_end.append(total)
        NUNITS = total
        GU_UNITS = unit_end[5]
        stage_count = []
        cnt = [0, 0, 0]
        for n, (loads, _) in enumerate(panels):
            cnt[n % 3] += 16 * len(loads)
            stage_count.append(cnt[n % 3])

        block = stack.enter_context(nc.Block())

        def setup_evac(eng, copy, parity, done):
            u = 0
            for n, (_, units) in enumerate(panels):
                for _, dst, rows, cols in units:
                    if u % 2 == parity:
                        eng.wait_ge(sm["unit_mm"], u + 1)
                        src = ps[0:rows, u % 8, 0:cols]
                        if len(dst.shape) == 3:
                            src = src.rearrange("p (a b) -> p a b", a=dst.shape[1])
                        copy(dst, src).then_inc(done, 1)
                    u += 1

        def setup_seen(eng, units):
            eng.wait_ge(sm["unit_act"], (units + 1) // 2)
            eng.wait_ge(sm["unit_dve"], units // 2)

        @block.sync
        def _(sp):
            sp.dma_start(xs[:, 0, :], xf[0:P, :]).then_inc(sm["x_first"], 16)
            for n, (loads, _) in enumerate(panels):
                if n >= 3:
                    sp.wait_ge(sm["unit_mm"], unit_end[n - 3])
                for dst, src in loads:
                    sp.dma_start(dst, src).then_inc(stage_sem[n % 3], 16)
                if n == 5:
                    sp.dma_start(xs[:, 1:NT, :], xf[P:T, :].rearrange("(t p) d -> p t d", p=P)).then_inc(sm["x_rest"], 16)
            for t in range(NT):
                if t == 0:
                    sp.wait_ge(sm["x1_done"], NT)
                if t >= 2:
                    sp.wait_ge(sm["cT_mm"], t - 1)
                sp.dma_start(cnat[t % 2], cf[t * P:(t + 1) * P, :]).then_inc(sm[f"ctx_loaded{t % 2}"], 16)
                if t >= 2:
                    sp.wait_ge(sm["x3_done"], t - 1)
                    sp.dma_start(of[(t - 2) * P:(t - 1) * P, :], yb[:, (t - 2) % 2, :]).then_inc(sm[f"out_stored{t % 2}"], 16)
            for t in range(NT - 2, NT):
                sp.wait_ge(sm["x3_done"], t + 1)
                sp.dma_start(of[t * P:(t + 1) * P, :], yb[:, t % 2, :]).then_inc(sm[f"out_stored{t % 2}"], 16)
            sp.wait_ge(sm["out_stored0"], 8 * NT)
            sp.wait_ge(sm["out_stored1"], 8 * NT)

        @block.gpsimd
        def _(pool):
            k = [0]

            def step_(ins):
                k[0] += 1
                ins.then_inc(sm["pool_step"], 1)
                pool.wait_ge(sm["pool_step"], k[0])

            pool.dma_start(int_hi[:, :], interference.rearrange("h i j -> (h i) j")).then_inc(sm["small_loaded"], 16)
            pool.dma_start(alpha[:, :], amp.rearrange("(a n) -> a n", a=1).to_broadcast([P, 1])).then_inc(sm["small_loaded"], 16)
            for n, b in enumerate((bk, bq, bv)):
                with nc.allow_non_contiguous_dma(reason="512 words, once"):
                    pool.dma_start(bcol[:, n, :], b.rearrange("(c p) -> p c", p=P)).then_inc(sm["small_loaded"], 16)
            for n, (b, d) in enumerate(((bo, bo_f), (b_base, bb_f))):
                pool.dma_start(d[:, :], b.rearrange("(a n) -> a n", a=1).to_broadcast([P, D])).then_inc(sm["small_loaded"], 16)
            step_(nc.gpsimd.memset(ident[:], 0.0))
            nc.gpsimd.affine_select(out=ident[:], in_=ident[:], compare_op=ALU.not_equal, fill=1.0, base=0,
                                    pattern=[[-1, P]], channel_multiplier=1).then_inc(sm["pool_const"], 1)
            step_(nc.gpsimd.memset(same_hd[:], 1.0))
            v = same_hd[:].rearrange("p (a j) -> p a j", j=M)
            step_(nc.gpsimd.affine_select(out=v, in_=v, compare_op=ALU.is_ge, fill=0.0, base=0,
                                          pattern=[[-M, P // M], [0, M]], channel_multiplier=1))
            nc.gpsimd.affine_select(out=v, in_=v, compare_op=ALU.is_ge, fill=0.0, base=M - 1,
                                    pattern=[[M, P // M], [0, M]], channel_multiplier=-1).then_inc(sm["pool_const"], 1)
            step_(nc.gpsimd.memset(spread, 0.0))
            v = spread.rearrange("p c (h d i) -> p (c h) d i", h=HC, d=DK)
            nc.gpsimd.affine_select(out=v, in_=v, compare_op=ALU.not_equal, fill=1.0, base=0,
                                    pattern=[[-M, NH], [0, DK], [-1, M]], channel_multiplier=1).then_inc(sm["pool_const"], 1)
            nc.gpsimd.memset(ones[:], 1.0).then_inc(sm["pool_const"], 1)
            nc.gpsimd.memset(half[:], -0.5).then_inc(sm["pool_const"], 1)
            nc.gpsimd.iota(iota16[:], pattern=[[1, CANDIDATES + 1]], base=0, channel_multiplier=0,
                           allow_small_or_imprecise_dtypes=True).then_inc(sm["pool_const"], 1)
            for b in range(31):
                nc.gpsimd.memset(bits[:, b:b + 1], 1 << (30 - b))
            ins = nc.gpsimd.memset(bits[:, 31:32], 0)
            ins.then_inc(sm["pool_const"], 1)
            pool.wait_ge(sm["unit_mm"], NUNITS)
            nc.gpsimd.memset(kx, 0.0).then_inc(sm["vx_zero"], 1)
            step_(nc.gpsimd.memset(vx, 0.0))
            for h2 in range(2):
                nc.gpsimd.memset(vx[S * h2:S * h2 + S, :, :, h2, W33 - 1:W33], 1.0).then_inc(sm["vx_zero"], 1)

            pool.wait_ge(sm["vx_zero"], 3)

            def rstd_(stage_v, stage_r, t):
                pool.wait_ge(sm[stage_v], t + 1)
                step_(nc.gpsimd.tensor_scalar(veps[:], mv[:, 1:2], EPS, None, ALU.add))
                nc.gpsimd.tensor_tensor(rstd[:], veps[:], half[:], ALU.pow).then_inc(sm[stage_r], 1)

            for t in range(NT):
                pool.wait_ge(sm["bad_seen"], t + 1)
                nc.gpsimd.partition_all_reduce(flag_all[:], flag[:, 2:3], P,
                                               bass.bass_isa.ReduceOp.max).then_inc(sm["flag_summed"], 1)
                if t >= 1:
                    rstd_("v1_done", "r1_done", t - 1)
            rstd_("v1_done", "r1_done", NT - 1)
            pool.wait_ge(sm["small_loaded"], 16 * 7)
            for t in range(-1, NT):
                u = t + 1
                if t >= 0:
                    rstd_("v2_done", "r2_done", t)
                if u < NT:
                    pool.wait_ge(sm["x1_done"], NT)
                    if u >= 1:
                        pool.wait_ge(sm["y2_done"], u)
                    nc.gpsimd.tensor_tensor(xbias[:, 0, :], xs[:, u, :], bo_f[:], ALU.add).then_inc(sm["xb1_done"], 1)
                    pool.wait_ge(sm["kb_done"], u + 1)
                    if u >= 1:
                        pool.wait_ge(sm["score_mm"], 8 * u)
                    pool.wait_ge(sm["xb1_done"], u + 1)
                    for h in range(HC):
                        q0 = 32 * h
                        if HC * u + h:
                            pool.wait_ge(sm["kx_done"], HC * u + h)
                        nc.gpsimd.tensor_copy(kx[q0:q0 + 32, :, :, h, :],
                                              kqb[q0:q0 + 32, :, :].rearrange("p c (b k) -> p c b k", b=BT)
                                              ).then_inc(sm["kx_done"], 1)
                    pool.wait_ge(sm["kx_done"], HC * (u + 1))
                if t >= 0:
                    pool.wait_ge(sm["x2_done"], t + 1)
                    if t >= 1:
                        pool.wait_ge(sm["y3_done"], t)
                    nc.gpsimd.tensor_tensor(xbias[:, 1, :], x2, bb_f[:], ALU.add).then_inc(sm["xb2_done"], 1)
                    rstd_("v3_done", "r3_done", t)

        @block.tensor
        def _(pe):
            mm = nc.tensor.matmul
            pe.wait_ge(sm["pool_const"], 6)
            pe.wait_ge(sm["small_loaded"], 16 * 7)

            def interference_blocks():
                for c in range(KC):
                    ins = mm(ps[:, 7, c * M:(c + 1) * M], spread[:, c, :], int_hi[:, :], start=True, stop=True)
                ins.then_inc(sm["ints_up"], 1)

            def folded_biases():
                pe.wait_ge(sm["blk_done"], 1)
                for c in range(KC):
                    mm(ps[:, 6, c:c + 1], blk[:, c, :], bcol[:, 0, c:c + 1], start=True, stop=True)
                    mm(ps[:, 6, KC + c:KC + c + 1], blk[:, c, :], bcol[:, 1, c:c + 1], start=True, stop=True)
                for c in range(KC):
                    ins = mm(ps[:, 7, c * P:(c + 1) * P], bcol_bc[:, c, :], blk[:, c, :], start=True, stop=True)
                ins.then_inc(sm["bias_mm"], 1)
                pe.wait_ge(sm["bias_done"], 2)

            interference_blocks()
            folded_biases()
            u = 0
            for n, (_, units) in enumerate(panels):
                pe.wait_ge(stage_sem[n % 3], stage_count[n])
                for mms, _, rows, cols in units:
                    if u >= 8:
                        e = u - 8
                        pe.wait_ge(sm["unit_act"] if e % 2 == 0 else sm["unit_dve"], e // 2 + 1)
                    for cs, lhs, rhs, m in mms:
                        ins = mm(ps[0:m, u % 8, cs], lhs, rhs, start=True, stop=True,
                                 is_transpose=None if rhs.tensor is blk[:].tensor else True)
                    ins.then_inc(sm["unit_mm"], 1)
                    u += 1
            setup_seen(pe, NUNITS)

            def x_turn(t):
                pe.wait_ge(sm["x_first" if t == 0 else "x_rest"], 16)
                if t >= 3:
                    pe.wait_ge(sm["y1_done"], t - 2)
                if t >= 2:
                    pass
                for c in range(KC):
                    ins = nc.tensor.transpose(M0[:, c * P:(c + 1) * P], xs[:, t, c * P:(c + 1) * P], ident[:])
                ins.then_inc(sm["xT_mm"], 1)

            def gate_up(t):
                pe.wait_ge(sm["xT_done"], t + 1)
                for w, acc, done, free in ((wgT, gate_ps, "gate_mm", "silu_done"), (wuT, up_ps, "up_mm", "prod_done")):
                    if t >= 1:
                        pe.wait_ge(sm[free], t)
                    for n0 in range(0, I, 512):
                        n1 = min(I, n0 + 512)
                        for c in range(KC):
                            ins = mm(acc[:, n0:n1], xT[t % 2][:, c, :], w[:, c, n0:n1], start=(c == 0), stop=(c == KC - 1))
                    ins.then_inc(sm[done], 1)

            def h_turn_down(t, last):
                pe.wait_ge(sm["masked"], t + 1)
                if t >= 1:
                    pe.wait_ge(sm["hT_done"], 3 * t)
                for g in range(3):
                    bank = M1 if g % 2 == 0 else M0
                    if g == 1:
                        pe.wait_ge(sm["xT_done"], min(t + 3, NT))
                        if t >= NT - 2:
                            pe.wait_ge(sm["y1_done"], t)
                    if g == 2:
                        pe.wait_ge(sm["hT_done"], 3 * t + 1)
                    n = min(4, IC - 4 * g)
                    for r in range(n):
                        i0 = (4 * g + r) * P
                        m = min(P, I - i0)
                        ins = nc.tensor.transpose(bank[0:m, r * P:(r + 1) * P], prod[t % 2][:, i0:i0 + m], ident[:])
                    ins.then_inc(sm["hT_mm"], 1)
                pe.wait_ge(sm["hT_done"], 3 * t + 2)
                for c in range(IC):
                    m = min(P, I - c * P)
                    if c == 8:
                        pe.wait_ge(sm["hT_done"], 3 * t + 3)
                    ins = mm(M0[:, :], hT[0:m, c, :], wdT[0:m, c, :], start=(c == 0), stop=(c == IC - 1))
                ins.then_inc(sm["down_mm"], 1)

            x_turn(0)
            gate_up(0)
            x_turn(1)
            for t in range(NT):
                if t + 1 < NT:
                    gate_up(t + 1)
                if t + 2 < NT:
                    x_turn(t + 2)
                h_turn_down(t, t == NT - 1)

            def turn4(bank, src, done):
                for c in range(KC):
                    ins = nc.tensor.transpose(bank[:, c * P:(c + 1) * P], src[:, c * P:(c + 1) * P], ident[:])
                ins.then_inc(sm[done], 1)

            def x1_ctx_turn(u):
                pe.wait_ge(sm["x1_done"], u + 1 if u else NT)
                if u >= 2:
                    pe.wait_ge(sm["rmax_done"], u - 1)
                    pe.wait_ge(sm["hw_done"], u - 1)
                if u == 1:
                    pe.wait_ge(sm["vx_done"], 4 * 1)
                turn4(M0, xs[:, u, :], "x1T_mm")
                pe.wait_ge(sm[f"ctx_loaded{u % 2}"], 16 * (u // 2 + 1))
                if u >= 2:
                    pe.wait_ge(sm["hwT_done"], u - 1)
                if u == 1:
                    pe.wait_ge(sm["qb_done"], 1)
                turn4(M1, cnat[u % 2], "cT_mm")

            def attn_out(t):
                pe.wait_ge(sm["av_done"], 8 * (t + 1))
                pe.wait_ge(sm["x1T_done"], min(t + 2, NT))
                if t == NT - 1:
                    pe.wait_ge(sm["hw_done"], t)
                for b in range(BT):
                    for a in range(2):
                        ins = nc.tensor.transpose(M0[:, (2 * b + a) * P:(2 * b + a + 1) * P],
                                                  attn_n[:, b, a * P:(a + 1) * P], ident[:])
                ins.then_inc(sm["aT_mm"], 1)
                pe.wait_ge(sm["aT_done"], BT * (t + 1))
                pe.wait_ge(sm["cT_done"], min(t + 2, NT))
                if t == NT - 1:
                    pe.wait_ge(sm["hwT_done"], t)
                for a in range(2):
                    for j in range(2):
                        ins = mm(M1[:, :], aT[:, a, j, :], woT[:, 2 * a + j, :], start=(a + j == 0), stop=(a + j == 2))
                ins.then_inc(sm["o_mm"], 1)

            def qkv(u):
                pe.wait_ge(sm["x1T_done"], u + 1)
                pe.wait_ge(sm["cT_done"], u + 1)
                if u >= 1:
                    pe.wait_ge(sm["aT_done"], BT * u)
                for w, src, bank, done in ((wkT, cT, M0, "k_mm"), (wqT, x1T, M1, "q_mm")):
                    if done == "q_mm" and u >= 1:
                        pe.wait_ge(sm["y2_done"], u)
                    for f in range(KC):
                        for c in range(KC):
                            ins = mm(bank[:, f * P:(f + 1) * P], w[:, c, f * P:(f + 1) * P], src[:, c, :],
                                     start=(c == 0), stop=(c == KC - 1))
                    ins.then_inc(sm[done], 1)
                pe.wait_ge(sm["kb_done"], u + 1)
                for c in range(KC):
                    ins = mm(M0[:, :], cT[:, c, :], wvT[:, c, :], start=(c == 0), stop=(c == KC - 1))
                ins.then_inc(sm["v_mm"], 1)

            def ffn_in(t):
                pe.wait_ge(sm["x2_done"], t + 1)
                pe.wait_ge(sm["qb_done"], min(t + 2, NT))
                if t == NT - 1:
                    pe.wait_ge(sm["y2_done"], t + 1)
                turn4(M1, x2, "x2T_mm")
                pe.wait_ge(sm["x2T_done"], t + 1)
                pe.wait_ge(sm["vx_done"], 4 * min(t + 2, NT))
                for c in range(KC):
                    ins = mm(M0[:, 0:ER + E], x2T[:, c, :], arT[:, c, :], start=(c == 0), stop=(c == KC - 1))
                ins.then_inc(sm["ar_mm"], 1)
                if t >= 1:
                    pe.wait_ge(sm["y3_done"], t)
                for c in range(KC):
                    mm(base_ps, x2T[:, c, :], wbT[:, c, :], start=(c == 0), stop=False)

            def lora_turn(t):
                pe.wait_ge(sm["hw_done"], t + 1)
                nc.tensor.transpose(M1[:, 0:ER], hw, ident[:]).then_inc(sm["hwT_mm"], 1)

            def lora_out(t):
                pe.wait_ge(sm["hwT_done"], t + 1)
                mm(base_ps, hwT, lbT[:, :], start=False, stop=True).then_inc(sm["lora_mm"], 1)

            def scores(u, g):
                b, c = divmod(g, KC)
                if g == 0:
                    pe.wait_ge(sm["kx_done"], HC * (u + 1))
                    pe.wait_ge(sm["qx_done"], M * (u + 1))
                n = 8 * u + g
                if n >= 2:
                    pe.wait_ge(sm["sub_done"], n - 1)
                for mp in range(2):
                    ins = mm(score_ps[g % 2][:, mp * 256:(mp + 1) * 256],
                             qx[:, c, b, 2 * mp:2 * mp + 2, :], kx[:, c, b, :, :], start=True, stop=True)
                ins.then_inc(sm["score_mm"], 1)

            def prob_turn(u, g):
                n = 8 * u + g
                pe.wait_ge(sm["exp_done"], n + 1)
                if n >= 2:
                    pe.wait_ge(sm["pT_done"], n - 1)
                for k4 in range(4):
                    ins = nc.tensor.transpose(ptr_ps[g % 2][:, k4 * P:(k4 + 1) * P],
                                              pr[g % 2][:, k4 * P:(k4 + 1) * P], ident[:])
                ins.then_inc(sm["ptr_mm"], 1)

            def weighted_v(u, g):
                b, c = divmod(g, KC)
                n = 8 * u + g
                if g == 0:
                    pe.wait_ge(sm["vx_done"], 4 * (u + 1))
                pe.wait_ge(sm["pT_done"], n + 1)
                if n >= 1:
                    pe.wait_ge(sm["av_done"], n)
                for mp in range(2):
                    for hp in range(2):
                        o0 = (mp * 2 + hp) * 2 * W33
                        k4 = 2 * mp + hp
                        ins = mm(av_ps[:, o0:o0 + 2 * W33], pT[g % 2][:, k4 * P:(k4 + 1) * P],
                                 vx[:, b, 2 * c + hp, :, :], start=True, stop=True)
                ins.then_inc(sm["av_mm"], 1)

            for t in range(-1, NT):
                u = t + 1
                if u < NT:
                    x1_ctx_turn(u)
                if t >= 0:
                    attn_out(t)
                if u < NT:
                    qkv(u)
                if t >= 0:
                    ffn_in(t)
                if u < NT:
                    scores(u, 0)
                    scores(u, 1)
                    prob_turn(u, 0)
                if t >= 0:
                    lora_turn(t)
                if u < NT:
                    scores(u, 2)
                    prob_turn(u, 1)
                    weighted_v(u, 0)
                if t >= 0:
                    lora_out(t)
                if u < NT:
                    for g in range(3, 8):
                        scores(u, g)
                        prob_turn(u, g - 1)
                        weighted_v(u, g - 2)
                    prob_turn(u, 7)
                    weighted_v(u, 6)
                    weighted_v(u, 7)

        @block.scalar
        def _(act):
            k = [0]

            def step_(ins):
                k[0] += 1
                ins.then_inc(sm["act_step"], 1)
                act.wait_ge(sm["act_step"], k[0])

            cp = lambda o_, i_: nc.scalar.activation(o_, i_, ACT.Copy)
            setup_evac(act, cp, 0, sm["unit_act"])

            def x_evac(t):
                act.wait_ge(sm["xT_mm"], t + 1)
                if t >= 2:
                    act.wait_ge(sm["up_mm"], t - 1)
                cp(xT[t % 2], M0.rearrange("p (c t) -> p c t", c=KC)).then_inc(sm["xT_done"], 1)

            def silu(t):
                act.wait_ge(sm["gate_mm"], t + 1)
                if t >= 1:
                    act.wait_ge(sm["prod_done"], t)
                nc.scalar.activation(act_s, gate_ps[:, 0:I], ACT.Silu).then_inc(sm["silu_done"], 1)
                act.wait_ge(sm["silu_done"], t + 1)
                if t >= 2:
                    act.wait_ge(sm["masked"], t - 1)
                nc.scalar.activation(mag[t % 2], act_s, ACT.Abs,
                                     accum_out=msum[:, t % 2:t % 2 + 1]).then_inc(sm["mag_done"], 1)

            def h_evac(t):
                for g in range(3):
                    act.wait_ge(sm["hT_mm"], 3 * t + g + 1)
                    if g == 0 and t >= 1:
                        act.wait_ge(sm["down_mm"], t)
                    bank = M1 if g % 2 == 0 else M0
                    n = min(4, IC - 4 * g)
                    if 4 * g + n == IC and IREM < P:
                        cp(hT[:, 4 * g:4 * g + n - 1, :].rearrange("p a b -> p (a b)"), bank[:, 0:(n - 1) * P])
                        cp(hT[0:IREM, IC - 1, :], bank[0:IREM, (n - 1) * P:n * P]).then_inc(sm["hT_done"], 1)
                    else:
                        cp(hT[:, 4 * g:4 * g + n, :].rearrange("p a b -> p (a b)"), bank[:, 0:n * P]).then_inc(sm["hT_done"], 1)

            x_evac(0)
            silu(0)
            x_evac(1)
            for t in range(NT):
                if t + 1 < NT:
                    silu(t + 1)
                if t + 2 < NT:
                    x_evac(t + 2)
                h_evac(t)

            def exps(u, g):
                n = 8 * u + g
                act.wait_ge(sm["sub_done"], n + 1)
                if n >= 2:
                    act.wait_ge(sm["ptr_mm"], n - 1)
                nc.scalar.activation(pr[g % 2], sub[g % 2], ACT.Exp).then_inc(sm["exp_done"], 1)

            def pT_evac(u, g):
                n = 8 * u + g
                act.wait_ge(sm["ptr_mm"], n + 1)
                if n >= 2:
                    act.wait_ge(sm["av_mm"], n - 1)
                cp(pT[g % 2], ptr_ps[g % 2]).then_inc(sm["pT_done"], 1)

            for t in range(-1, NT):
                u = t + 1
                if u < NT:
                    act.wait_ge(sm["x1T_mm"], u + 1)
                    if u >= 1:
                        act.wait_ge(sm["q_mm"], u)
                    cp(x1T, M0.rearrange("p (c t) -> p c t", c=KC)).then_inc(sm["x1T_done"], 1)
                if t >= 0:
                    act.wait_ge(sm["aT_mm"], t + 1)
                    if t >= 1:
                        act.wait_ge(sm["o_mm"], t)
                    src = M0.rearrange("p (b a j q) -> p b a j q", b=BT, a=2, j=2)
                    for b in range(BT):
                        cp(aT[:, :, :, b * S:(b + 1) * S], src[:, b]).then_inc(sm["aT_done"], 1)
                if u < NT:
                    act.wait_ge(sm["qb_done"], u + 1)
                    if u >= 1:
                        act.wait_ge(sm["score_mm"], 8 * u)
                    for m in range(M):
                        nc.scalar.activation(qx[:, :, :, m, :].rearrange("p c b q -> p (c b) q"),
                                             qb.rearrange("p c (b q) -> p (c b) q", b=BT), ACT.Copy,
                                             scale=mcol[:, m:m + 1]).then_inc(sm["qx_done"], 1)
                if t >= 0:
                    act.wait_ge(sm["x2T_mm"], t + 1)
                    if t >= 1:
                        act.wait_ge(sm["lora_mm"], t)
                    cp(x2T, M1.rearrange("p (c t) -> p c t", c=KC)).then_inc(sm["x2T_done"], 1)
                    act.wait_ge(sm["rmax_done"], t + 1)
                    nc.scalar.activation(re[:], M0[:, ER:ER + E], ACT.Exp, bias=rsum[:, 0:1]).then_inc(sm["rexp_done"], 1)
                if u < NT:
                    exps(u, 0)
                    for g in range(1, 8):
                        exps(u, g)
                        pT_evac(u, g - 1)
                    pT_evac(u, 7)

        @block.vector
        def _(dve):
            V = nc.vector
            k = [0]

            def step_(ins):
                k[0] += 1
                ins.then_inc(sm["dve_step"], 1)
                dve.wait_ge(sm["dve_step"], k[0])

            dve.wait_ge(sm["pool_const"], 6)
            dve.wait_ge(sm["small_loaded"], 16 * 7)
            step_(V.tensor_reduce(mcol[:], ident[:].rearrange("p (a m) -> p m a", m=M), AX.X, ALU.add))
            step_(V.tensor_scalar(mcol[:], mcol[:], float(DK) ** -0.5, None, ALU.mult))
            step_(V.tensor_scalar(alpha[:], alpha[:], 0.1, None, ALU.mult))
            dve.wait_ge(sm["ints_up"], 1)
            for c in range(KC):
                r = ps[:, 7, c * M:(c + 1) * M].rearrange("p (a j) -> p a j", a=1).to_broadcast([P, P // M, M])
                step_(V.scalar_tensor_tensor(blk_tmp[:, c, :].rearrange("p (a j) -> p a j", j=M), r, alpha[:, 0:1],
                                             same_hd[:].rearrange("p (a j) -> p a j", j=M), ALU.mult, ALU.mult))
                step_(V.tensor_tensor(blk[:, c, :], blk_tmp[:, c, :], ident[:], ALU.add))
                ins = V.tensor_scalar(bcol_bc[:, c, :], ones[:], bcol[:, 2, c:c + 1], None, ALU.mult)
            ins.then_inc(sm["blk_done"], 1)
            dve.wait_ge(sm["bias_mm"], 1)
            V.tensor_copy(bk_f[:], ps[:, 6, 0:KC])
            V.tensor_copy(bq_f[:], ps[:, 6, KC:2 * KC]).then_inc(sm["bias_done"], 1)
            V.tensor_copy(bv_f[:], ps[:, 7, :]).then_inc(sm["bias_done"], 1)
            setup_evac(dve, V.tensor_copy, 1, sm["unit_dve"])

            def bisect(t):
                a = mag[t % 2]
                cur, val, cnt_, m_, r_ = lo[:, 0:1], lo[:, 1:2], lo[:, 2:3], lo[:, 3:4], step[:, 3:4]
                curi, mi = cur.bitcast(I32), m_.bitcast(I32)
                V.memset(curi, 1 << 30)
                V.drain()
                with dve.Fori(0, 31) as b:
                    V.tensor_scalar(junk[:, 0:I], a, cur, None, ALU.is_lt, ALU.add, accum_out=cnt_)
                    V.drain()
                    V.tensor_scalar(val, cnt_, float(KEEP_OUT) - 0.5, None, ALU.is_gt)
                    V.drain()
                    V.tensor_tensor(mi, val, bits[:, bass.ds(b, 1)], ALU.mult)
                    V.drain()
                    V.tensor_tensor(curi, curi, mi, ALU.bitwise_xor)
                    V.drain()
                    V.tensor_tensor(curi, curi, bits[:, bass.ds(b + 1, 1)], ALU.bitwise_xor)
                    V.drain()
                V.tensor_scalar(junk[:, 0:I], a, cur, None, ALU.is_lt, ALU.add, accum_out=cnt_)
                V.drain()
                V.tensor_scalar(r_, cnt_, -1.0, float(KEEP_OUT), ALU.mult, ALU.add)
                V.tensor_scalar(junk[:, 0:I], a, cur, None, ALU.is_equal)
                V.drain()
                V.tensor_tensor_scan(cand, junk[:, 0:I], junk[:, 0:I], 0.0, ALU.add, ALU.bypass)
                V.drain()
                V.scalar_tensor_tensor(cand, cand, r_, junk[:, 0:I], ALU.is_gt, ALU.mult)
                V.drain()
                V.scalar_tensor_tensor(a, a, cur, cand, ALU.is_gt, ALU.add)
                V.memset(thr[:, 0:1], 0.5)
                V.drain()

            def search(t):
                a = mag[t % 2]
                s = msum[:, t % 2:t % 2 + 1]
                dve.wait_ge(sm["mag_done"], t + 1)
                step_(V.tensor_scalar(tcol[:, 0:1], s, GUESS / I, None, ALU.mult))
                for i, d in enumerate(STEPS):
                    V.tensor_scalar(step[:, i:i + 1], s, d * SLOPE / I / KEEP_OUT, None, ALU.mult)
                for i in range(COUNTS):
                    step_(V.tensor_scalar(junk[:, 0:I], a, tcol[:, i:i + 1], None, ALU.is_lt, ALU.add,
                                          accum_out=ccol[:, i:i + 1]))
                    if i < COUNTS - 1:
                        step_(V.tensor_scalar(okc[:, 0:1], ccol[:, i:i + 1], float(AIM), step[:, i:i + 1],
                                              ALU.subtract, ALU.mult))
                        step_(V.tensor_tensor(tcol[:, i + 1:i + 2], tcol[:, i:i + 1], okc[:, 0:1], ALU.subtract))
                step_(V.tensor_scalar(okc[:], ccol[:], float(KEEP_OUT) + 0.5, None, ALU.is_lt))
                V.tensor_tensor(okt[:], okc[:], tcol[:], ALU.mult)
                step_(V.tensor_tensor(okc[:], okc[:], ccol[:], ALU.mult))
                V.tensor_reduce(lo[:, 0:1], okt[:], AX.X, ALU.max)
                step_(V.tensor_reduce(lo[:, 1:2], okc[:], AX.X, ALU.max))
                V.tensor_scalar(lo[:, 2:3], lo[:, 1:2], -1.0, float(KEEP_OUT), ALU.mult, ALU.add)
                step_(V.tensor_scalar(cand, a, lo[:, 0:1], -BIG, ALU.is_lt, ALU.mult))
                step_(V.tensor_tensor(cand, cand, a, ALU.subtract))
                step_(V.max(top[:, 0:8], cand))
                step_(V.match_replace(cand, top[:, 0:8], cand, -2 * BIG))
                step_(V.max(top[:, 8:16], cand))
                j = lo[:, 2:3]
                V.tensor_scalar(flag[:, 0:1], j, float(CANDIDATES) - 0.5, None, ALU.is_gt)
                step_(V.scalar_tensor_tensor(pick[:, 0:16], iota16[:, 0:16], j, top[:, 0:16], ALU.is_equal, ALU.mult))
                step_(V.scalar_tensor_tensor(pick2[:, 0:16], iota16[:, 1:17], j, top[:, 0:16], ALU.is_equal, ALU.mult))
                V.tensor_reduce(thr[:, 1:2], pick[:, 0:16], AX.X, ALU.min)
                step_(V.tensor_reduce(flag[:, 1:2], pick2[:, 0:16], AX.X, ALU.min))
                V.tensor_scalar(thr[:, 0:1], thr[:, 1:2], -1.0, None, ALU.mult)
                step_(V.tensor_tensor(flag[:, 1:2], flag[:, 1:2], thr[:, 1:2], ALU.is_equal))
                V.tensor_tensor(flag[:, 2:3], flag[:, 0:1], flag[:, 1:2], ALU.max).then_inc(sm["bad_seen"], 1)

            def product(t):
                dve.wait_ge(sm["up_mm"], t + 1)
                if t >= 2:
                    dve.wait_ge(sm["hT_mm"], 3 * (t - 1))
                V.tensor_tensor(prod[t % 2], act_s, up_ps[:, 0:I], ALU.mult).then_inc(sm["prod_done"], 1)

            def apply_mask(t):
                dve.wait_ge(sm["flag_summed"], t + 1)
                if GENERAL:
                    bad = dve.value_load(flag_all[0:1, 0:1].bitcast(I32), min_val=0, max_val=0x7fffffff)
                    with dve.If(bad >= 0 if FORCE else bad != 0):
                        bisect(t)
                dve.wait_ge(sm["prod_done"], t + 1)
                V.scalar_tensor_tensor(prod[t % 2], mag[t % 2], thr[:, 0:1], prod[t % 2],
                                       ALU.is_ge, ALU.mult).then_inc(sm["masked"], 1)

            def norm_stats(y, done):
                step_(V.bn_stats(stats[:], y))
                V.bn_aggr(mv[:], stats[:]).then_inc(sm[done], 1)

            def norm1(t):
                dve.wait_ge(sm["down_mm"], t + 1)
                y = y1
                if t >= 1:
                    dve.wait_ge(sm["x1_done"], t)
                ins = V.tensor_tensor(y, M0[:, :], xs[:, t, :], ALU.add)
                ins.then_inc(sm["y1_done"], 1)
                dve.wait_ge(sm["y1_done"], t + 1)
                norm_stats(y, "v1_done")
                dve.wait_ge(sm["r1_done"], t + 1)
                dve.wait_ge(sm["v1_done"], t + 1)
                V.tensor_scalar(xs[:, t, :], y, mv[:, 0:1], rstd[:, 0:1], ALU.subtract, ALU.mult).then_inc(sm["x1_done"], 1)

            search(0)
            product(0)
            apply_mask(0)
            for t in range(NT):
                if t + 1 < NT:
                    search(t + 1)
                    product(t + 1)
                    apply_mask(t + 1)
                norm1(t)

            def softmax_rows(u, g):
                n = 8 * u + g
                dve.wait_ge(sm["score_mm"], n + 1)
                sc = score_ps[g % 2].rearrange("p (r k) -> p r k", k=S)
                step_(V.tensor_reduce(smax[:, g % 2, :], sc, AX.X, ALU.max))
                if n >= 2:
                    dve.wait_ge(sm["exp_done"], n - 1)
                mb = smax[:, g % 2, :].rearrange("p (r a) -> p r a", a=1).to_broadcast([P, 8, S])
                V.tensor_tensor(sub[g % 2].rearrange("p (r k) -> p r k", k=S), sc, mb,
                                ALU.subtract).then_inc(sm["sub_done"], 1)

            def normalise(u, g):
                b, c = divmod(g, KC)
                n = 8 * u + g
                dve.wait_ge(sm["av_mm"], n + 1)
                if g == 0 and u >= 1:
                    dve.wait_ge(sm["aT_mm"], u)
                av = av_ps[:, 0:8 * W33].rearrange("p (r w) -> p r w", w=W33)
                step_(V.reciprocal(rden[:, :], av[:, :, W33 - 1]))
                for j in range(2):
                    rows = slice(S * j, S * j + S)
                    src = av_ps[rows, 0:8 * W33].rearrange("p (m r w) -> p m r w", m=2, w=W33)
                    dst = attn_n[rows, b, c * 64:(c + 1) * 64].rearrange("p (r d m) -> p m r d", r=4, m=2)
                    for mp in range(2):
                        s3 = src[:, mp, :, 2 * mp + j:2 * mp + j + 4 * DK - 3:4]
                        rd = rden[rows, 4 * mp:4 * mp + 4].rearrange("p (r a) -> p r a", a=1).to_broadcast([S, 4, DK])
                        ins = V.tensor_tensor(dst[:, mp], s3, rd, ALU.mult)
                ins.then_inc(sm["av_done"], 1)

            for t in range(-1, NT):
                u = t + 1
                if u < NT:
                    dve.wait_ge(sm["cT_mm"], u + 1)
                    if u >= 1:
                        dve.wait_ge(sm["v_mm"], u)
                    V.tensor_copy(cT, M1.rearrange("p (c t) -> p c t", c=KC)).then_inc(sm["cT_done"], 1)
                y = yb[:, t % 2, :]
                if t >= 0:
                    dve.wait_ge(sm["o_mm"], t + 1)
                    dve.wait_ge(sm["xb1_done"], t + 1)
                    if t >= 2:
                        dve.wait_ge(sm[f"out_stored{t % 2}"], 16 * (t // 2))
                    ins = V.tensor_tensor(y, M1[:, :], xbias[:, 0, :], ALU.add)
                    ins.then_inc(sm["y2_done"], 1)
                    dve.wait_ge(sm["y2_done"], t + 1)
                    norm_stats(y, "v2_done")
                if u < NT:
                    dve.wait_ge(sm["k_mm"], u + 1)
                    if u >= 1:
                        dve.wait_ge(sm["kx_done"], HC * u)
                    kb = bk_f[:].rearrange("p (c a) -> p c a", a=1).to_broadcast([P, KC, P])
                    V.tensor_tensor(kqb, M0.rearrange("p (c t) -> p c t", c=KC), kb, ALU.add).then_inc(sm["kb_done"], 1)
                if t >= 0:
                    dve.wait_ge(sm["r2_done"], t + 1)
                    dve.wait_ge(sm["v2_done"], t + 1)
                    if t >= 1:
                        dve.wait_ge(sm["x2T_mm"], t)
                        dve.wait_ge(sm["xb2_done"], t)
                    V.tensor_scalar(x2, y, mv[:, 0:1], rstd[:, 0:1], ALU.subtract, ALU.mult).then_inc(sm["x2_done"], 1)
                if u < NT:
                    dve.wait_ge(sm["q_mm"], u + 1)
                    if u >= 1:
                        dve.wait_ge(sm["qx_done"], M * u)
                    kb = bq_f[:].rearrange("p (c a) -> p c a", a=1).to_broadcast([P, KC, P])
                    V.tensor_tensor(qb, M1.rearrange("p (c t) -> p c t", c=KC), kb, ALU.add).then_inc(sm["qb_done"], 1)
                    dve.wait_ge(sm["v_mm"], u + 1)
                    if u == 0:
                        dve.wait_ge(sm["vx_zero"], 3)
                    else:
                        dve.wait_ge(sm["av_mm"], 8 * u)
                    for b in range(BT):
                        for h2 in range(2):
                            rows = slice(S * b, S * b + S)
                            fv = lambda z: z.rearrange("p (a h f) -> p a h f", h=2, f=M * DK)[:, :, h2, :]
                            V.tensor_tensor(vx[S * h2:S * h2 + S, b, :, h2, 0:M * DK], fv(M0[rows, :]),
                                            fv(bv_f[rows, :]), ALU.add).then_inc(sm["vx_done"], 1)
                if t >= 0:
                    dve.wait_ge(sm["ar_mm"], t + 1)
                    ins = V.tensor_reduce(rsum[:, 0:1], M0[:, ER:ER + E], AX.X, ALU.max, negate=True)
                    ins.then_inc(sm["rmax_done"], 1)
                if u < NT:
                    softmax_rows(u, 0)
                if t >= 0:
                    dve.wait_ge(sm["rexp_done"], t + 1)
                    step_(V.max(rt[:, 0, :], re[:]))
                    v = rt[:, 0, 1:2]
                    step_(V.tensor_scalar(rt[:, 1, :], re[:], v, None, ALU.is_gt, ALU.add, accum_out=rsum[:, 1:2]))
                    V.tensor_scalar(rt[:, 2, :], re[:], v, None, ALU.is_equal)
                    step_(V.tensor_scalar(rsum[:, 1:2], rsum[:, 1:2], -1.0, 2.0, ALU.mult, ALU.add))
                    step_(V.tensor_tensor_scan(rt[:, 3, :], rt[:, 2, :], rt[:, 2, :], 0.0, ALU.add, ALU.bypass))
                    step_(V.scalar_tensor_tensor(rt[:, 4, :], rt[:, 3, :], rsum[:, 1:2], rt[:, 2, :], ALU.is_le, ALU.mult))
                    step_(V.tensor_tensor(rt[:, 5, :], rt[:, 4, :], rt[:, 1, :], ALU.add))
                    step_(V.tensor_tensor(rt[:, 6, :], rt[:, 5, :], re[:], ALU.mult))
                    step_(V.tensor_reduce(rsum[:, 2:3], rt[:, 6, :], AX.X, ALU.add))
                    step_(V.reciprocal(rsum[:, 3:4], rsum[:, 2:3]))
                    step_(V.tensor_scalar(rt[:, 7, :], rt[:, 6, :], rsum[:, 3:4], LORA_SCALING, ALU.mult, ALU.mult))
                    if t >= 1:
                        dve.wait_ge(sm["hwT_mm"], t)
                    wb = rt[:, 7, :].rearrange("p (e a) -> p e a", a=1).to_broadcast([P, E, R])
                    V.tensor_tensor(hw.rearrange("p (e r) -> p e r", e=E), M0[:, 0:ER].rearrange("p (e r) -> p e r", e=E),
                                    wb, ALU.mult).then_inc(sm["hw_done"], 1)
                if u < NT:
                    softmax_rows(u, 1)
                if t >= 0:
                    dve.wait_ge(sm["hwT_mm"], t + 1)
                    if t >= 1:
                        dve.wait_ge(sm["lora_mm"], t)
                    V.tensor_copy(hwT, M1[:, 0:ER]).then_inc(sm["hwT_done"], 1)
                if u < NT:
                    softmax_rows(u, 2)
                    softmax_rows(u, 3)
                    normalise(u, 0)
                if t >= 0:
                    dve.wait_ge(sm["lora_mm"], t + 1)
                    dve.wait_ge(sm["xb2_done"], t + 1)
                    dve.wait_ge(sm["x2_done"], t + 1)
                    ins = V.tensor_tensor(y, base_ps, xbias[:, 1, :], ALU.add)
                    ins.then_inc(sm["y3_done"], 1)
                    dve.wait_ge(sm["y3_done"], t + 1)
                    norm_stats(y, "v3_done")
                if u < NT:
                    softmax_rows(u, 4)
                    normalise(u, 1)
                if t >= 0:
                    dve.wait_ge(sm["r3_done"], t + 1)
                    dve.wait_ge(sm["v3_done"], t + 1)
                    V.tensor_scalar(y, y, mv[:, 0:1], rstd[:, 0:1], ALU.subtract, ALU.mult).then_inc(sm["x3_done"], 1)
                if u < NT:
                    for g in range(5, 8):
                        softmax_rows(u, g)
                        normalise(u, g - 3)
                    for g in range(5, 8):
                        normalise(u, g)


GENERAL = True
FORCE = False

_INS = ['x', 'ctx_4096', 'L0_attn_w_gate', 'L0_attn_w_up', 'L0_attn_w_down', 'L0_xattn_Wq', 'L0_xattn_bq',
        'L0_xattn_Wk', 'L0_xattn_bk', 'L0_xattn_Wv', 'L0_xattn_bv', 'L0_xattn_interference', 'L0_xattn_amp',
        'L0_xattn_Wo', 'L0_xattn_bo', 'L0_ffn_W_base', 'L0_ffn_b_base', 'L0_ffn_W_router', 'L0_ffn_lora_A',
        'L0_ffn_lora_B']


def kernel(**inputs):
    import numpy as _np
    import concourse.bacc as _bacc
    from concourse import mybir as _mybir
    from concourse.bass_utils import run_bass_kernel_spmd as _run

    nc = _bacc.Bacc("TRN2", target_bir_lowering=False, num_devices=1)
    arrays, args = {}, []
    for name in _INS:
        a = _np.ascontiguousarray(inputs[name])
        arrays[f"in_{name}"] = a
        args.append(nc.dram_tensor(f"in_{name}", a.shape, _mybir.dt.from_np(a.dtype), kind="ExternalInput").ap())
    shape = inputs['x'].shape
    args.append(nc.dram_tensor("out", tuple(shape), _mybir.dt.float32, kind="ExternalOutput").ap())
    decoder_kernel(nc, *args)
    r = _run(nc, [arrays], core_ids=[0])
    return r.results[0]["out"]
```

```python
from contextlib import ExitStack

import concourse.bass as bass
from concourse import mybir

P = 128
F32 = mybir.dt.float32
F32R = mybir.dt.float32r
BF16 = mybir.dt.bfloat16
I32 = mybir.dt.int32
ALU = mybir.AluOpType
ACT = mybir.ActivationFunctionType
AX = mybir.AxisListType
BIG = 1.0e38
EPS = 1e-5
LORA_SCALING = 2.0

GUESS, SLOPE = 0.78, 0.83
STEPS = (1.0, 1.0, 0.5)
COUNTS = len(STEPS) + 1
CANDIDATES = 16


def decoder_kernel(nc, x, ctx_in, w_gate, w_up, w_down, wq, bq, wk, bk, wv, bv, interference, amp, wo, bo,
                   w_base, b_base, w_router, lora_a, lora_b, out):
    B, S, D = x.shape
    I = w_gate.shape[0]
    NH, M, _ = interference.shape
    DK = D // (NH * M)
    E, R, _ = lora_a.shape
    T = B * S
    NT = T // P
    KC = D // P
    IC = (I + P - 1) // P
    IREM = I - (IC - 1) * P
    KEEP_OUT = I // 2
    AIM = KEEP_OUT - 5
    HC = NH // KC
    BT = P // S
    W33 = M * DK + 1
    ER = E * R
    assert S * 2 == P and M == 4 and DK == 8 and HC == 4 and ER == P and D == 512

    xf = x.rearrange("b s d -> (b s) d")
    cf = ctx_in.rearrange("b s d -> (b s) d")
    of = out.rearrange("b s d -> (b s) d")

    with ExitStack() as stack:
        def sb(name, shape, dt=F32):
            return stack.enter_context(nc.sbuf_tensor(name, shape, dt))

        def sem(name):
            return stack.enter_context(nc.semaphore(name))

        ident = sb("ident", [P, P])
        blk = sb("blk", [P, KC, P])
        int_hi = sb("int_hi", [M * NH, M])
        alpha = sb("alpha", [P, 1])
        mcol = sb("mcol", [P, M])
        half = sb("half", [P, 1])
        iota16 = sb("iota16", [P, CANDIDATES + 1])
        bits = sb("bits", [P, 32], I32)
        bcol = sb("bcol", [P, 3, KC])
        bk_f = sb("bk_f", [P, KC])
        bq_f = sb("bq_f", [P, KC])
        bv_f = sb("bv_f", [P, D])
        bo_f = sb("bo_f", [P, D])
        bb_f = sb("bb_f", [P, D])
        SLOTS = 2
        stage = sb("stage", [P, SLOTS, 4 * D])
        wsplit = sb("wsplit", [P, 4 * KC * I], F32R)
        xsplit = sb("xsplit", [P, 8 * D], F32R)

        def split_pair(buf, at, n):
            return buf[:, at:at + n], buf[:, at + n:at + 2 * n]

        def chunked(pair, c):
            return tuple(v.rearrange("p (c n) -> p c n", c=c) for v in pair)

        wg2 = chunked(split_pair(wsplit, 0, KC * I), KC)
        wu2 = chunked(split_pair(wsplit, 2 * KC * I, KC * I), KC)
        wk2, wq2, wv2, wo2, wb2 = (chunked(split_pair(wsplit, 2 * n * KC * D, KC * D), KC) for n in range(5))
        xT2 = [chunked(split_pair(xsplit, 2 * n * D, D), KC) for n in range(2)]
        pairT2 = chunked(split_pair(xsplit, 0, 2 * D), KC)
        x2T2 = chunked(split_pair(xsplit, 4 * D, D), KC)
        aT2 = tuple(v.rearrange("p (a j t) -> p a j t", a=2, j=2) for v in split_pair(xsplit, 4 * D, D))
        arT = sb("arT", [P, KC, ER + E])
        wdT = sb("wdT", [P, IC, D])
        lbT = sb("lbT", [P, D])
        xs = sb("xs", [P, NT, D])
        WORK = 5 * I + I // 2 + IC * P + D
        work = sb("work", [P, WORK])
        o = 0

        def carve(n):
            nonlocal o
            v = work[:, o:o + n]
            o += n
            assert o <= WORK
            return v

        mag = [carve(I) for _ in range(2)]
        prod = [carve(I) for _ in range(2)]
        cand = carve(I)
        junk = carve(I // 2).bitcast(BF16)
        o_setup = o
        hT = carve(IC * P).rearrange("p (c t) -> p c t", c=IC)
        y1 = carve(D)
        o = o_setup
        spread = carve(D)[0:M * NH].rearrange("p (c n) -> p c n", c=KC)
        blk_tmp = carve(D).rearrange("p (c n) -> p c n", c=KC)
        bcol_bc = carve(D).rearrange("p (c n) -> p c n", c=KC)
        same_hd = carve(P)
        ones = carve(P)
        o = 0
        cnat = [carve(D) for _ in range(2)]
        kb, qb = (carve(2 * D).rearrange("p (c t) -> p c t", c=KC) for _ in range(2))
        attn_n = carve(BT * D // 2).rearrange("p (b f) -> p b f", b=BT)
        x2 = carve(D)
        pT = [carve(D) for _ in range(2)]
        yb = carve(2 * D).rearrange("p (a n) -> p a n", a=2)
        xbias = carve(2 * D).rearrange("p (a n) -> p a n", a=2)
        wd_flat = wdT[:].rearrange("p a n -> p (a n)")
        kx = wd_flat[:, 0:2048].rearrange("p (c b h k) -> p c b h k", c=KC, b=BT, h=HC)
        qx = wd_flat[:, 2048:4096].rearrange("p (c b m q) -> p c b m q", c=KC, b=BT, m=M)
        VX = BT * NH * W33
        st_flat = stage[:].rearrange("p s n -> p (s n)")
        sub = [st_flat[:, n * D:(n + 1) * D] for n in range(2)]
        pr = [st_flat[:, (2 + n) * D:(3 + n) * D] for n in range(2)]
        x2Tf = st_flat[:, 4 * D:5 * D]
        hw = st_flat[:, 5 * D:5 * D + ER]
        hwT = st_flat[:, 5 * D + ER:5 * D + 2 * ER]
        vx_flat = [wd_flat[:, 4096:4096 + VX], carve(VX), carve(VX), st_flat[:, 5 * D + 2 * ER:5 * D + 2 * ER + VX]]
        VXN = len(vx_flat)
        vx = [v.rearrange("p (b a h w) -> p b a h w", b=BT, a=NH // 2, h=2) for v in vx_flat]
        msum = sb("msum", [P, 2])
        step = sb("step", [P, 4])
        tcol = sb("tcol", [P, COUNTS])
        tpre = sb("tpre", [P, 1])
        ccol = sb("ccol", [P, COUNTS])
        okc = sb("okc", [P, COUNTS])
        okt = sb("okt", [P, COUNTS])
        lo = sb("lo", [P, 4])
        top = sb("top", [P, CANDIDATES + 1])
        pick = sb("pick", [P, CANDIDATES + 1])
        pick2 = sb("pick2", [P, CANDIDATES + 1])
        thr = sb("thr", [P, 2])
        flag = sb("flag", [P, 4])
        flag_all = sb("flag_all", [P, 1])
        stats = sb("stats", [P, 6])
        mv = sb("mv", [P, 2])
        veps = sb("veps", [P, 1])
        rstd = sb("rstd", [P, 1])
        smax = sb("smax", [P, 2, 8])
        rden = sb("rden", [P, 8])
        rt = sb("rt", [P, 8, 8])
        re = sb("re", [P, 8])
        rsum = sb("rsum", [P, 4])

        ps = stack.enter_context(nc.psum_tensor("ps", [P, 8, 512], F32))
        def x2T_bank(t):
            return ps[:, 7 if t % 2 == 0 else 6, :]

        gate_ps = ps[:, 0:3, :].rearrange("p b n -> p (b n)")
        up_ps = ps[:, 3:6, :].rearrange("p b n -> p (b n)")
        M0, M1 = ps[:, 6, :], ps[:, 7, :]
        score_ps = [ps[:, 0, :], ps[:, 1, :]]
        ptr_ps = [ps[:, 2, :], ps[:, 3, :]]
        av_ps, base_ps = ps[:, 4, :], ps[:, 5, :]

        names = """x_first x_rest small_loaded pool_const ints_up ints_done blk_done bias_mm bias_done
            unit_mm unit_act unit_dve ctx_loaded0 ctx_loaded1 out_stored0 out_stored1
            xT_mm xT_done gate_mm silu_done mag_done up_mm prod_done masked bad_seen flag_summed
            hT_mm hT_done down_mm y1_done v1_done r1_done x1_done
            x1T_mm x1T_done x1T_lo cT_mm cT_done cT_lo aT_mm aT_done aT_lo x2T_lo xT_lo o_mm y2_done v2_done r2_done x2_done xb1_done xb2_done
            k_mm kb_done kx_done q_mm qb_done qx_done v_mm vx_done
            x2T_mm x2T_done x2Tf_done ar_mm base_mm rmax_done rexp_done hw_done max_done rden_done router_step hwT_mm hwT_done lora_mm y3_done v3_done r3_done
            x3_done score_mm sub_done exp_done ptr_mm pT_done av_mm av_done dve_step act_step pool_step vx_zero
            attn_read""".split()
        sm = {n: sem(n) for n in names}
        stage_sem = [sem(f"stage{i}") for i in range(SLOTS + 3)]

        panels = []
        def panel(loads, units):
            panels.append((loads, units))

        EXTRA = 3
        slot_no = [n if n < SLOTS + EXTRA else (n - SLOTS - EXTRA) % SLOTS for n in range(15)]

        def slot_of():
            n = slot_no[len(panels)]
            return stage[:, n, :] if n < SLOTS else work[:, (n - SLOTS) * 4 * D:(n - SLOTS + 1) * 4 * D]

        def rows_panel(w, dstT, p0):
            st = slot_of().rearrange("p (r d) -> p r d", d=D)
            n = min(4, IC - p0)
            full = n if p0 + n < IC or IREM == P else n - 1
            loads = [(st[:, 0:full, :], w[p0 * P:(p0 + full) * P, :].rearrange("(r p) d -> p r d", p=P))]
            if full < n:
                loads.append((st[0:IREM, full, :], w[(p0 + full) * P:I, :]))
            cols = full * P + (IREM if full < n else 0)
            units = []
            for ic in range(KC):
                mms = []
                for r in range(n):
                    k = P if r < full else IREM
                    mms.append((slice(r * P, r * P + k), st[0:k, r, ic * P:(ic + 1) * P], ident[0:k, 0:k], P))
                units.append((mms, tuple(v[:, ic, p0 * P:p0 * P + cols] for v in dstT), P, cols))
            panel(loads, units)

        def down_panel(p0):
            n = min(4, IC - p0)
            cols = min(I - p0 * P, n * P)
            st = slot_of().rearrange("p (r d) -> p r d", d=D)
            loads = [(st[:, :, 0:cols], w_down[:, p0 * P:p0 * P + cols].rearrange("(r p) i -> p r i", p=P))]
            units = []
            for c in range(n):
                m = min(P, cols - c * P)
                mms = [(slice(oc * P, oc * P + P), st[:, oc, c * P:c * P + m], ident[:, :], m) for oc in range(KC)]
                units.append((mms, (wdT[0:m, p0 + c, :],), m, D))
            panel(loads, units)

        def square_panel(w, dstT, kind):
            st = slot_of().rearrange("p (r d) -> p r d", d=D)
            loads = [(st[:, :, :], w.rearrange("(r p) d -> p r d", p=P))]
            units = []
            for ic in range(KC):
                mms = []
                for oc in range(KC):
                    if kind == "wo":
                        a = (ic // 2) * 2 * P + ic % 2
                        lhs = st[:, oc, a:a + 2 * P - 1:2]
                    else:
                        lhs = st[:, oc, ic * P:(ic + 1) * P]
                    rhs = blk[:, oc, :] if kind == "qkv" else ident[:, :]
                    mms.append((slice(oc * P, oc * P + P), lhs, rhs, P))
                units.append((mms, tuple(v[:, ic, :] for v in dstT), P, D))
            panel(loads, units)

        for p0 in range(0, IC, 4):
            rows_panel(w_gate, wg2, p0)
        for p0 in range(0, IC, 4):
            rows_panel(w_up, wu2, p0)
        for p0 in range(0, IC, 4):
            down_panel(p0)
        square_panel(wk, wk2, "qkv")
        square_panel(wv, wv2, "qkv")
        square_panel(wq, wq2, "qkv")
        square_panel(wo, wo2, "wo")
        square_panel(w_base, wb2, "plain")
        st = slot_of()
        loads = [(st[:, 0:D], lora_a.rearrange("e r d -> (e r) d")),
                 (st[0:E, 2 * D:3 * D], w_router)]
        for oc in range(KC):
            loads.append((st[:, D + oc * P:D + (oc + 1) * P].rearrange("p (e r) -> p e r", e=E),
                          lora_b[:, oc * P:(oc + 1) * P, :].rearrange("e p r -> p e r")))
        panel(loads, [
            ([(slice(ic * P, ic * P + P), st[:, ic * P:(ic + 1) * P], ident[:, :], P) for ic in range(KC)],
             (arT[:, :, 0:ER],), P, D),
            ([(slice(ic * E, ic * E + E), st[0:E, 2 * D + ic * P:2 * D + (ic + 1) * P], ident[0:E, 0:E], P) for ic in range(KC)],
             (arT[:, :, ER:ER + E],), P, KC * E),
            ([(slice(oc * P, oc * P + P), st[:, D + oc * P:D + (oc + 1) * P], ident[:, :], P) for oc in range(KC)],
             (lbT[:, :],), P, D)])

        units_all = []
        unit_end = []
        splits = 0
        for n, (_, units) in enumerate(panels):
            for unit in units:
                u = len(units_all)
                splits += len(unit[1]) == 2
                units_all.append((n, unit, u + 1, splits))
            unit_end.append(len(units_all))
        GATE_UP = range(0, unit_end[5])
        DOWN = range(unit_end[5], unit_end[8])
        REST = range(unit_end[8], len(units_all))
        NUNITS = len(units_all)
        R0, R1 = 4, 4 + IC

        def bank_of(u):
            if u in GATE_UP:
                return (0, 1, 2, 3, 4, 5, 7)[u % 7]
            if u in DOWN:
                return 7 if (u - DOWN[0]) % 2 else 6
            return (u - REST[0]) % 6

        def evac_of(u):
            _, unit, nth, nsplit = units_all[u]
            return (sm["unit_dve"], nsplit) if len(unit[1]) == 2 else (sm["unit_act"], nth)

        def last_in(bank, before):
            return max(u for u in range(before) if bank_of(u) == bank)

        stage_count = []
        cnt = [0] * (SLOTS + EXTRA)
        for n, (loads, _) in enumerate(panels):
            cnt[slot_no[n]] += 16 * len(loads)
            stage_count.append(cnt[slot_no[n]])

        block = stack.enter_context(nc.Block())

        def unit_src(u, dst):
            _, (_, _, rows, cols), _, _ = units_all[u]
            src = ps[0:rows, bank_of(u), 0:cols]
            return src.rearrange("p (a b) -> p a b", a=dst.shape[1]) if len(dst.shape) == 3 else src

        def units_hi(act, which):
            for u in which:
                act.wait_ge(sm["unit_mm"], u + 1)
                dst = units_all[u][1][1][0]
                nc.scalar.activation(dst, unit_src(u, dst), ACT.Copy).then_inc(sm["unit_act"], 1)

        def units_lo(dve, which):
            for u in which:
                dst = units_all[u][1][1]
                if len(dst) == 2:
                    dve.wait_ge(sm["unit_act"], u + 1)
                    nc.vector.tensor_tensor(dst[1], unit_src(u, dst[0]), dst[0].bitcast(F32),
                                            ALU.subtract).then_inc(sm["unit_dve"], 1)

        @block.sync
        def _(sp):
            def load_ctx(k):
                if k >= 2:
                    sp.wait_ge(sm["cT_mm"], k - 1)
                sp.dma_start(cnat[k % 2], cf[k * P:(k + 1) * P, :]).then_inc(sm[f"ctx_loaded{k % 2}"], 16)

            sp.dma_start(xs[:, 0, :], xf[0:P, :]).then_inc(sm["x_first"], 16)
            for n, (loads, _) in enumerate(panels):
                before = [v for v in range(n) if slot_no[v] == slot_no[n]]
                if before:
                    sp.wait_ge(sm["unit_mm"], unit_end[before[-1]])
                if n == 11:
                    sp.wait_ge(sm["masked"], NT - 1)
                    load_ctx(0)
                    load_ctx(1)
                for dst, src in loads:
                    sp.dma_start(dst, src).then_inc(stage_sem[slot_no[n]], 16)
                if n == 5:
                    sp.dma_start(xs[:, 1:NT, :], xf[P:T, :].rearrange("(t p) d -> p t d", p=P)).then_inc(sm["x_rest"], 16)

            for k in range(2, 4):
                load_ctx(k)
            for u in range(NT + 2):
                if u % 2 == 0:
                    for k in (u + 4, u + 5):
                        if k < NT:
                            load_ctx(k)
                w = u - 2
                if w >= 0:
                    sp.wait_ge(sm["x3_done"], w + 1)
                    sp.dma_start(of[w * P:(w + 1) * P, :], yb[:, w % 2, :]).then_inc(sm[f"out_stored{w % 2}"], 16)
            sp.wait_ge(sm["out_stored0"], 8 * NT)
            sp.wait_ge(sm["out_stored1"], 8 * NT)

        @block.gpsimd
        def _(pool):
            k = [0]

            def step_(ins):
                k[0] += 1
                ins.then_inc(sm["pool_step"], 1)
                pool.wait_ge(sm["pool_step"], k[0])

            pool.dma_start(int_hi[:, :], interference.rearrange("h i j -> (h i) j")).then_inc(sm["small_loaded"], 16)
            pool.dma_start(alpha[:, :], amp.rearrange("(a n) -> a n", a=1).to_broadcast([P, 1])).then_inc(sm["small_loaded"], 16)
            for n, b in enumerate((bk, bq, bv)):
                with nc.allow_non_contiguous_dma(reason="512 words, once"):
                    pool.dma_start(bcol[:, n, :], b.rearrange("(c p) -> p c", p=P)).then_inc(sm["small_loaded"], 16)
            for n, (b, d) in enumerate(((bo, bo_f), (b_base, bb_f))):
                pool.dma_start(d[:, :], b.rearrange("(a n) -> a n", a=1).to_broadcast([P, D])).then_inc(sm["small_loaded"], 16)
            step_(nc.gpsimd.memset(ident[:], 0.0))
            nc.gpsimd.affine_select(out=ident[:], in_=ident[:], compare_op=ALU.not_equal, fill=1.0, base=0,
                                    pattern=[[-1, P]], channel_multiplier=1).then_inc(sm["pool_const"], 1)
            step_(nc.gpsimd.memset(same_hd, 1.0))
            v = same_hd.rearrange("p (a j) -> p a j", j=M)
            step_(nc.gpsimd.affine_select(out=v, in_=v, compare_op=ALU.is_ge, fill=0.0, base=0,
                                          pattern=[[-M, P // M], [0, M]], channel_multiplier=1))
            nc.gpsimd.affine_select(out=v, in_=v, compare_op=ALU.is_ge, fill=0.0, base=M - 1,
                                    pattern=[[M, P // M], [0, M]], channel_multiplier=-1).then_inc(sm["pool_const"], 1)
            step_(nc.gpsimd.memset(spread, 0.0))
            v = spread.rearrange("p c (h d i) -> p (c h) d i", h=HC, d=DK)
            nc.gpsimd.affine_select(out=v, in_=v, compare_op=ALU.not_equal, fill=1.0, base=0,
                                    pattern=[[-M, NH], [0, DK], [-1, M]], channel_multiplier=1).then_inc(sm["pool_const"], 1)
            nc.gpsimd.memset(ones, 1.0).then_inc(sm["pool_const"], 1)
            nc.gpsimd.memset(half[:], -0.5).then_inc(sm["pool_const"], 1)
            nc.gpsimd.iota(iota16[:], pattern=[[1, CANDIDATES + 1]], base=0, channel_multiplier=0,
                           allow_small_or_imprecise_dtypes=True).then_inc(sm["pool_const"], 1)
            for b in range(31):
                nc.gpsimd.memset(bits[:, b:b + 1], 1 << (30 - b))
            ins = nc.gpsimd.memset(bits[:, 31:32], 0)
            ins.then_inc(sm["pool_const"], 1)

            def rstd_(stage_v, stage_r, t):
                pool.wait_ge(sm[stage_v], t + 1)
                step_(nc.gpsimd.tensor_scalar(veps[:], mv[:, 1:2], EPS, None, ALU.add))
                nc.gpsimd.tensor_tensor(rstd[:], veps[:], half[:], ALU.pow).then_inc(sm[stage_r], 1)

            for t in range(NT):
                pool.wait_ge(sm["bad_seen"], t + 1)
                nc.gpsimd.partition_all_reduce(flag_all[:], flag[:, 2:3], P,
                                               bass.bass_isa.ReduceOp.max).then_inc(sm["flag_summed"], 1)
                if t >= 1:
                    rstd_("v1_done", "r1_done", t - 1)
            pool.wait_ge(sm["down_mm"], NT)
            step_(nc.gpsimd.memset(kx, 0.0))
            rstd_("v1_done", "r1_done", NT - 1)
            pool.wait_ge(sm["r1_done"], NT)
            pool.wait_ge(sm["x1_done"], NT)

            def vx_zeros(j):
                nc.gpsimd.memset(vx_flat[j], 0.0).then_inc(sm["vx_zero"], 1)
                for h2 in range(2):
                    pool.wait_ge(sm["vx_zero"], 3 * j + h2 + 1)
                    nc.gpsimd.memset(vx[j][S * h2:S * h2 + S, :, :, h2, W33 - 1:W33], 1.0).then_inc(sm["vx_zero"], 1)
                pool.wait_ge(sm["vx_zero"], 3 * j + 3)

            for j in range(VXN - 1):
                vx_zeros(j)

            def keys_out(u, b):
                hf = 2 * u + b
                pool.wait_ge(sm["kb_done"], 2 * (u // 2) + 2)
                if hf >= 2:
                    pool.wait_ge(sm["score_mm"], 4 * (hf - 1))
                for h in range(HC):
                    q0 = 32 * h
                    nc.gpsimd.tensor_copy(kx[q0:q0 + 32, :, b, h, :],
                                          kb[q0:q0 + 32, :, (u % 2) * P + b * S:(u % 2) * P + b * S + S]
                                          ).then_inc(sm["kx_done"], 1)
                    pool.wait_ge(sm["kx_done"], HC * hf + h + 1)

            pool.wait_ge(sm["unit_mm"], NUNITS)
            vx_zeros(VXN - 1)
            keys_out(0, 0)
            for u in range(NT + 2):
                t, w = u - 1, u - 2
                if u < NT:
                    keys_out(u, 1)
                if 0 <= t < NT:
                    if t >= 1:
                        pool.wait_ge(sm["y2_done"], t)
                    nc.gpsimd.tensor_tensor(xbias[:, 0, :], xs[:, t, :], bo_f[:], ALU.add).then_inc(sm["xb1_done"], 1)
                if w >= 0:
                    rstd_("v3_done", "r3_done", w)
                if 0 <= t < NT:
                    rstd_("v2_done", "r2_done", t)
                    pool.wait_ge(sm["x2_done"], t + 1)
                    if t >= 1:
                        pool.wait_ge(sm["y3_done"], t)
                    nc.gpsimd.tensor_tensor(xbias[:, 1, :], x2, bb_f[:], ALU.add).then_inc(sm["xb2_done"], 1)
                    pool.wait_ge(sm["xb2_done"], t + 1)
                if u + 1 < NT:
                    keys_out(u + 1, 0)

        @block.tensor
        def _(pe):
            mm = nc.tensor.matmul
            pe.wait_ge(sm["pool_const"], 1)

            def interference_blocks():
                pe.wait_ge(sm["pool_const"], 6)
                pe.wait_ge(sm["small_loaded"], 16 * 7)
                pe.wait_ge(*evac_of(last_in(7, len(GATE_UP))))
                for c in range(KC):
                    ins = mm(ps[:, 7, c * M:(c + 1) * M], spread[:, c, :], int_hi[:, :], start=True, stop=True)
                ins.then_inc(sm["ints_up"], 1)

            def folded_biases():
                for bank in (6, 7):
                    pe.wait_ge(*evac_of(last_in(bank, NUNITS - len(REST))))
                for c in range(KC):
                    mm(ps[:, 6, c:c + 1], blk[:, c, :], bcol[:, 0, c:c + 1], start=True, stop=True)
                    mm(ps[:, 6, KC + c:KC + c + 1], blk[:, c, :], bcol[:, 1, c:c + 1], start=True, stop=True)
                for c in range(KC):
                    ins = mm(ps[:, 7, c * P:(c + 1) * P], bcol_bc[:, c, :], blk[:, c, :], start=True, stop=True)
                ins.then_inc(sm["bias_mm"], 1)

            def mm3(dst, a, b, first=True, last=True):
                mm(dst, a[1], b[0], start=first, stop=False)
                mm(dst, a[0], b[1], start=False, stop=False)
                return mm(dst, a[0], b[0], start=False, stop=last)

            def turn_units(which, first=None):
                for u in which:
                    n, (mms, _, rows, cols), _, _ = units_all[u]
                    if u == (unit_end[n - 1] if n else 0):
                        pe.wait_ge(stage_sem[slot_no[n]], stage_count[n])
                    bank = bank_of(u)
                    if any(bank_of(v) == bank for v in range(which[0] if first is None else first, u)):
                        pe.wait_ge(*evac_of(last_in(bank, u)))
                    for cs, lhs, rhs, m in mms:
                        ins = mm(ps[0:m, bank, cs], lhs, rhs, start=True, stop=True,
                                 is_transpose=None if rhs.tensor is blk[:].tensor else True)
                    ins.then_inc(sm["unit_mm"], 1)

            def x_turn(t):
                pe.wait_ge(sm["x_first" if t == 0 else "x_rest"], 16)
                if t == 1:
                    pe.wait_ge(sm["xT_lo"], 1)
                if t == 2:
                    pe.wait_ge(sm["bias_done"], 2)
                if t >= 3:
                    pe.wait_ge(sm["y1_done"], t - 2)
                for c in range(KC):
                    ins = nc.tensor.transpose(M0[:, c * P:(c + 1) * P], xs[:, t, c * P:(c + 1) * P], ident[:])
                ins.then_inc(sm["xT_mm"], 1)

            def gate_up(t):
                pe.wait_ge(sm["xT_lo"], t + 1)
                for w, acc, done, free in ((wg2, gate_ps, "gate_mm", "silu_done"), (wu2, up_ps, "up_mm", "prod_done")):
                    if t >= 1:
                        pe.wait_ge(sm[free], t)
                    for n0 in range(0, I, 512):
                        n1 = min(I, n0 + 512)
                        for c in range(KC):
                            ins = mm3(acc[:, n0:n1], [v[:, c, :] for v in xT2[t % 2]], [v[:, c, n0:n1] for v in w],
                                      c == 0, c == KC - 1)
                    ins.then_inc(sm[done], 1)
                    if done == "gate_mm" and t + 1 < NT:
                        x_turn(t + 1)

            def h_turn_down(t, beside=()):
                if t >= 1:
                    pe.wait_ge(sm["hT_done"], 3 * t)
                pe.wait_ge(sm["masked"], t + 1)
                for g in range(3):
                    bank = M1 if g % 2 == 0 else M0
                    if g == 1:
                        pe.wait_ge(sm["xT_lo"], min(t + 3, NT))
                        if t >= NT - 2:
                            pe.wait_ge(sm["y1_done"], t)
                    if g == 2:
                        pe.wait_ge(sm["hT_done"], 3 * t + 1)
                    n = min(4, IC - 4 * g)
                    for r in range(n):
                        i0 = (4 * g + r) * P
                        m = min(P, I - i0)
                        ins = nc.tensor.transpose(bank[0:m, r * P:(r + 1) * P], prod[t % 2][:, i0:i0 + m], ident[:])
                    ins.then_inc(sm["hT_mm"], 1)
                pe.wait_ge(sm["hT_done"], 3 * t + 2)
                for c in range(IC):
                    m = min(P, I - c * P)
                    if c == 8:
                        pe.wait_ge(sm["hT_done"], 3 * t + 3)
                    ins = mm(M0[:, :], hT[0:m, c, :], wdT[0:m, c, :], start=(c == 0), stop=(c == IC - 1))
                    if c < len(beside):
                        turn_units(beside[c:c + 1], REST[0])
                ins.then_inc(sm["down_mm"], 1)

            x_turn(0)
            turn_units(GATE_UP)
            interference_blocks()
            for bank in range(6):
                pe.wait_ge(*evac_of(last_in(bank, len(GATE_UP))))
            gate_up(0)
            pe.wait_ge(sm["xT_lo"], 2)
            pe.wait_ge(sm["blk_done"], 1)
            turn_units(DOWN)
            folded_biases()
            for t in range(NT):
                if t + 1 < NT:
                    gate_up(t + 1)
                if t == NT - 1:
                    pe.wait_ge(sm["silu_done"], NT)
                    pe.wait_ge(sm["prod_done"], NT)
                    turn_units(REST[0:R0])
                h_turn_down(t, REST[R0:R1] if t == NT - 1 else ())

            def turn4(bank, src, done):
                for c in range(KC):
                    ins = nc.tensor.transpose(bank[:, c * P:(c + 1) * P], src[:, c * P:(c + 1) * P], ident[:])
                ins.then_inc(sm[done], 1)

            def ctx_turn(k, bank):
                pe.wait_ge(sm[f"ctx_loaded{k % 2}"], 16 * (k // 2 + 1))
                turn4(bank, cnat[k % 2], "cT_mm")

            def project_turned(w2, bank, fs, done=None):
                for f in fs:
                    for c in range(KC):
                        ins = mm3(bank[:, (f % 2) * 2 * P:(f % 2 + 1) * 2 * P], [v[:, c, f * P:(f + 1) * P] for v in w2],
                                  [v[:, c, :] for v in pairT2], c == 0, c == KC - 1)
                if done:
                    ins.then_inc(sm[done], 1)

            def attn_turn(t):
                pe.wait_ge(sm["av_done"], 8 * (t + 1))
                for b in range(BT):
                    for a in range(2):
                        ins = nc.tensor.transpose(M0[:, (2 * b + a) * P:(2 * b + a + 1) * P],
                                                  attn_n[:, b, a * P:(a + 1) * P], ident[:])
                ins.then_inc(sm["aT_mm"], 1)

            def values(k):
                pe.wait_ge(sm["cT_lo"], k + 1)
                cols = slice((k % 2) * P, (k % 2 + 1) * P)
                for c in range(KC):
                    ins = mm3(M1[:, :], [v[:, c, cols] for v in pairT2], [v[:, c, :] for v in wv2], c == 0, c == KC - 1)
                ins.then_inc(sm["v_mm"], 1)

            def attn_out(t):
                pe.wait_ge(sm["aT_lo"], t + 1)
                for a in range(2):
                    for j in range(2):
                        ins = mm3(M0[:, :], [v[:, a, j, :] for v in aT2], [v[:, 2 * a + j, :] for v in wo2],
                                  a + j == 0, a + j == 2)
                ins.then_inc(sm["o_mm"], 1)

            def x2_turn(t):
                pe.wait_ge(sm["x2_done"], t + 1)
                turn4(x2T_bank(t), x2, "x2T_mm")

            def lora_router_in(t):
                pe.wait_ge(sm["x2T_lo"], t + 1)
                for c in range(KC):
                    ins = mm(M1[:, 0:ER + E], x2Tf[:, c * P:(c + 1) * P], arT[:, c, :], start=(c == 0), stop=(c == KC - 1))
                ins.then_inc(sm["ar_mm"], 1)

            def base_part(t, cs):
                if t >= 1:
                    pe.wait_ge(sm["y3_done"], t)
                for c in cs:
                    ins = mm3(base_ps, [v[:, c, :] for v in x2T2], [v[:, c, :] for v in wb2], c == 0, False)
                if cs[-1] == KC - 1:
                    ins.then_inc(sm["base_mm"], 1)

            def lora_turn(t):
                pe.wait_ge(sm["hw_done"], t + 1)
                nc.tensor.transpose(M0[:, 0:ER], hw, ident[:]).then_inc(sm["hwT_mm"], 1)

            def lora_out(t):
                pe.wait_ge(sm["hwT_done"], t + 1)
                mm(base_ps, hwT, lbT[:, :], start=False, stop=True).then_inc(sm["lora_mm"], 1)

            def scores(u, g):
                b, c = divmod(g, KC)
                n = 8 * u + g
                if c == 0:
                    pe.wait_ge(sm["kx_done"], HC * (n // 4 + 1))
                    pe.wait_ge(sm["qx_done"], M * (n // 4 + 1))
                if n >= 2:
                    pe.wait_ge(sm["sub_done"], n - 1)
                for mp in range(2):
                    ins = mm(score_ps[g % 2][:, mp * 256:(mp + 1) * 256],
                             qx[:, c, b, 2 * mp:2 * mp + 2, :], kx[:, c, b, :, :], start=True, stop=True)
                ins.then_inc(sm["score_mm"], 1)

            def prob_turn(u, g):
                n = 8 * u + g
                pe.wait_ge(sm["exp_done"], n + 1)
                if n >= 2:
                    pe.wait_ge(sm["pT_done"], n - 1)
                for k4 in range(4):
                    ins = nc.tensor.transpose(ptr_ps[g % 2][:, k4 * P:(k4 + 1) * P],
                                              pr[g % 2][:, k4 * P:(k4 + 1) * P], ident[:])
                ins.then_inc(sm["ptr_mm"], 1)

            def weighted_v(u, g):
                b, c = divmod(g, KC)
                n = 8 * u + g
                pe.wait_ge(sm["pT_done"], n + 1)
                if n >= 1:
                    pe.wait_ge(sm["av_done"], n)
                for mp in range(2):
                    for hp in range(2):
                        o0 = (mp * 2 + hp) * 2 * W33
                        k4 = 2 * mp + hp
                        ins = mm(av_ps[:, o0:o0 + 2 * W33], pT[g % 2][:, k4 * P:(k4 + 1) * P],
                                 vx[u % VXN][:, b, 2 * c + hp, :, :], start=True, stop=True)
                ins.then_inc(sm["av_mm"], 1)

            FIRST_PAIR = ("ctx_a", "ctx_b", "k_0", "k_1", "v_a", "v_b", "x_a", "x_b", "q_0", "q_1")

            def prepare(p, part):
                a, b = 2 * p, 2 * p + 1
                if part == "ctx_a":
                    ctx_turn(a, M1)
                elif part == "ctx_b":
                    if a >= 3:
                        pe.wait_ge(sm["hwT_done"], a - 3)
                    ctx_turn(b, M0)
                elif part == "v_a":
                    if p == 0:
                        pe.wait_ge(sm["kb_done"], 1)
                    values(a)
                elif part == "v_b":
                    pe.wait_ge(sm["vx_done"], 4 * (a + 1))
                    values(b)
                elif part == "k_0":
                    if p == 0:
                        pe.wait_ge(sm["cT_lo"], 2)
                    else:
                        pe.wait_ge(sm["vx_done"], 4 * (b + 1))
                    project_turned(wk2, M1, (0, 1), "k_mm")
                elif part == "k_1":
                    if p >= 1:
                        pe.wait_ge(sm["hwT_done"], max(b - 3, 0)) if b > 3 else None
                    project_turned(wk2, M0, (2, 3), "k_mm")
                elif part == "x_a":
                    if p == 0:
                        pe.wait_ge(sm["vx_done"], 4 * 2)
                    pe.wait_ge(sm["kb_done"], 2 * p + 1)
                    turn4(M1, xs[:, a, :], "x1T_mm")
                elif part == "x_b":
                    pe.wait_ge(sm["x1T_lo"], a + 1)
                    turn4(M1, xs[:, b, :], "x1T_mm")
                elif part == "q_0":
                    pe.wait_ge(sm["x1T_lo"], b + 1)
                    if p >= 1:
                        pe.wait_ge(sm["y2_done"], 2 * p - 1)
                    else:
                        pe.wait_ge(sm["kb_done"], 2)
                    project_turned(wq2, M0, (0, 1), "q_mm")
                else:
                    pe.wait_ge(sm["qb_done"], 2 * p + 1)
                    project_turned(wq2, M0, (2, 3), "q_mm")

            pe.wait_ge(sm["y1_done"], NT)
            for i, part in enumerate(FIRST_PAIR):
                prepare(0, part)
                turn_units(REST[R1 + i:R1 + i + 1], REST[0])
            for bank in range(6):
                pe.wait_ge(*evac_of(last_in(bank, NUNITS)))
            for u in range(NT + 2):
                t, w = u - 1, u - 2
                attn, rest, last = u < NT, 0 <= t < NT, w >= 0
                p = u // 2 + 1
                even, odd = (attn and p < NT // 2 and u % 2 == j for j in range(2))

                def earlier(g):
                    n = 8 * u + g
                    if 1 <= n <= 8 * NT:
                        prob_turn(*divmod(n - 1, 8))
                    if 2 <= n <= 8 * NT + 1:
                        weighted_v(*divmod(n - 2, 8))

                for g in range(8):
                    if attn:
                        scores(u, g)
                    if g == 0 and last:
                        if u % 2 == 0 and u <= NT:
                            pe.wait_ge(sm["qb_done"], 2 * (u // 2) + 2) if u < NT else None
                        lora_turn(w)
                    if g == 1 and even:
                        prepare(p, "ctx_b")
                    if g == 1 and odd:
                        prepare(p, "k_1")
                    if g == 2 and rest:
                        if even:
                            pe.wait_ge(sm["cT_lo"], 2 * p + 2)
                        if odd:
                            pe.wait_ge(sm["kb_done"], 2 * p + 2)
                        if last:
                            pe.wait_ge(sm["hwT_done"], w + 1)
                        attn_turn(t)
                    if g == 3 and rest:
                        attn_out(t)
                    if g == 5 and rest:
                        if odd:
                            pe.wait_ge(sm["x1T_lo"], 2 * p + 2)
                        x2_turn(t)
                    if g == 7 and rest:
                        base_part(t, (0, 1))
                    earlier(g)
                    if g == 0 and even:
                        prepare(p, "ctx_a")
                    if g == 0 and odd:
                        prepare(p, "k_0")
                    if g == 0 and last:
                        lora_out(w)
                    if g == 2 and even:
                        prepare(p, "v_a")
                    if g == 4 and even:
                        prepare(p, "v_b")
                    if g == 2 and odd:
                        prepare(p, "x_a")
                    if g == 3 and odd:
                        prepare(p, "x_b")
                    if g == 4 and odd:
                        prepare(p, "q_0")
                    if g == 5 and odd:
                        prepare(p, "q_1")
                    if g == 6 and rest:
                        if even:
                            pe.wait_ge(sm["vx_done"], 4 * (2 * p + 2))
                        lora_router_in(t)
                    if g == 7 and rest:
                        base_part(t, (2, 3))

        @block.scalar
        def _(act):
            k = [0]

            def step_(ins):
                k[0] += 1
                ins.then_inc(sm["act_step"], 1)
                act.wait_ge(sm["act_step"], k[0])

            cp = lambda o_, i_: nc.scalar.activation(o_, i_, ACT.Copy)

            def x_evac(t):
                act.wait_ge(sm["xT_mm"], t + 1)
                if t >= 2:
                    act.wait_ge(sm["up_mm"], t - 1)
                cp(xT2[t % 2][0], M0.rearrange("p (c t) -> p c t", c=KC)).then_inc(sm["xT_done"], 1)

            def silu(t):
                act.wait_ge(sm["gate_mm"], t + 1)
                if t >= 2:
                    act.wait_ge(sm["hT_mm"], 3 * (t - 1))
                nc.scalar.activation(prod[t % 2], gate_ps[:, 0:I], ACT.Silu).then_inc(sm["silu_done"], 1)
                act.wait_ge(sm["silu_done"], t + 1)
                if t >= 2:
                    act.wait_ge(sm["masked"], t - 1)
                nc.scalar.activation(mag[t % 2], prod[t % 2], ACT.Abs,
                                     accum_out=msum[:, t % 2:t % 2 + 1]).then_inc(sm["mag_done"], 1)

            def h_evac(t):
                for g in range(3):
                    act.wait_ge(sm["hT_mm"], 3 * t + g + 1)
                    if g == 0:
                        if t >= 1:
                            act.wait_ge(sm["down_mm"], t)
                        else:
                            act.wait_ge(sm["bias_mm"], 1)
                            act.wait_ge(sm["blk_done"], 1)
                    bank = M1 if g % 2 == 0 else M0
                    n = min(4, IC - 4 * g)
                    if 4 * g + n == IC and IREM < P:
                        cp(hT[:, 4 * g:4 * g + n - 1, :].rearrange("p a b -> p (a b)"), bank[:, 0:(n - 1) * P])
                        cp(hT[0:IREM, IC - 1, :], bank[0:IREM, (n - 1) * P:n * P]).then_inc(sm["hT_done"], 1)
                    else:
                        cp(hT[:, 4 * g:4 * g + n, :].rearrange("p a b -> p (a b)"), bank[:, 0:n * P]).then_inc(sm["hT_done"], 1)

            x_evac(0)
            units_hi(act, GATE_UP)
            silu(0)
            x_evac(1)
            units_hi(act, DOWN)
            for t in range(NT):
                if t + 1 < NT:
                    silu(t + 1)
                if t + 2 < NT:
                    x_evac(t + 2)
                if t == NT - 1:
                    act.wait_ge(sm["up_mm"], NT)
                    units_hi(act, REST[0:R0])
                h_evac(t)
            units_hi(act, REST[R0:R1])

            def exps(u, g):
                n = 8 * u + g
                act.wait_ge(sm["sub_done"], n + 1)
                if n >= 2:
                    act.wait_ge(sm["ptr_mm"], n - 1)
                nc.scalar.activation(pr[g % 2], sub[g % 2], ACT.Exp).then_inc(sm["exp_done"], 1)

            def pT_evac(u, g):
                n = 8 * u + g
                act.wait_ge(sm["ptr_mm"], n + 1)
                if n >= 2:
                    act.wait_ge(sm["av_mm"], n - 1)
                cp(pT[g % 2], ptr_ps[g % 2]).then_inc(sm["pT_done"], 1)

            def pair_cols(k):
                return slice((k % 2) * P, (k % 2 + 1) * P)

            def ctx_hi(k, bank):
                act.wait_ge(sm["cT_mm"], k + 1)
                if k >= 2:
                    act.wait_ge(sm["q_mm"], 2 * (k // 2))
                cp(pairT2[0][:, :, pair_cols(k)], bank.rearrange("p (c t) -> p c t", c=KC)).then_inc(sm["cT_done"], 1)

            def x1_hi(k):
                act.wait_ge(sm["x1T_mm"], k + 1)
                act.wait_ge(sm["k_mm"], 2 * (k // 2) + 2)
                cp(pairT2[0][:, :, pair_cols(k)], M1.rearrange("p (c t) -> p c t", c=KC)).then_inc(sm["x1T_done"], 1)

            def queries_out(u, b):
                hf = 2 * u + b
                act.wait_ge(sm["qb_done"], 2 * (u // 2) + 2)
                if hf >= 2:
                    act.wait_ge(sm["score_mm"], 4 * (hf - 1))
                if hf == 0:
                    act.wait_ge(sm["down_mm"], NT)
                for m in range(M):
                    nc.scalar.activation(qx[:, :, b, m, :], qb[:, :, (u % 2) * P + b * S:(u % 2) * P + b * S + S],
                                         ACT.Copy, scale=mcol[:, m:m + 1]).then_inc(sm["qx_done"], 1)

            for i, one in enumerate((lambda: ctx_hi(0, M1), lambda: ctx_hi(1, M0), None, None, None, None,
                                     lambda: x1_hi(0), lambda: x1_hi(1), None, None)):
                if one:
                    one()
                units_hi(act, REST[R1 + i:R1 + i + 1])
            queries_out(0, 0)
            for u in range(NT + 2):
                t, w = u - 1, u - 2
                attn, rest, last = u < NT, 0 <= t < NT, w >= 0
                p = u // 2 + 1
                even, odd = (attn and p < NT // 2 and u % 2 == j for j in range(2))
                for g in range(8):
                    if g == 0 and last:
                        act.wait_ge(sm["hwT_mm"], w + 1)
                        if w >= 1:
                            act.wait_ge(sm["lora_mm"], w)
                        cp(hwT, M0[:, 0:ER]).then_inc(sm["hwT_done"], 1)
                    n = 8 * u + g
                    if g == 1 and even:
                        ctx_hi(2 * p, M1)
                    if g == 3 and odd:
                        x1_hi(2 * p)
                    if g == 4 and odd:
                        x1_hi(2 * p + 1)
                    if g == 7 and rest:
                        act.wait_ge(sm["rmax_done"], t + 1)
                        nc.scalar.activation(re[:], M1[:, ER:ER + E], ACT.Exp, bias=rsum[:, 0:1]).then_inc(sm["rexp_done"], 1)
                    if attn:
                        exps(u, g)
                    if 1 <= n <= 8 * NT:
                        pT_evac(*divmod(n - 1, 8))
                    if g == 1 and even:
                        ctx_hi(2 * p + 1, M0)
                    if g == 1 and attn:
                        queries_out(u, 1)
                    if g == 2 and rest:
                        act.wait_ge(sm["aT_mm"], t + 1)
                        if t >= 1:
                            act.wait_ge(sm["base_mm"], t)
                        src = M0.rearrange("p (b a j q) -> p b a j q", b=BT, a=2, j=2)
                        for b in range(BT):
                            cp(aT2[0][:, :, :, b * S:(b + 1) * S], src[:, b]).then_inc(sm["aT_done"], 1)
                    if g == 5 and rest:
                        act.wait_ge(sm["x2T_mm"], t + 1)
                        act.wait_ge(sm["o_mm"], t + 1)
                        cp(x2T2[0], x2T_bank(t).rearrange("p (c t) -> p c t", c=KC)).then_inc(sm["x2T_done"], 1)
                        if t >= 1:
                            act.wait_ge(sm["ar_mm"], t)
                        cp(x2Tf, x2T_bank(t)).then_inc(sm["x2Tf_done"], 1)
                    if g == 6 and u + 1 < NT:
                        queries_out(u + 1, 0)

        @block.vector
        def _(dve):
            V = nc.vector
            k = [0]

            def step_(ins):
                k[0] += 1
                ins.then_inc(sm["dve_step"], 1)
                dve.wait_ge(sm["dve_step"], k[0])

            def interference():
                dve.wait_ge(sm["pool_const"], 6)
                dve.wait_ge(sm["small_loaded"], 16 * 7)
                step_(V.tensor_reduce(mcol[:], ident[:].rearrange("p (a m) -> p m a", m=M), AX.X, ALU.add))
                step_(V.tensor_scalar(mcol[:], mcol[:], float(DK) ** -0.5, None, ALU.mult))
                step_(V.tensor_scalar(alpha[:], alpha[:], 0.1, None, ALU.mult))
                dve.wait_ge(sm["ints_up"], 1)
                for c in range(KC):
                    r = ps[:, 7, c * M:(c + 1) * M].rearrange("p (a j) -> p a j", a=1).to_broadcast([P, P // M, M])
                    step_(V.scalar_tensor_tensor(blk_tmp[:, c, :].rearrange("p (a j) -> p a j", j=M), r, alpha[:, 0:1],
                                                 same_hd.rearrange("p (a j) -> p a j", j=M), ALU.mult, ALU.mult))
                    step_(V.tensor_tensor(blk[:, c, :], blk_tmp[:, c, :], ident[:], ALU.add))
                    ins = V.tensor_scalar(bcol_bc[:, c, :], ones, bcol[:, 2, c:c + 1], None, ALU.mult)
                ins.then_inc(sm["blk_done"], 1)

            def biases():
                dve.wait_ge(sm["bias_mm"], 1)
                V.tensor_copy(bk_f[:], ps[:, 6, 0:KC])
                V.tensor_copy(bq_f[:], ps[:, 6, KC:2 * KC]).then_inc(sm["bias_done"], 1)
                V.tensor_copy(bv_f[:], ps[:, 7, :]).then_inc(sm["bias_done"], 1)

            def bisect(t):
                a = mag[t % 2]
                cur, val, cnt_, m_, r_ = lo[:, 0:1], lo[:, 1:2], lo[:, 2:3], lo[:, 3:4], step[:, 3:4]
                curi, mi = cur.bitcast(I32), m_.bitcast(I32)
                V.memset(curi, 1 << 30)
                V.drain()
                with dve.Fori(0, 31) as b:
                    V.tensor_scalar(junk[:, 0:I], a, cur, None, ALU.is_lt, ALU.add, accum_out=cnt_)
                    V.drain()
                    V.tensor_scalar(val, cnt_, float(KEEP_OUT) - 0.5, None, ALU.is_gt)
                    V.drain()
                    V.tensor_tensor(mi, val, bits[:, bass.ds(b, 1)], ALU.mult)
                    V.drain()
                    V.tensor_tensor(curi, curi, mi, ALU.bitwise_xor)
                    V.drain()
                    V.tensor_tensor(curi, curi, bits[:, bass.ds(b + 1, 1)], ALU.bitwise_xor)
                    V.drain()
                V.tensor_scalar(junk[:, 0:I], a, cur, None, ALU.is_lt, ALU.add, accum_out=cnt_)
                V.drain()
                V.tensor_scalar(r_, cnt_, -1.0, float(KEEP_OUT), ALU.mult, ALU.add)
                V.tensor_scalar(junk[:, 0:I], a, cur, None, ALU.is_equal)
                V.drain()
                V.tensor_tensor_scan(cand, junk[:, 0:I], junk[:, 0:I], 0.0, ALU.add, ALU.bypass)
                V.drain()
                V.scalar_tensor_tensor(cand, cand, r_, junk[:, 0:I], ALU.is_gt, ALU.mult)
                V.drain()
                V.scalar_tensor_tensor(a, a, cur, cand, ALU.is_gt, ALU.add)
                V.memset(thr[:, 0:1], 0.5)
                V.drain()

            def search(t):
                a = mag[t % 2]
                s = msum[:, t % 2:t % 2 + 1]
                dve.wait_ge(sm["mag_done"], t + 1)
                for i, d in enumerate(STEPS):
                    V.tensor_scalar(step[:, i:i + 1], s, -d * SLOPE / I / KEEP_OUT, None, ALU.mult)
                step_(V.tensor_scalar(tcol[:, 0:1], s, GUESS / I, None, ALU.mult))
                for i in range(COUNTS):
                    ins = V.tensor_scalar(junk[:, 0:I], a, tcol[:, i:i + 1], None, ALU.is_lt, ALU.add,
                                          accum_out=ccol[:, i:i + 1])
                    if i == 1 and t + 1 < NT:
                        x_lo(t + 1)
                    if i == 2:
                        product(t)
                    if i < COUNTS - 1:
                        ins = V.scalar_tensor_tensor(tpre[:], step[:, i:i + 1], -float(AIM), tcol[:, i:i + 1],
                                                     ALU.mult, ALU.add)
                    step_(ins)
                    if i < COUNTS - 1:
                        step_(V.scalar_tensor_tensor(tcol[:, i + 1:i + 2], ccol[:, i:i + 1], step[:, i:i + 1], tpre[:],
                                                     ALU.mult, ALU.add))
                step_(V.tensor_scalar(okc[:], ccol[:], float(KEEP_OUT) + 0.5, None, ALU.is_lt))
                V.tensor_tensor(okt[:], okc[:], tcol[:], ALU.mult)
                step_(V.tensor_tensor(okc[:], okc[:], ccol[:], ALU.mult))
                V.tensor_reduce(lo[:, 0:1], okt[:], AX.X, ALU.max)
                step_(V.tensor_reduce(lo[:, 1:2], okc[:], AX.X, ALU.max))
                V.tensor_scalar(lo[:, 2:3], lo[:, 1:2], -1.0, float(KEEP_OUT), ALU.mult, ALU.add)
                step_(V.tensor_scalar(cand, a, lo[:, 0:1], -BIG, ALU.is_lt, ALU.mult))
                step_(V.tensor_tensor(cand, cand, a, ALU.subtract))
                step_(V.max(top[:, 0:8], cand))
                step_(V.match_replace(cand, top[:, 0:8], cand, -2 * BIG))
                step_(V.max(top[:, 8:16], cand))
                j = lo[:, 2:3]
                V.tensor_scalar(flag[:, 0:1], j, float(CANDIDATES) - 0.5, None, ALU.is_gt)
                step_(V.scalar_tensor_tensor(pick[:, 0:16], iota16[:, 0:16], j, top[:, 0:16], ALU.is_equal, ALU.mult))
                step_(V.scalar_tensor_tensor(pick2[:, 0:16], iota16[:, 1:17], j, top[:, 0:16], ALU.is_equal, ALU.mult))
                V.tensor_reduce(thr[:, 1:2], pick[:, 0:16], AX.X, ALU.min)
                step_(V.tensor_reduce(flag[:, 1:2], pick2[:, 0:16], AX.X, ALU.min))
                V.tensor_scalar(thr[:, 0:1], thr[:, 1:2], -1.0, None, ALU.mult)
                step_(V.tensor_tensor(flag[:, 1:2], flag[:, 1:2], thr[:, 1:2], ALU.is_equal))
                V.tensor_tensor(flag[:, 2:3], flag[:, 0:1], flag[:, 1:2], ALU.max).then_inc(sm["bad_seen"], 1)

            def product(t):
                dve.wait_ge(sm["up_mm"], t + 1)
                dve.wait_ge(sm["mag_done"], t + 1)
                V.tensor_tensor(prod[t % 2], prod[t % 2], up_ps[:, 0:I], ALU.mult).then_inc(sm["prod_done"], 1)

            def x_lo(t):
                dve.wait_ge(sm["xT_done"], t + 1)
                V.tensor_tensor(xT2[t % 2][1], M0.rearrange("p (c t) -> p c t", c=KC), xT2[t % 2][0].bitcast(F32),
                                ALU.subtract).then_inc(sm["xT_lo"], 1)

            def apply_mask(t):
                dve.wait_ge(sm["flag_summed"], t + 1)
                if GENERAL:
                    bad = dve.value_load(flag_all[0:1, 0:1].bitcast(I32), min_val=0, max_val=0x7fffffff)
                    with dve.If(bad >= 0 if FORCE else bad != 0):
                        bisect(t)
                dve.wait_ge(sm["prod_done"], t + 1)
                V.scalar_tensor_tensor(prod[t % 2], mag[t % 2], thr[:, 0:1], prod[t % 2],
                                       ALU.is_ge, ALU.mult).then_inc(sm["masked"], 1)

            def norm_stats(y, done):
                step_(V.bn_stats(stats[:], y))
                V.bn_aggr(mv[:], stats[:]).then_inc(sm[done], 1)

            def norm1(t):
                dve.wait_ge(sm["down_mm"], t + 1)
                y = y1
                if t >= 1:
                    dve.wait_ge(sm["x1_done"], t)
                ins = V.tensor_tensor(y, M0[:, :], xs[:, t, :], ALU.add)
                ins.then_inc(sm["y1_done"], 1)
                dve.wait_ge(sm["y1_done"], t + 1)
                norm_stats(y, "v1_done")
                dve.wait_ge(sm["r1_done"], t + 1)
                dve.wait_ge(sm["v1_done"], t + 1)
                V.tensor_scalar(xs[:, t, :], y, mv[:, 0:1], rstd[:, 0:1], ALU.subtract, ALU.mult).then_inc(sm["x1_done"], 1)

            x_lo(0)
            units_lo(dve, GATE_UP)
            interference()
            search(0)
            apply_mask(0)
            biases()
            for t in range(NT):
                if t + 1 < NT:
                    search(t + 1)
                    apply_mask(t + 1)
                if t == NT - 1:
                    units_lo(dve, REST[0:R1])
                norm1(t)

            def lo_part(dst2, bank, hi_sem, done, n):
                dve.wait_ge(sm[hi_sem], n)
                V.tensor_tensor(dst2[1], bank.rearrange("p (c t) -> p c t", c=KC), dst2[0].bitcast(F32),
                                ALU.subtract).then_inc(sm[done], 1)

            def row_max(u, g):
                n = 8 * u + g
                dve.wait_ge(sm["score_mm"], n + 1)
                if n >= 2:
                    dve.wait_ge(sm["sub_done"], n - 1)
                sc = score_ps[g % 2].rearrange("p (r k) -> p r k", k=S)
                V.tensor_reduce(smax[:, g % 2, :], sc, AX.X, ALU.max).then_inc(sm["max_done"], 1)

            def less_max(u, g):
                n = 8 * u + g
                dve.wait_ge(sm["max_done"], n + 1)
                if n >= 2:
                    dve.wait_ge(sm["exp_done"], n - 1)
                sc = score_ps[g % 2].rearrange("p (r k) -> p r k", k=S)
                mb = smax[:, g % 2, :].rearrange("p (r a) -> p r a", a=1).to_broadcast([P, 8, S])
                V.tensor_tensor(sub[g % 2].rearrange("p (r k) -> p r k", k=S), sc, mb,
                                ALU.subtract).then_inc(sm["sub_done"], 1)

            def inverse_sum(u, g):
                n = 8 * u + g
                dve.wait_ge(sm["av_mm"], n + 1)
                if n >= 1:
                    dve.wait_ge(sm["av_done"], n)
                av = av_ps[:, 0:8 * W33].rearrange("p (r w) -> p r w", w=W33)
                V.reciprocal(rden[:, :], av[:, :, W33 - 1]).then_inc(sm["rden_done"], 1)

            def normalise(u, g):
                b, c = divmod(g, KC)
                n = 8 * u + g
                dve.wait_ge(sm["rden_done"], n + 1)
                if g == 0 and u >= 1:
                    dve.wait_ge(sm["aT_mm"], u)
                for j in range(2):
                    rows = slice(S * j, S * j + S)
                    src = av_ps[rows, j:j + 2 * (4 * W33 + 2)].rearrange("p (m z) -> p m z", m=2)[:, :, 0:4 * W33]
                    src = src.rearrange("p m (r w) -> p m r w", w=W33)[:, :, :, 0:4 * DK - 3:4]
                    dst = attn_n[rows, b, c * 64:(c + 1) * 64].rearrange("p (r d m) -> p m r d", r=4, m=2)
                    rd = rden[rows, :].rearrange("p (m r a) -> p m r a", m=2, a=1).to_broadcast([S, 2, 4, DK])
                    ins = V.tensor_tensor(dst, src, rd, ALU.mult)
                ins.then_inc(sm["av_done"], 1)

            def biased(w_sem, bank, bias, dst, free, done, p, half_):
                dve.wait_ge(sm[w_sem], 2 * p + half_ + 1)
                if p >= 1:
                    dve.wait_ge(sm[free], 16 * p)
                bb = bias[:, 2 * half_:2 * half_ + 2].rearrange("p (c a) -> p c a", a=1).to_broadcast([P, 2, 2 * P])
                V.tensor_tensor(dst[:, 2 * half_:2 * half_ + 2, :], bank.rearrange("p (c t) -> p c t", c=2), bb,
                                ALU.add).then_inc(sm[done], 1)

            def values_out(k):
                dve.wait_ge(sm["v_mm"], k + 1)
                if k < VXN:
                    dve.wait_ge(sm["vx_zero"], 3 * k + 3)
                else:
                    dve.wait_ge(sm["av_mm"], 8 * (k - VXN + 1))
                for b in range(BT):
                    for h2 in range(2):
                        rows = slice(S * b, S * b + S)
                        fv = lambda z: z.rearrange("p (a h f) -> p a h f", h=2, f=M * DK)[:, :, h2, :]
                        V.tensor_tensor(vx[k % VXN][S * h2:S * h2 + S, b, :, h2, 0:M * DK], fv(M1[rows, :]),
                                        fv(bv_f[rows, :]), ALU.add).then_inc(sm["vx_done"], 1)

            def router_steps(t):
                n = [10 * t]
                v = rt[:, 0, 1:2]

                def link(ins):
                    n[0] += 1
                    ins.then_inc(sm["router_step"], 1)

                def seen():
                    dve.wait_ge(sm["router_step"], n[0])

                def s0():
                    dve.wait_ge(sm["rexp_done"], t + 1)
                    link(V.max(rt[:, 0, :], re[:]))

                def s1():
                    seen()
                    link(V.tensor_scalar(rt[:, 1, :], re[:], v, None, ALU.is_gt, ALU.add, accum_out=rsum[:, 1:2]))

                def s2():
                    seen()
                    V.tensor_scalar(rt[:, 2, :], re[:], v, None, ALU.is_equal)
                    link(V.tensor_scalar(rsum[:, 1:2], rsum[:, 1:2], -1.0, 2.0, ALU.mult, ALU.add))

                def s3():
                    seen()
                    link(V.tensor_tensor_scan(rt[:, 3, :], rt[:, 2, :], rt[:, 2, :], 0.0, ALU.add, ALU.bypass))

                def s4():
                    seen()
                    link(V.scalar_tensor_tensor(rt[:, 4, :], rt[:, 3, :], rsum[:, 1:2], rt[:, 2, :], ALU.is_le, ALU.mult))

                def s5():
                    seen()
                    link(V.tensor_tensor(rt[:, 5, :], rt[:, 4, :], rt[:, 1, :], ALU.add))

                def s6():
                    seen()
                    link(V.tensor_tensor(rt[:, 6, :], rt[:, 5, :], re[:], ALU.mult))

                def s7():
                    seen()
                    link(V.tensor_reduce(rsum[:, 2:3], rt[:, 6, :], AX.X, ALU.add))

                def s8():
                    seen()
                    link(V.reciprocal(rsum[:, 3:4], rsum[:, 2:3]))

                def s9():
                    seen()
                    link(V.tensor_scalar(rt[:, 7, :], rt[:, 6, :], rsum[:, 3:4], LORA_SCALING, ALU.mult, ALU.mult))

                def s10():
                    seen()
                    if t >= 1:
                        dve.wait_ge(sm["hwT_mm"], t)
                    wb = rt[:, 7, :].rearrange("p (e a) -> p e a", a=1).to_broadcast([P, E, R])
                    V.tensor_tensor(hw.rearrange("p (e r) -> p e r", e=E), M1[:, 0:ER].rearrange("p (e r) -> p e r", e=E),
                                    wb, ALU.mult).then_inc(sm["hw_done"], 1)

                return [s0, s1, s2, s3, s4, s5, s6, s7, s8, s9, s10]

            def pair_lo(k, bank, hi_sem, done):
                dve.wait_ge(sm[hi_sem], k + 1)
                cols = slice((k % 2) * P, (k % 2 + 1) * P)
                V.tensor_tensor(pairT2[1][:, :, cols], bank.rearrange("p (c t) -> p c t", c=KC),
                                pairT2[0][:, :, cols].bitcast(F32), ALU.subtract).then_inc(sm[done], 1)

            for i, one in enumerate((lambda: pair_lo(0, M1, "cT_done", "cT_lo"),
                                     lambda: pair_lo(1, M0, "cT_done", "cT_lo"),
                                     lambda: biased("k_mm", M1, bk_f, kb, "kx_done", "kb_done", 0, 0),
                                     lambda: biased("k_mm", M0, bk_f, kb, "kx_done", "kb_done", 0, 1),
                                     lambda: values_out(0),
                                     lambda: values_out(1),
                                     lambda: pair_lo(0, M1, "x1T_done", "x1T_lo"),
                                     lambda: pair_lo(1, M1, "x1T_done", "x1T_lo"),
                                     lambda: biased("q_mm", M0, bq_f, qb, "qx_done", "qb_done", 0, 0),
                                     lambda: biased("q_mm", M0, bq_f, qb, "qx_done", "qb_done", 0, 1))):
                one()
                units_lo(dve, REST[R1 + i:R1 + i + 1])
            for u in range(NT + 2):
                t, w = u - 1, u - 2
                attn, rest, last = u < NT, 0 <= t < NT, w >= 0
                p = u // 2 + 1
                even, odd = (attn and p < NT // 2 and u % 2 == j for j in range(2))
                y, yw = yb[:, t % 2, :], yb[:, w % 2, :]
                for g in range(8):
                    n = 8 * u + g
                    if g == 1 and odd:
                        biased("k_mm", M1, bk_f, kb, "kx_done", "kb_done", p, 0)
                    if g == 1 and last:
                        dve.wait_ge(sm["lora_mm"], w + 1)
                        dve.wait_ge(sm["xb2_done"], w + 1)
                        dve.wait_ge(sm["x2_done"], w + 1)
                        V.tensor_tensor(yw, base_ps, xbias[:, 1, :], ALU.add).then_inc(sm["y3_done"], 1)
                    if g == 3 and even:
                        values_out(2 * p)
                    if g == 5 and even:
                        values_out(2 * p + 1)
                    if g == 5 and odd:
                        biased("q_mm", M0, bq_f, qb, "qx_done", "qb_done", p, 0)
                    if g == 6 and odd:
                        biased("q_mm", M0, bq_f, qb, "qx_done", "qb_done", p, 1)
                    if g == 7 and rest:
                        dve.wait_ge(sm["ar_mm"], t + 1)
                        V.tensor_reduce(rsum[:, 0:1], M1[:, ER:ER + E], AX.X, ALU.max, negate=True).then_inc(sm["rmax_done"], 1)
                    if attn:
                        row_max(u, g)
                        less_max(u, g)
                    if g == 1 and even:
                        pair_lo(2 * p, M1, "cT_done", "cT_lo")
                    if g == 1 and last:
                        dve.wait_ge(sm["y3_done"], w + 1)
                        norm_stats(yw, "v3_done")
                    if g == 3 and odd:
                        pair_lo(2 * p, M1, "x1T_done", "x1T_lo")
                    if g == 4 and odd:
                        pair_lo(2 * p + 1, M1, "x1T_done", "x1T_lo")
                    if g == 4 and rest:
                        dve.wait_ge(sm["r2_done"], t + 1)
                        dve.wait_ge(sm["v2_done"], t + 1)
                        if t >= 1:
                            dve.wait_ge(sm["x2T_mm"], t)
                            dve.wait_ge(sm["xb2_done"], t)
                        V.tensor_scalar(x2, y, mv[:, 0:1], rstd[:, 0:1], ALU.subtract, ALU.mult).then_inc(sm["x2_done"], 1)
                    if g == 7 and rest:
                        rs = router_steps(t)
                        for one in rs[:5]:
                            one()
                    if 2 <= n <= 8 * NT + 1:
                        inverse_sum(*divmod(n - 2, 8))
                        normalise(*divmod(n - 2, 8))
                    if g == 1 and odd:
                        biased("k_mm", M0, bk_f, kb, "kx_done", "kb_done", p, 1)
                    if g == 1 and even:
                        pair_lo(2 * p + 1, M0, "cT_done", "cT_lo")
                    if g == 2 and last:
                        dve.wait_ge(sm["r3_done"], w + 1)
                        dve.wait_ge(sm["v3_done"], w + 1)
                        V.tensor_scalar(yw, yw, mv[:, 0:1], rstd[:, 0:1], ALU.subtract, ALU.mult).then_inc(sm["x3_done"], 1)
                    if g == 2 and rest:
                        dve.wait_ge(sm["aT_done"], BT * (t + 1))
                        src = M0.rearrange("p (b a j q) -> p b a j q", b=BT, a=2, j=2)
                        for b in range(BT):
                            qs = slice(b * S, (b + 1) * S)
                            ins = V.tensor_tensor(aT2[1][:, :, :, qs], src[:, b], aT2[0][:, :, :, qs].bitcast(F32), ALU.subtract)
                        ins.then_inc(sm["aT_lo"], 1)
                    if g == 3 and rest:
                        dve.wait_ge(sm["o_mm"], t + 1)
                        dve.wait_ge(sm["xb1_done"], t + 1)
                        if t >= 2:
                            dve.wait_ge(sm[f"out_stored{t % 2}"], 16 * (t // 2))
                        V.tensor_tensor(y, M0[:, :], xbias[:, 0, :], ALU.add).then_inc(sm["y2_done"], 1)
                        dve.wait_ge(sm["y2_done"], t + 1)
                        norm_stats(y, "v2_done")
                    if g == 5 and rest:
                        dve.wait_ge(sm["x2Tf_done"], t + 1)
                        lo_part(x2T2, x2T_bank(t), "x2T_done", "x2T_lo", t + 1)
                    if g == 7 and rest:
                        for one in rs[5:]:
                            one()


GENERAL = True
FORCE = False

_INS = ['x', 'ctx_4096', 'L0_attn_w_gate', 'L0_attn_w_up', 'L0_attn_w_down', 'L0_xattn_Wq', 'L0_xattn_bq',
        'L0_xattn_Wk', 'L0_xattn_bk', 'L0_xattn_Wv', 'L0_xattn_bv', 'L0_xattn_interference', 'L0_xattn_amp',
        'L0_xattn_Wo', 'L0_xattn_bo', 'L0_ffn_W_base', 'L0_ffn_b_base', 'L0_ffn_W_router', 'L0_ffn_lora_A',
        'L0_ffn_lora_B']


def kernel(**inputs):
    import numpy as _np
    import concourse.bacc as _bacc
    from concourse import mybir as _mybir
    from concourse.bass_utils import run_bass_kernel_spmd as _run

    nc = _bacc.Bacc("TRN2", target_bir_lowering=False, num_devices=1)
    arrays, args = {}, []
    for name in _INS:
        a = _np.ascontiguousarray(inputs[name])
        arrays[f"in_{name}"] = a
        args.append(nc.dram_tensor(f"in_{name}", a.shape, _mybir.dt.from_np(a.dtype), kind="ExternalInput").ap())
    shape = inputs['x'].shape
    args.append(nc.dram_tensor("out", tuple(shape), _mybir.dt.float32, kind="ExternalOutput").ap())
    decoder_kernel(nc, *args)
    r = _run(nc, [arrays], core_ids=[0])
    return r.results[0]["out"]
```

```python
from contextlib import ExitStack

import concourse.bass as bass
from concourse import mybir

P = 128
F32 = mybir.dt.float32
F32R = mybir.dt.float32r
BF16 = mybir.dt.bfloat16
I32 = mybir.dt.int32
ALU = mybir.AluOpType
ACT = mybir.ActivationFunctionType
AX = mybir.AxisListType
BIG = 1.0e38
EPS = 1e-5
LORA_SCALING = 2.0

GUESS, SLOPE = 0.78, 0.83
STEPS = (1.0, 1.0, 0.5)
COUNTS = len(STEPS) + 1
CANDIDATES = 16



def decoder_kernel(nc, x, ctx_in, w_gate, w_up, w_down, wq, bq, wk, bk, wv, bv, interference, amp, wo, bo,
                   w_base, b_base, w_router, lora_a, lora_b, out):
    B, S, D = x.shape
    I = w_gate.shape[0]
    NH, M, _ = interference.shape
    DK = D // (NH * M)
    E, R, _ = lora_a.shape
    T = B * S
    NT = T // P
    KC = D // P
    IC = (I + P - 1) // P
    IREM = I - (IC - 1) * P
    KEEP_OUT = I // 2
    AIM = KEEP_OUT - 5
    HC = NH // KC
    BT = P // S
    W33 = M * DK + 1
    ER = E * R
    assert S * 2 == P and M == 4 and DK == 8 and HC == 4 and ER == P and D == 512

    xf = x.rearrange("b s d -> (b s) d")
    cf = ctx_in.rearrange("b s d -> (b s) d")
    of = out.rearrange("b s d -> (b s) d")

    with ExitStack() as stack:
        def sb(name, shape, dt=F32):
            return stack.enter_context(nc.sbuf_tensor(name, shape, dt))

        def sem(name):
            return stack.enter_context(nc.semaphore(name))

        ident = sb("ident", [P, P])
        blk = sb("blk", [P, KC, P])
        int_hi = sb("int_hi", [M * NH, M])
        alpha = sb("alpha", [P, 1])
        mcol = sb("mcol", [P, M])
        half = sb("half", [P, 1])
        iota16 = sb("iota16", [P, CANDIDATES + 1])
        bits = sb("bits", [P, 32], I32)
        bcol = sb("bcol", [P, 3, KC])
        bk_f = sb("bk_f", [P, KC])
        bq_f = sb("bq_f", [P, KC])
        bv_f = sb("bv_f", [P, D])
        bo_f = sb("bo_f", [P, D])
        bb_f = sb("bb_f", [P, D])
        SLOTS = 2
        stage = sb("stage", [P, SLOTS, 4 * D])
        wsplit = sb("wsplit", [P, 4 * KC * I], F32R)
        xsplit = sb("xsplit", [P, 8 * D], F32R)

        def split_pair(buf, at, n):
            return buf[:, at:at + n], buf[:, at + n:at + 2 * n]

        def chunked(pair, c):
            return tuple(v.rearrange("p (c n) -> p c n", c=c) for v in pair)

        wg2 = chunked(split_pair(wsplit, 0, KC * I), KC)
        wu2 = chunked(split_pair(wsplit, 2 * KC * I, KC * I), KC)
        wk2, wq2, wv2, wo2, wb2 = (chunked(split_pair(wsplit, 2 * n * KC * D, KC * D), KC) for n in range(5))
        xT2 = [chunked(split_pair(xsplit, 2 * n * D, D), KC) for n in range(2)]
        pairT2 = chunked(split_pair(xsplit, 0, 2 * D), KC)
        firstT2 = chunked(split_pair(xsplit, 4 * D, 2 * D), KC)
        x2T2 = chunked(split_pair(xsplit, 4 * D, D), KC)
        aT2 = tuple(v.rearrange("p (a j t) -> p a j t", a=2, j=2) for v in split_pair(xsplit, 4 * D, D))
        arT = sb("arT", [P, KC, ER + E])
        wdT = sb("wdT", [P, IC, D])
        lbT = sb("lbT", [P, D])
        xs = sb("xs", [P, NT, D])
        WORK = 5 * I + I // 2 + IC * P + D
        work = sb("work", [P, WORK])
        o = 0

        def carve(n):
            nonlocal o
            v = work[:, o:o + n]
            o += n
            assert o <= WORK
            return v

        mag = [carve(I) for _ in range(2)]
        prod = [carve(I) for _ in range(2)]
        cand = carve(I)
        junk = carve(I // 2).bitcast(BF16)
        o_setup = o
        hT = carve(IC * P).rearrange("p (c t) -> p c t", c=IC)
        y1 = carve(D)
        o = o_setup
        spread = carve(D)[0:M * NH].rearrange("p (c n) -> p c n", c=KC)
        blk_tmp = carve(D).rearrange("p (c n) -> p c n", c=KC)
        bcol_bc = carve(D).rearrange("p (c n) -> p c n", c=KC)
        same_hd = carve(P)
        ones = carve(P)
        o = 0
        cnat = [carve(D) for _ in range(2)]
        kb, qb = (carve(2 * D).rearrange("p (c t) -> p c t", c=KC) for _ in range(2))
        attn_n = carve(BT * D // 2).rearrange("p (b f) -> p b f", b=BT)
        x2 = carve(D)
        pT = [carve(D) for _ in range(2)]
        yb = carve(2 * D).rearrange("p (a n) -> p a n", a=2)
        xbias = carve(2 * D).rearrange("p (a n) -> p a n", a=2)
        wd_flat = wdT[:].rearrange("p a n -> p (a n)")
        kx = wd_flat[:, 0:2048].rearrange("p (c b h k) -> p c b h k", c=KC, b=BT, h=HC)
        qx = wd_flat[:, 2048:4096].rearrange("p (c b m q) -> p c b m q", c=KC, b=BT, m=M)
        VX = BT * NH * W33
        st_flat = stage[:].rearrange("p s n -> p (s n)")
        sub = [st_flat[:, n * D:(n + 1) * D] for n in range(2)]
        pr = [st_flat[:, (2 + n) * D:(3 + n) * D] for n in range(2)]
        x2Tf = st_flat[:, 4 * D:5 * D]
        hw = st_flat[:, 5 * D:5 * D + ER]
        hwT = st_flat[:, 5 * D + ER:5 * D + 2 * ER]
        vx_flat = [wd_flat[:, 4096:4096 + VX], carve(VX), carve(VX), st_flat[:, 5 * D + 2 * ER:5 * D + 2 * ER + VX]]
        VXN = len(vx_flat)
        vx = [v.rearrange("p (b a h w) -> p b a h w", b=BT, a=NH // 2, h=2) for v in vx_flat]
        msum = sb("msum", [P, 2])
        step = sb("step", [P, 4])
        tcol = sb("tcol", [P, COUNTS])
        tpre = sb("tpre", [P, 1])
        ccol = sb("ccol", [P, COUNTS])
        okc = sb("okc", [P, COUNTS])
        okt = sb("okt", [P, COUNTS])
        lo = sb("lo", [P, 4])
        top = sb("top", [P, CANDIDATES + 1])
        pick = sb("pick", [P, CANDIDATES + 1])
        pick2 = sb("pick2", [P, CANDIDATES + 1])
        thr = sb("thr", [P, 2])
        flag = sb("flag", [P, 4])
        flag_all = sb("flag_all", [P, 1])
        stats = sb("stats", [P, 6])
        mv = sb("mv", [P, 2])
        veps = sb("veps", [P, 1])
        rstd = sb("rstd", [P, 1])
        smax = sb("smax", [P, 2, 8])
        rden = sb("rden", [P, 8])
        rt = sb("rt", [P, 8, 8])
        re = sb("re", [P, 8])
        rsum = sb("rsum", [P, 4])

        ps = stack.enter_context(nc.psum_tensor("ps", [P, 8, 512], F32))
        gate_ps = ps[:, 0:3, :].rearrange("p b n -> p (b n)")
        up_ps = ps[:, 3:6, :].rearrange("p b n -> p (b n)")
        M0, M1 = ps[:, 6, :], ps[:, 7, :]
        score_ps = [ps[:, 0, :], ps[:, 1, :]]
        ptr_ps = [ps[:, 2, :], ps[:, 3, :]]
        av_ps, base_ps = ps[:, 4, :], ps[:, 5, :]

        def x2T_bank(t):
            return M1 if t % 2 == 0 else M0

        names = """
            x_first x_rest small_loaded pool_const ints_up blk_done bias_mm bias_done unit_mm unit_act unit_dve
            ctx_loaded0 ctx_loaded1 out_stored0 out_stored1 xT_mm xT_done gate_mm silu_done mag_done up_mm
            prod_done masked bad_seen flag_summed hT_mm hT_done down_mm y1_done v1_done r1_done x1_done x1T_mm
            x1T_done x1T_lo cT_mm cT_done cT_lo aT_mm aT_done aT_lo x2T_lo xT_lo o_mm y2_done v2_done r2_done
            x2_done xb1_done xb2_done k_mm kb_done kx_done q_mm qb_done qx_done v_mm vx_done x2T_mm x2T_done
            x2Tf_done ar_mm base_mm rmax_done rexp_done hw_done max_done rden_done router_step hwT_mm hwT_done
            lora_mm y3_done v3_done r3_done x3_done score_mm sub_done exp_done ptr_mm pT_done av_mm av_done
            dve_step pool_step vx_zero
        """.split()
        sm = {n: sem(n) for n in names}
        EXTRA = 3
        stage_sem = [sem(f"stage{i}") for i in range(SLOTS + EXTRA)]

        panels = []

        def panel(loads, units):
            panels.append((loads, units))

        slot_no = [n if n < SLOTS + EXTRA else (n - SLOTS - EXTRA) % SLOTS for n in range(15)]

        def slot_of():
            n = slot_no[len(panels)]
            return stage[:, n, :] if n < SLOTS else work[:, (n - SLOTS) * 4 * D:(n - SLOTS + 1) * 4 * D]

        def rows_panel(w, dstT, p0):
            st = slot_of().rearrange("p (r d) -> p r d", d=D)
            n = min(4, IC - p0)
            full = n if p0 + n < IC or IREM == P else n - 1
            loads = [(st[:, 0:full, :], w[p0 * P:(p0 + full) * P, :].rearrange("(r p) d -> p r d", p=P))]
            if full < n:
                loads.append((st[0:IREM, full, :], w[(p0 + full) * P:I, :]))
            cols = full * P + (IREM if full < n else 0)
            units = []
            for ic in range(KC):
                mms = []
                for r in range(n):
                    k = P if r < full else IREM
                    mms.append((slice(r * P, r * P + k), st[0:k, r, ic * P:(ic + 1) * P], ident[0:k, 0:k], P))
                units.append((mms, tuple(v[:, ic, p0 * P:p0 * P + cols] for v in dstT), P, cols))
            panel(loads, units)

        def down_panel(p0):
            n = min(4, IC - p0)
            cols = min(I - p0 * P, n * P)
            st = slot_of().rearrange("p (r d) -> p r d", d=D)
            loads = [(st[:, :, 0:cols], w_down[:, p0 * P:p0 * P + cols].rearrange("(r p) i -> p r i", p=P))]
            units = []
            for c in range(n):
                m = min(P, cols - c * P)
                mms = [(slice(oc * P, oc * P + P), st[:, oc, c * P:c * P + m], ident[:, :], m) for oc in range(KC)]
                units.append((mms, (wdT[0:m, p0 + c, :],), m, D))
            panel(loads, units)

        def square_panel(w, dstT, kind):
            st = slot_of().rearrange("p (r d) -> p r d", d=D)
            loads = [(st[:, :, :], w.rearrange("(r p) d -> p r d", p=P))]
            units = []
            for ic in range(KC):
                mms = []
                for oc in range(KC):
                    if kind == "wo":
                        a = (ic // 2) * 2 * P + ic % 2
                        lhs = st[:, oc, a:a + 2 * P - 1:2]
                    else:
                        lhs = st[:, oc, ic * P:(ic + 1) * P]
                    rhs = blk[:, oc, :] if kind == "qkv" else ident[:, :]
                    mms.append((slice(oc * P, oc * P + P), lhs, rhs, P))
                units.append((mms, tuple(v[:, ic, :] for v in dstT), P, D))
            panel(loads, units)

        for p0 in range(0, IC, 4):
            rows_panel(w_gate, wg2, p0)
        for p0 in range(0, IC, 4):
            rows_panel(w_up, wu2, p0)
        for p0 in range(0, IC, 4):
            down_panel(p0)
        square_panel(wk, wk2, "qkv")
        square_panel(wv, wv2, "qkv")
        square_panel(wq, wq2, "qkv")
        square_panel(wo, wo2, "wo")
        square_panel(w_base, wb2, "plain")
        st = slot_of()
        loads = [(st[:, 0:D], lora_a.rearrange("e r d -> (e r) d")),
                 (st[0:E, 2 * D:3 * D], w_router)]
        for oc in range(KC):
            loads.append((st[:, D + oc * P:D + (oc + 1) * P].rearrange("p (e r) -> p e r", e=E),
                          lora_b[:, oc * P:(oc + 1) * P, :].rearrange("e p r -> p e r")))
        panel(loads, [
            ([(slice(ic * P, ic * P + P), st[:, ic * P:(ic + 1) * P], ident[:, :], P) for ic in range(KC)],
             (arT[:, :, 0:ER],), P, D),
            ([(slice(ic * E, ic * E + E), st[0:E, 2 * D + ic * P:2 * D + (ic + 1) * P], ident[0:E, 0:E], P) for ic in range(KC)],
             (arT[:, :, ER:ER + E],), P, KC * E),
            ([(slice(oc * P, oc * P + P), st[:, D + oc * P:D + (oc + 1) * P], ident[:, :], P) for oc in range(KC)],
             (lbT[:, :],), P, D)])

        units_all = []
        unit_end = []
        splits = 0
        for n, (_, units) in enumerate(panels):
            for unit in units:
                u = len(units_all)
                splits += len(unit[1]) == 2
                units_all.append((n, unit, u + 1, splits))
            unit_end.append(len(units_all))
        LAST_UP, WV = 5, 10
        GATE_UP = range(0, unit_end[LAST_UP])
        GATE, UP = range(0, unit_end[2]), range(unit_end[2], unit_end[5])
        DOWN = range(unit_end[5], unit_end[8])
        REST = range(unit_end[8], len(units_all))
        NUNITS = len(units_all)
        R0, R1 = 6, 6 + IC
        FIRST_PAIR = ("q_0", "unit", "ctx_a", "unit", "q_1", "unit", "ctx_b", "unit", "k_0", "unit", "k_1", "unit",
                      "v_a", "v_b")
        assert len(REST) == R1 + FIRST_PAIR.count("unit")

        def bank_of(u):
            if u in GATE:
                return (0, 1, 2, 3, 4, 5, 7)[u % 7]
            if u in UP:
                return (3, 4, 5, 7)[u % 4]
            if u in DOWN:
                return (6, 7, 0, 1, 2)[(u - DOWN[0]) % 5]
            return (u - REST[0]) % 6

        def evac_of(u):
            _, unit, nth, nsplit = units_all[u]
            return (sm["unit_dve"], nsplit) if len(unit[1]) == 2 else (sm["unit_act"], nth)

        def last_in(bank, before):
            return max(u for u in range(before) if bank_of(u) == bank)

        stage_count = []
        cnt = [0] * (SLOTS + EXTRA)
        for n, (loads, _) in enumerate(panels):
            cnt[slot_no[n]] += 16 * len(loads)
            stage_count.append(cnt[slot_no[n]])

        block = stack.enter_context(nc.Block())

        def unit_src(u, dst):
            _, (_, _, rows, cols), _, _ = units_all[u]
            src = ps[0:rows, bank_of(u), 0:cols]
            return src.rearrange("p (a b) -> p a b", a=dst.shape[1]) if len(dst.shape) == 3 else src

        def units_hi(act, which):
            for u in which:
                act.wait_ge(sm["unit_mm"], u + 1)
                dst = units_all[u][1][1][0]
                nc.scalar.activation(dst, unit_src(u, dst), ACT.Copy).then_inc(sm["unit_act"], 1)

        def units_lo(dve, which):
            for u in which:
                dst = units_all[u][1][1]
                if len(dst) == 2:
                    dve.wait_ge(sm["unit_act"], u + 1)
                    nc.vector.tensor_tensor(dst[1], unit_src(u, dst[0]), dst[0].bitcast(F32),
                                            ALU.subtract).then_inc(sm["unit_dve"], 1)

        @block.sync
        def _(sp):
            def load_ctx(k):
                if k >= 2:
                    sp.wait_ge(sm["cT_mm"], k - 1)
                sp.dma_start(cnat[k % 2], cf[k * P:(k + 1) * P, :]).then_inc(sm[f"ctx_loaded{k % 2}"], 16)

            sp.dma_start(xs[:, 0, :], xf[0:P, :]).then_inc(sm["x_first"], 16)
            for n, (loads, _) in enumerate(panels):
                before = [v for v in range(n) if slot_no[v] == slot_no[n]]
                if before:
                    sp.wait_ge(sm["unit_mm"], unit_end[before[-1]])
                if n == WV + 1:
                    sp.wait_ge(sm["masked"], NT - 1)
                    load_ctx(0)
                    load_ctx(1)
                for dst, src in loads:
                    sp.dma_start(dst, src).then_inc(stage_sem[slot_no[n]], 16)
                if n == LAST_UP:
                    sp.dma_start(xs[:, 1:NT, :], xf[P:T, :].rearrange("(t p) d -> p t d", p=P)).then_inc(sm["x_rest"], 16)

            for k in range(2, 4):
                load_ctx(k)
            for u in range(NT + 2):
                if u % 2 == 0:
                    for k in (u + 4, u + 5):
                        if k < NT:
                            load_ctx(k)
                w = u - 2
                if w >= 0:
                    sp.wait_ge(sm["x3_done"], w + 1)
                    sp.dma_start(of[w * P:(w + 1) * P, :], yb[:, w % 2, :]).then_inc(sm[f"out_stored{w % 2}"], 16)
            sp.wait_ge(sm["out_stored0"], 8 * NT)
            sp.wait_ge(sm["out_stored1"], 8 * NT)

        @block.gpsimd
        def _(pool):
            k = [0]

            def step_(ins):
                k[0] += 1
                ins.then_inc(sm["pool_step"], 1)
                pool.wait_ge(sm["pool_step"], k[0])

            step_(nc.gpsimd.memset(ident[:], 0.0))
            nc.gpsimd.affine_select(out=ident[:], in_=ident[:], compare_op=ALU.not_equal, fill=1.0, base=0,
                                    pattern=[[-1, P]], channel_multiplier=1).then_inc(sm["pool_const"], 1)
            pool.dma_start(int_hi[:, :], interference.rearrange("h i j -> (h i) j")).then_inc(sm["small_loaded"], 16)
            pool.dma_start(alpha[:, :], amp.rearrange("(a n) -> a n", a=1).to_broadcast([P, 1])).then_inc(sm["small_loaded"], 16)
            for n, b in enumerate((bk, bq, bv)):
                with nc.allow_non_contiguous_dma(reason="512 words, once"):
                    pool.dma_start(bcol[:, n, :], b.rearrange("(c p) -> p c", p=P)).then_inc(sm["small_loaded"], 16)
            for n, (b, d) in enumerate(((bo, bo_f), (b_base, bb_f))):
                pool.dma_start(d[:, :], b.rearrange("(a n) -> a n", a=1).to_broadcast([P, D])).then_inc(sm["small_loaded"], 16)
            step_(nc.gpsimd.memset(same_hd, 1.0))
            v = same_hd.rearrange("p (a j) -> p a j", j=M)
            step_(nc.gpsimd.affine_select(out=v, in_=v, compare_op=ALU.is_ge, fill=0.0, base=0,
                                          pattern=[[-M, P // M], [0, M]], channel_multiplier=1))
            nc.gpsimd.affine_select(out=v, in_=v, compare_op=ALU.is_ge, fill=0.0, base=M - 1,
                                    pattern=[[M, P // M], [0, M]], channel_multiplier=-1).then_inc(sm["pool_const"], 1)
            step_(nc.gpsimd.memset(spread, 0.0))
            v = spread.rearrange("p c (h d i) -> p (c h) d i", h=HC, d=DK)
            nc.gpsimd.affine_select(out=v, in_=v, compare_op=ALU.not_equal, fill=1.0, base=0,
                                    pattern=[[-M, NH], [0, DK], [-1, M]], channel_multiplier=1).then_inc(sm["pool_const"], 1)
            nc.gpsimd.memset(ones, 1.0).then_inc(sm["pool_const"], 1)
            nc.gpsimd.memset(half[:], -0.5).then_inc(sm["pool_const"], 1)
            nc.gpsimd.iota(iota16[:], pattern=[[1, CANDIDATES + 1]], base=0, channel_multiplier=0,
                           allow_small_or_imprecise_dtypes=True).then_inc(sm["pool_const"], 1)
            for b in range(31):
                nc.gpsimd.memset(bits[:, b:b + 1], 1 << (30 - b))
            ins = nc.gpsimd.memset(bits[:, 31:32], 0)
            ins.then_inc(sm["pool_const"], 1)

            def rstd_(stage_v, stage_r, t):
                pool.wait_ge(sm[stage_v], t + 1)
                step_(nc.gpsimd.tensor_scalar(veps[:], mv[:, 1:2], EPS, None, ALU.add))
                nc.gpsimd.tensor_tensor(rstd[:], veps[:], half[:], ALU.pow).then_inc(sm[stage_r], 1)

            for t in range(NT):
                pool.wait_ge(sm["bad_seen"], t + 1)
                nc.gpsimd.partition_all_reduce(flag_all[:], flag[:, 2:3], P,
                                               bass.bass_isa.ReduceOp.max).then_inc(sm["flag_summed"], 1)
                if t >= 1:
                    rstd_("v1_done", "r1_done", t - 1)
            pool.wait_ge(sm["down_mm"], NT)
            step_(nc.gpsimd.memset(kx, 0.0))
            rstd_("v1_done", "r1_done", NT - 1)
            pool.wait_ge(sm["r1_done"], NT)
            pool.wait_ge(sm["x1_done"], NT)

            def vx_zeros(j):
                nc.gpsimd.memset(vx_flat[j], 0.0).then_inc(sm["vx_zero"], 1)
                for h2 in range(2):
                    pool.wait_ge(sm["vx_zero"], 3 * j + h2 + 1)
                    nc.gpsimd.memset(vx[j][S * h2:S * h2 + S, :, :, h2, W33 - 1:W33], 1.0).then_inc(sm["vx_zero"], 1)
                pool.wait_ge(sm["vx_zero"], 3 * j + 3)

            for j in range(VXN - 1):
                vx_zeros(j)

            def keys_out(u, b):
                hf = 2 * u + b
                pool.wait_ge(sm["kb_done"], 2 * (u // 2) + 2)
                if hf >= 2:
                    pool.wait_ge(sm["score_mm"], 4 * (hf - 1))
                for h in range(HC):
                    q0 = 32 * h
                    nc.gpsimd.tensor_copy(kx[q0:q0 + 32, :, b, h, :],
                                          kb[q0:q0 + 32, :, (u % 2) * P + b * S:(u % 2) * P + b * S + S]
                                          ).then_inc(sm["kx_done"], 1)
                    pool.wait_ge(sm["kx_done"], HC * hf + h + 1)

            pool.wait_ge(sm["unit_mm"], NUNITS)
            vx_zeros(VXN - 1)
            keys_out(0, 0)
            for u in range(NT + 2):
                t, w = u - 1, u - 2
                if u < NT:
                    keys_out(u, 1)
                if 0 <= t < NT:
                    if t >= 1:
                        pool.wait_ge(sm["y2_done"], t)
                    nc.gpsimd.tensor_tensor(xbias[:, 0, :], xs[:, t, :], bo_f[:], ALU.add).then_inc(sm["xb1_done"], 1)
                if w >= 0:
                    rstd_("v3_done", "r3_done", w)
                if 0 <= t < NT:
                    rstd_("v2_done", "r2_done", t)
                    pool.wait_ge(sm["x2_done"], t + 1)
                    if t >= 1:
                        pool.wait_ge(sm["y3_done"], t)
                    nc.gpsimd.tensor_tensor(xbias[:, 1, :], x2, bb_f[:], ALU.add).then_inc(sm["xb2_done"], 1)
                    pool.wait_ge(sm["xb2_done"], t + 1)
                if u + 1 < NT:
                    keys_out(u + 1, 0)

        @block.tensor
        def _(pe):
            mm = nc.tensor.matmul
            pe.wait_ge(sm["pool_const"], 1)

            def interference_blocks():
                pe.wait_ge(sm["pool_const"], 6)
                pe.wait_ge(sm["small_loaded"], 16 * 7)
                pe.wait_ge(*evac_of(last_in(7, len(GATE_UP))))
                for c in range(KC):
                    ins = mm(ps[:, 7, c * M:(c + 1) * M], spread[:, c, :], int_hi[:, :], start=True, stop=True)
                ins.then_inc(sm["ints_up"], 1)

            def folded_biases():
                for bank in (6, 7, 0, 1, 2):
                    pe.wait_ge(*evac_of(last_in(bank, NUNITS - len(REST))))
                for c in range(KC):
                    mm(ps[:, 6, 2 * c:2 * c + 2], blk[:, c, :], bcol[:, 0:2, c], start=True, stop=True)
                for c in range(KC):
                    ins = mm(ps[:, 7, c * P:(c + 1) * P], bcol_bc[:, c, :], blk[:, c, :], start=True, stop=True)
                ins.then_inc(sm["bias_mm"], 1)

            def mm3(dst, a, b, first=True, last=True):
                mm(dst, a[1], b[0], start=first, stop=False)
                mm(dst, a[0], b[1], start=False, stop=False)
                return mm(dst, a[0], b[0], start=False, stop=last)

            def turn_units(which, first=None):
                for u in which:
                    n, (mms, _, rows, cols), _, _ = units_all[u]
                    if u == (unit_end[n - 1] if n else 0):
                        pe.wait_ge(stage_sem[slot_no[n]], stage_count[n])
                    bank = bank_of(u)
                    if any(bank_of(v) == bank for v in range(which[0] if first is None else first, u)):
                        pe.wait_ge(*evac_of(last_in(bank, u)))
                    for cs, lhs, rhs, m in mms:
                        ins = mm(ps[0:m, bank, cs], lhs, rhs, start=True, stop=True,
                                 is_transpose=None if rhs.tensor is blk[:].tensor else True)
                    ins.then_inc(sm["unit_mm"], 1)

            def x_turn(t):
                pe.wait_ge(sm["x_first" if t == 0 else "x_rest"], 16)
                if t == 1:
                    pe.wait_ge(sm["xT_lo"], 1)
                if t == 2:
                    pe.wait_ge(sm["bias_done"], 2)
                if t >= 3:
                    pe.wait_ge(sm["y1_done"], t - 2)
                for c in range(KC):
                    ins = nc.tensor.transpose(M0[:, c * P:(c + 1) * P], xs[:, t, c * P:(c + 1) * P], ident[:])
                ins.then_inc(sm["xT_mm"], 1)

            def gate_up(t, beside=None):
                pe.wait_ge(sm["xT_lo"], t + 1)
                for w, acc, done, free in ((wg2, gate_ps, "gate_mm", "silu_done"), (wu2, up_ps, "up_mm", "prod_done")):
                    if t >= 1:
                        pe.wait_ge(sm[free], t)
                    for n0 in range(0, I, 512):
                        n1 = min(I, n0 + 512)
                        for c in range(KC):
                            ins = mm3(acc[:, n0:n1], [v[:, c, :] for v in xT2[t % 2]], [v[:, c, n0:n1] for v in w],
                                      c == 0, c == KC - 1)
                        if beside and done == "gate_mm":
                            if n1 == I:
                                ins.then_inc(sm[done], 1)
                            beside(n0 // 512)
                    if not (beside and done == "gate_mm"):
                        ins.then_inc(sm[done], 1)
                    if done == "gate_mm" and t + 1 < NT:
                        x_turn(t + 1)

            def h_turn_down(t, beside=None):
                if t >= 1:
                    pe.wait_ge(sm["hT_done"], 3 * t)
                pe.wait_ge(sm["masked"], t + 1)
                for g in range(3):
                    bank = M1 if g % 2 == 0 else M0
                    if g == 1:
                        pe.wait_ge(sm["xT_lo"], min(t + 3, NT))
                        if t >= NT - 2:
                            pe.wait_ge(sm["y1_done"], t)
                    if g == 2:
                        pe.wait_ge(sm["hT_done"], 3 * t + 1)
                    n = min(4, IC - 4 * g)
                    for r in range(n):
                        i0 = (4 * g + r) * P
                        m = min(P, I - i0)
                        ins = nc.tensor.transpose(bank[0:m, r * P:(r + 1) * P], prod[t % 2][:, i0:i0 + m], ident[:])
                    ins.then_inc(sm["hT_mm"], 1)
                pe.wait_ge(sm["hT_done"], 3 * t + 2)
                for c in range(IC):
                    m = min(P, I - c * P)
                    if c == 8:
                        pe.wait_ge(sm["hT_done"], 3 * t + 3)
                    ins = mm(M0[:, :], hT[0:m, c, :], wdT[0:m, c, :], start=(c == 0), stop=(c == IC - 1))
                    if beside:
                        beside(c)
                ins.then_inc(sm["down_mm"], 1)

            x_turn(0)
            turn_units(GATE)
            for bank in range(3):
                pe.wait_ge(*evac_of(last_in(bank, len(GATE))))
            pe.wait_ge(*evac_of(GATE[-1]))

            def beside_gate(n):
                turn_units(UP[4 * n:4 * n + 4], 0)
                if n == 2:
                    interference_blocks()
                    for bank in range(3, 6):
                        pe.wait_ge(*evac_of(last_in(bank, len(GATE_UP))))
                    pe.wait_ge(*evac_of(UP[-1]))

            gate_up(0, beside_gate)
            pe.wait_ge(sm["xT_lo"], 2)
            pe.wait_ge(sm["blk_done"], 1)
            pe.wait_ge(sm["silu_done"], 1)
            turn_units(DOWN)
            folded_biases()
            for t in range(NT):
                if t + 1 < NT:
                    gate_up(t + 1)
                if t == NT - 1:
                    pe.wait_ge(sm["silu_done"], NT)
                    pe.wait_ge(sm["prod_done"], NT)
                    turn_units(REST[0:R0])
                if t < NT - 1:
                    h_turn_down(t)

            def turn4(bank, src, done):
                for c in range(KC):
                    ins = nc.tensor.transpose(bank[:, c * P:(c + 1) * P], src[:, c * P:(c + 1) * P], ident[:])
                ins.then_inc(sm[done], 1)

            def ctx_turn(k, bank):
                pe.wait_ge(sm[f"ctx_loaded{k % 2}"], 16 * (k // 2 + 1))
                turn4(bank, cnat[k % 2], "cT_mm")

            def project_turned(w2, bank, fs, done, src2=pairT2):
                for f in fs:
                    for c in range(KC):
                        ins = mm3(bank[:, (f % 2) * 2 * P:(f % 2 + 1) * 2 * P], [v[:, c, f * P:(f + 1) * P] for v in w2],
                                  [v[:, c, :] for v in src2], c == 0, c == KC - 1)
                ins.then_inc(sm[done], 1)

            def attn_turn(t):
                pe.wait_ge(sm["av_done"], 8 * (t + 1))
                for b in range(BT):
                    for a in range(2):
                        ins = nc.tensor.transpose(M0[:, (2 * b + a) * P:(2 * b + a + 1) * P],
                                                  attn_n[:, b, a * P:(a + 1) * P], ident[:])
                ins.then_inc(sm["aT_mm"], 1)

            def values(k, bank=M1):
                pe.wait_ge(sm["cT_lo"], k + 1)
                cols = slice((k % 2) * P, (k % 2 + 1) * P)
                for c in range(KC):
                    ins = mm3(bank[:, :], [v[:, c, cols] for v in pairT2], [v[:, c, :] for v in wv2], c == 0, c == KC - 1)
                ins.then_inc(sm["v_mm"], 1)

            def attn_out(t):
                pe.wait_ge(sm["aT_lo"], t + 1)
                for a in range(2):
                    for j in range(2):
                        ins = mm3(M0[:, :], [v[:, a, j, :] for v in aT2], [v[:, 2 * a + j, :] for v in wo2],
                                  a + j == 0, a + j == 2)
                ins.then_inc(sm["o_mm"], 1)

            def x2_turn(t):
                pe.wait_ge(sm["x2_done"], t + 1)
                turn4(x2T_bank(t), x2, "x2T_mm")

            def lora_router_in(t):
                pe.wait_ge(sm["x2T_lo"], t + 1)
                for c in range(KC):
                    ins = mm(M1[:, 0:ER + E], x2Tf[:, c * P:(c + 1) * P], arT[:, c, :], start=(c == 0), stop=(c == KC - 1))
                ins.then_inc(sm["ar_mm"], 1)

            def base_part(t, cs):
                if t >= 1:
                    pe.wait_ge(sm["y3_done"], t)
                for c in cs:
                    ins = mm3(base_ps, [v[:, c, :] for v in x2T2], [v[:, c, :] for v in wb2], c == 0, False)
                if cs[-1] == KC - 1:
                    ins.then_inc(sm["base_mm"], 1)

            def lora_turn(t):
                pe.wait_ge(sm["hw_done"], t + 1)
                nc.tensor.transpose(M0[:, 0:ER], hw, ident[:]).then_inc(sm["hwT_mm"], 1)

            def lora_out(t):
                pe.wait_ge(sm["hwT_done"], t + 1)
                mm(base_ps, hwT, lbT[:, :], start=False, stop=True).then_inc(sm["lora_mm"], 1)

            def scores(u, g):
                b, c = divmod(g, KC)
                n = 8 * u + g
                if c == 0:
                    pe.wait_ge(sm["kx_done"], HC * (n // 4 + 1))
                    pe.wait_ge(sm["qx_done"], M * (n // 4 + 1))
                if n >= 2:
                    pe.wait_ge(sm["sub_done"], n - 1)
                for mp in range(2):
                    ins = mm(score_ps[g % 2][:, mp * 256:(mp + 1) * 256],
                             qx[:, c, b, 2 * mp:2 * mp + 2, :], kx[:, c, b, :, :], start=True, stop=True)
                ins.then_inc(sm["score_mm"], 1)

            def prob_turn(u, g):
                n = 8 * u + g
                pe.wait_ge(sm["exp_done"], n + 1)
                if n >= 2:
                    pe.wait_ge(sm["pT_done"], n - 1)
                for k4 in range(4):
                    ins = nc.tensor.transpose(ptr_ps[g % 2][:, k4 * P:(k4 + 1) * P],
                                              pr[g % 2][:, k4 * P:(k4 + 1) * P], ident[:])
                ins.then_inc(sm["ptr_mm"], 1)

            def weighted_v(u, g):
                b, c = divmod(g, KC)
                n = 8 * u + g
                pe.wait_ge(sm["pT_done"], n + 1)
                if n >= 1:
                    pe.wait_ge(sm["av_done"], n)
                for mp in range(2):
                    for hp in range(2):
                        o0 = (mp * 2 + hp) * 2 * W33
                        k4 = 2 * mp + hp
                        ins = mm(av_ps[:, o0:o0 + 2 * W33], pT[g % 2][:, k4 * P:(k4 + 1) * P],
                                 vx[u % VXN][:, b, 2 * c + hp, :, :], start=True, stop=True)
                ins.then_inc(sm["av_mm"], 1)

            def prepare(p, part):
                a, b = 2 * p, 2 * p + 1
                if part == "ctx_a":
                    if p == 1:
                        pe.wait_ge(sm["vx_done"], 4)
                    ctx_turn(a, M1)
                elif part == "ctx_b":
                    if p == 1:
                        pe.wait_ge(sm["vx_done"], 8)
                    else:
                        pe.wait_ge(sm["hwT_done"], a - 3)
                    ctx_turn(b, M0)
                elif part == "v_a":
                    values(a)
                elif part == "v_b":
                    pe.wait_ge(sm["vx_done"], 4 * (a + 1))
                    values(b)
                elif part == "k_0":
                    pe.wait_ge(sm["vx_done"], 4 * (b + 1))
                    project_turned(wk2, M1, (0, 1), "k_mm")
                elif part == "k_1":
                    if p >= 2:
                        pe.wait_ge(sm["hwT_done"], b - 3)
                    project_turned(wk2, M0, (2, 3), "k_mm")
                elif part == "x_a":
                    pe.wait_ge(sm["kb_done"], 2 * p + 1)
                    turn4(M1, xs[:, a, :], "x1T_mm")
                elif part == "x_b":
                    pe.wait_ge(sm["x1T_lo"], a + 1)
                    turn4(M1, xs[:, b, :], "x1T_mm")
                elif part == "q_0":
                    pe.wait_ge(sm["x1T_lo"], b + 1)
                    pe.wait_ge(sm["y2_done"], 2 * p - 1)
                    project_turned(wq2, M0, (0, 1), "q_mm")
                else:
                    pe.wait_ge(sm["qb_done"], 2 * p + 1)
                    project_turned(wq2, M0, (2, 3), "q_mm")

            def beside_down(c):
                turn_units(REST[R0 + c:R0 + c + 1], REST[0])
                if c == 8:
                    turn4(M1, xs[:, 0, :], "x1T_mm")
                if c == 10:
                    pe.wait_ge(sm["x1T_lo"], 1)
                    turn4(M1, xs[:, 1, :], "x1T_mm")

            h_turn_down(NT - 1, beside_down)
            r = R1
            for part in FIRST_PAIR:
                if part == "unit":
                    turn_units(REST[r:r + 1], REST[0])
                    r += 1
                elif part == "q_0":
                    pe.wait_ge(*evac_of(unit_end[WV + 1] - 1))
                    pe.wait_ge(sm["x1T_lo"], 2)
                    project_turned(wq2, M1, (0, 1), "q_mm", firstT2)
                elif part == "ctx_a":
                    pe.wait_ge(sm["y1_done"], NT)
                    ctx_turn(0, M0)
                elif part == "q_1":
                    pe.wait_ge(sm["qb_done"], 1)
                    project_turned(wq2, M1, (2, 3), "q_mm", firstT2)
                elif part == "ctx_b":
                    pe.wait_ge(sm["cT_lo"], 1)
                    ctx_turn(1, M0)
                elif part == "k_0":
                    pe.wait_ge(sm["qb_done"], 2)
                    pe.wait_ge(sm["cT_lo"], 2)
                    project_turned(wk2, M1, (0, 1), "k_mm")
                elif part == "k_1":
                    project_turned(wk2, M0, (2, 3), "k_mm")
                elif part == "v_a":
                    pe.wait_ge(sm["kb_done"], 1)
                    values(0, M1)
                elif part == "v_b":
                    pe.wait_ge(sm["kb_done"], 2)
                    values(1, M0)
            for bank in range(6):
                pe.wait_ge(*evac_of(last_in(bank, NUNITS)))
            for u in range(NT + 2):
                t, w = u - 1, u - 2
                attn, rest, last = u < NT, 0 <= t < NT, w >= 0
                p = u // 2 + 1
                even, odd = (attn and p < NT // 2 and u % 2 == j for j in range(2))

                def earlier(g):
                    n = 8 * u + g
                    if 1 <= n <= 8 * NT:
                        prob_turn(*divmod(n - 1, 8))
                    if 2 <= n <= 8 * NT + 1:
                        weighted_v(*divmod(n - 2, 8))

                for g in range(8):
                    if attn:
                        scores(u, g)
                    if g == 0 and last:
                        lora_turn(w)
                    if g == 1 and odd:
                        prepare(p, "k_1")
                    if g == 2 and rest and odd:
                        pe.wait_ge(sm["kb_done"], 2 * p + 2)
                        attn_turn(t)
                    if g == 3 and rest and odd:
                        attn_out(t)
                    if g == 5 and rest:
                        if odd:
                            pe.wait_ge(sm["x1T_lo"], 2 * p + 2)
                        x2_turn(t)
                    if g == 7 and rest:
                        base_part(t, (0, 1))
                    earlier(g)
                    if g == 0 and even:
                        prepare(p, "ctx_a")
                        prepare(p, "ctx_b")
                    if g == 0 and odd:
                        prepare(p, "k_0")
                    if g == 0 and last:
                        lora_out(w)
                    if g == 2 and even:
                        prepare(p, "v_a")
                    if g == 2 and rest and not odd:
                        if even:
                            pe.wait_ge(sm["cT_lo"], 2 * p + 2)
                        elif last:
                            pe.wait_ge(sm["hwT_done"], w + 1)
                        attn_turn(t)
                    if g == 3 and rest and not odd:
                        attn_out(t)
                    if g == 4 and even:
                        prepare(p, "v_b")
                    if g == 1 and odd:
                        prepare(p, "x_a")
                    if g == 2 and odd:
                        prepare(p, "x_b")
                    if g == 4 and odd:
                        prepare(p, "q_0")
                    if g == 5 and odd:
                        prepare(p, "q_1")
                    if g == 6 and rest:
                        if even:
                            pe.wait_ge(sm["vx_done"], 4 * (2 * p + 2))
                        lora_router_in(t)
                    if g == 7 and rest:
                        base_part(t, (2, 3))

        @block.scalar
        def _(act):
            cp = lambda o_, i_: nc.scalar.activation(o_, i_, ACT.Copy)

            def x_evac(t):
                act.wait_ge(sm["xT_mm"], t + 1)
                if t >= 2:
                    act.wait_ge(sm["up_mm"], t - 1)
                cp(xT2[t % 2][0], M0.rearrange("p (c t) -> p c t", c=KC)).then_inc(sm["xT_done"], 1)

            def silu(t):
                act.wait_ge(sm["gate_mm"], t + 1)
                if t >= 2:
                    act.wait_ge(sm["hT_mm"], 3 * (t - 1))
                nc.scalar.activation(prod[t % 2], gate_ps[:, 0:I], ACT.Silu).then_inc(sm["silu_done"], 1)
                act.wait_ge(sm["silu_done"], t + 1)
                if t >= 2:
                    act.wait_ge(sm["masked"], t - 1)
                nc.scalar.activation(mag[t % 2], prod[t % 2], ACT.Abs,
                                     accum_out=msum[:, t % 2:t % 2 + 1]).then_inc(sm["mag_done"], 1)

            def h_evac(t):
                for g in range(3):
                    act.wait_ge(sm["hT_mm"], 3 * t + g + 1)
                    if g == 0:
                        if t >= 1:
                            act.wait_ge(sm["down_mm"], t)
                        else:
                            act.wait_ge(sm["bias_mm"], 1)
                            act.wait_ge(sm["blk_done"], 1)
                    bank = M1 if g % 2 == 0 else M0
                    n = min(4, IC - 4 * g)
                    if 4 * g + n == IC and IREM < P:
                        cp(hT[:, 4 * g:4 * g + n - 1, :].rearrange("p a b -> p (a b)"), bank[:, 0:(n - 1) * P])
                        cp(hT[0:IREM, IC - 1, :], bank[0:IREM, (n - 1) * P:n * P]).then_inc(sm["hT_done"], 1)
                    else:
                        cp(hT[:, 4 * g:4 * g + n, :].rearrange("p a b -> p (a b)"), bank[:, 0:n * P]).then_inc(sm["hT_done"], 1)

            x_evac(0)
            units_hi(act, GATE_UP)
            silu(0)
            x_evac(1)
            units_hi(act, DOWN)
            for t in range(NT):
                if t + 1 < NT:
                    silu(t + 1)
                if t + 2 < NT:
                    x_evac(t + 2)
                if t == NT - 1:
                    act.wait_ge(sm["up_mm"], NT)
                    units_hi(act, REST[0:R0])
                h_evac(t)

            def exps(u, g):
                n = 8 * u + g
                act.wait_ge(sm["sub_done"], n + 1)
                if n >= 2:
                    act.wait_ge(sm["ptr_mm"], n - 1)
                nc.scalar.activation(pr[g % 2], sub[g % 2], ACT.Exp).then_inc(sm["exp_done"], 1)

            def pT_evac(u, g):
                n = 8 * u + g
                act.wait_ge(sm["ptr_mm"], n + 1)
                if n >= 2:
                    act.wait_ge(sm["av_mm"], n - 1)
                cp(pT[g % 2], ptr_ps[g % 2]).then_inc(sm["pT_done"], 1)

            def pair_cols(k):
                return slice((k % 2) * P, (k % 2 + 1) * P)

            def ctx_hi(k, bank):
                act.wait_ge(sm["cT_mm"], k + 1)
                if k >= 2:
                    act.wait_ge(sm["q_mm"], 2 * (k // 2))
                cp(pairT2[0][:, :, pair_cols(k)], bank.rearrange("p (c t) -> p c t", c=KC)).then_inc(sm["cT_done"], 1)

            def x1_hi(k):
                act.wait_ge(sm["x1T_mm"], k + 1)
                if k >= 2:
                    act.wait_ge(sm["k_mm"], 2 * (k // 2) + 2)
                cp((firstT2 if k < 2 else pairT2)[0][:, :, pair_cols(k)], M1.rearrange("p (c t) -> p c t", c=KC)).then_inc(sm["x1T_done"], 1)

            def queries_out(u, b):
                hf = 2 * u + b
                act.wait_ge(sm["qb_done"], 2 * (u // 2) + 2)
                if hf >= 2:
                    act.wait_ge(sm["score_mm"], 4 * (hf - 1))
                if hf == 0:
                    act.wait_ge(sm["down_mm"], NT)
                for m in range(M):
                    nc.scalar.activation(qx[:, :, b, m, :], qb[:, :, (u % 2) * P + b * S:(u % 2) * P + b * S + S],
                                         ACT.Copy, scale=mcol[:, m:m + 1]).then_inc(sm["qx_done"], 1)

            for c in range(IC):
                units_hi(act, REST[R0 + c:R0 + c + 1])
                if c in (8, 10):
                    x1_hi((c - 8) // 2)
            r = R1
            for part in FIRST_PAIR:
                if part == "unit":
                    units_hi(act, REST[r:r + 1])
                    r += 1
                if part == "ctx_a":
                    ctx_hi(0, M0)
                if part == "ctx_b":
                    ctx_hi(1, M0)
            queries_out(0, 0)
            for u in range(NT + 2):
                t, w = u - 1, u - 2
                attn, rest, last = u < NT, 0 <= t < NT, w >= 0
                p = u // 2 + 1
                even, odd = (attn and p < NT // 2 and u % 2 == j for j in range(2))
                for g in range(8):
                    if g == 0 and last:
                        act.wait_ge(sm["hwT_mm"], w + 1)
                        if w >= 1:
                            act.wait_ge(sm["lora_mm"], w)
                        cp(hwT, M0[:, 0:ER]).then_inc(sm["hwT_done"], 1)
                    n = 8 * u + g
                    if g == 1 and even:
                        ctx_hi(2 * p, M1)
                        ctx_hi(2 * p + 1, M0)
                    if g == 2 and odd:
                        x1_hi(2 * p)
                    if g == 3 and odd:
                        x1_hi(2 * p + 1)
                    if g == 5 and rest:
                        act.wait_ge(sm["x2T_mm"], t + 1)
                        act.wait_ge(sm["o_mm"], t + 1)
                        cp(x2T2[0], x2T_bank(t).rearrange("p (c t) -> p c t", c=KC)).then_inc(sm["x2T_done"], 1)
                        if t >= 1:
                            act.wait_ge(sm["ar_mm"], t)
                        cp(x2Tf, x2T_bank(t)).then_inc(sm["x2Tf_done"], 1)
                    if g == 7 and rest:
                        act.wait_ge(sm["rmax_done"], t + 1)
                        nc.scalar.activation(re[:], M1[:, ER:ER + E], ACT.Exp, bias=rsum[:, 0:1]).then_inc(sm["rexp_done"], 1)
                    if attn:
                        exps(u, g)
                    if 1 <= n <= 8 * NT:
                        pT_evac(*divmod(n - 1, 8))
                    if g == 1 and attn:
                        queries_out(u, 1)
                    if g == 2 and rest:
                        act.wait_ge(sm["aT_mm"], t + 1)
                        if t >= 1:
                            act.wait_ge(sm["base_mm"], t)
                        src = M0.rearrange("p (b a j q) -> p b a j q", b=BT, a=2, j=2)
                        for b in range(BT):
                            cp(aT2[0][:, :, :, b * S:(b + 1) * S], src[:, b]).then_inc(sm["aT_done"], 1)
                    if g == 6 and u + 1 < NT:
                        queries_out(u + 1, 0)

        @block.vector
        def _(dve):
            V = nc.vector
            k = [0]

            def step_(ins):
                k[0] += 1
                ins.then_inc(sm["dve_step"], 1)
                dve.wait_ge(sm["dve_step"], k[0])

            def interference():
                dve.wait_ge(sm["pool_const"], 6)
                dve.wait_ge(sm["small_loaded"], 16 * 7)
                step_(V.tensor_reduce(mcol[:], ident[:].rearrange("p (a m) -> p m a", m=M), AX.X, ALU.add))
                step_(V.tensor_scalar(mcol[:], mcol[:], float(DK) ** -0.5, None, ALU.mult))
                step_(V.tensor_scalar(alpha[:], alpha[:], 0.1, None, ALU.mult))
                dve.wait_ge(sm["ints_up"], 1)
                for c in range(KC):
                    r = ps[:, 7, c * M:(c + 1) * M].rearrange("p (a j) -> p a j", a=1).to_broadcast([P, P // M, M])
                    step_(V.scalar_tensor_tensor(blk_tmp[:, c, :].rearrange("p (a j) -> p a j", j=M), r, alpha[:, 0:1],
                                                 same_hd.rearrange("p (a j) -> p a j", j=M), ALU.mult, ALU.mult))
                    step_(V.tensor_tensor(blk[:, c, :], blk_tmp[:, c, :], ident[:], ALU.add))
                    ins = V.tensor_scalar(bcol_bc[:, c, :], ones, bcol[:, 2, c:c + 1], None, ALU.mult)
                ins.then_inc(sm["blk_done"], 1)

            def biases():
                dve.wait_ge(sm["bias_mm"], 1)
                V.tensor_copy(bk_f[:], ps[:, 6, 0:2 * KC - 1:2])
                V.tensor_copy(bq_f[:], ps[:, 6, 1:2 * KC:2]).then_inc(sm["bias_done"], 1)
                V.tensor_copy(bv_f[:], ps[:, 7, :]).then_inc(sm["bias_done"], 1)

            def bisect(t):
                a = mag[t % 2]
                cur, val, cnt_, m_, r_ = lo[:, 0:1], lo[:, 1:2], lo[:, 2:3], lo[:, 3:4], step[:, 3:4]
                curi, mi = cur.bitcast(I32), m_.bitcast(I32)
                V.memset(curi, 1 << 30)
                V.drain()
                with dve.Fori(0, 31) as b:
                    V.tensor_scalar(junk[:, 0:I], a, cur, None, ALU.is_lt, ALU.add, accum_out=cnt_)
                    V.drain()
                    V.tensor_scalar(val, cnt_, float(KEEP_OUT) - 0.5, None, ALU.is_gt)
                    V.drain()
                    V.tensor_tensor(mi, val, bits[:, bass.ds(b, 1)], ALU.mult)
                    V.drain()
                    V.tensor_tensor(curi, curi, mi, ALU.bitwise_xor)
                    V.drain()
                    V.tensor_tensor(curi, curi, bits[:, bass.ds(b + 1, 1)], ALU.bitwise_xor)
                    V.drain()
                V.tensor_scalar(junk[:, 0:I], a, cur, None, ALU.is_lt, ALU.add, accum_out=cnt_)
                V.drain()
                V.tensor_scalar(r_, cnt_, -1.0, float(KEEP_OUT), ALU.mult, ALU.add)
                V.tensor_scalar(junk[:, 0:I], a, cur, None, ALU.is_equal)
                V.drain()
                V.tensor_tensor_scan(cand, junk[:, 0:I], junk[:, 0:I], 0.0, ALU.add, ALU.bypass)
                V.drain()
                V.scalar_tensor_tensor(cand, cand, r_, junk[:, 0:I], ALU.is_gt, ALU.mult)
                V.drain()
                V.scalar_tensor_tensor(a, a, cur, cand, ALU.is_gt, ALU.add)
                V.memset(thr[:, 0:1], 0.5)
                V.drain()

            def search(t):
                a = mag[t % 2]
                s = msum[:, t % 2:t % 2 + 1]
                dve.wait_ge(sm["mag_done"], t + 1)
                for i, d in enumerate(STEPS):
                    V.tensor_scalar(step[:, i:i + 1], s, -d * SLOPE / I / KEEP_OUT, None, ALU.mult)
                step_(V.tensor_scalar(tcol[:, 0:1], s, GUESS / I, None, ALU.mult))
                for i in range(COUNTS):
                    ins = V.tensor_scalar(junk[:, 0:I], a, tcol[:, i:i + 1], None, ALU.is_lt, ALU.add,
                                          accum_out=ccol[:, i:i + 1])
                    if i == 1 and t + 1 < NT:
                        x_lo(t + 1)
                    if i == 2:
                        product(t)
                    if i < COUNTS - 1:
                        ins = V.scalar_tensor_tensor(tpre[:], step[:, i:i + 1], -float(AIM), tcol[:, i:i + 1],
                                                     ALU.mult, ALU.add)
                    step_(ins)
                    if i < COUNTS - 1:
                        step_(V.scalar_tensor_tensor(tcol[:, i + 1:i + 2], ccol[:, i:i + 1], step[:, i:i + 1], tpre[:],
                                                     ALU.mult, ALU.add))
                step_(V.tensor_scalar(okc[:], ccol[:], float(KEEP_OUT) + 0.5, None, ALU.is_lt))
                V.tensor_tensor(okt[:], okc[:], tcol[:], ALU.mult)
                step_(V.tensor_tensor(okc[:], okc[:], ccol[:], ALU.mult))
                V.tensor_reduce(lo[:, 0:1], okt[:], AX.X, ALU.max)
                step_(V.tensor_reduce(lo[:, 1:2], okc[:], AX.X, ALU.max))
                V.tensor_scalar(lo[:, 2:3], lo[:, 1:2], -1.0, float(KEEP_OUT), ALU.mult, ALU.add)
                step_(V.tensor_scalar(cand, a, lo[:, 0:1], -BIG, ALU.is_lt, ALU.mult))
                step_(V.tensor_tensor(cand, cand, a, ALU.subtract))
                step_(V.max(top[:, 0:8], cand))
                step_(V.match_replace(cand, top[:, 0:8], cand, -2 * BIG))
                step_(V.max(top[:, 8:16], cand))
                j = lo[:, 2:3]
                V.tensor_scalar(flag[:, 0:1], j, float(CANDIDATES) - 0.5, None, ALU.is_gt)
                step_(V.scalar_tensor_tensor(pick[:, 0:16], iota16[:, 0:16], j, top[:, 0:16], ALU.is_equal, ALU.mult))
                step_(V.scalar_tensor_tensor(pick2[:, 0:16], iota16[:, 1:17], j, top[:, 0:16], ALU.is_equal, ALU.mult))
                V.tensor_reduce(thr[:, 1:2], pick[:, 0:16], AX.X, ALU.min)
                step_(V.tensor_reduce(flag[:, 1:2], pick2[:, 0:16], AX.X, ALU.min))
                V.tensor_scalar(thr[:, 0:1], thr[:, 1:2], -1.0, None, ALU.mult)
                step_(V.tensor_tensor(flag[:, 1:2], flag[:, 1:2], thr[:, 1:2], ALU.is_equal))
                V.tensor_tensor(flag[:, 2:3], flag[:, 0:1], flag[:, 1:2], ALU.max).then_inc(sm["bad_seen"], 1)

            def product(t):
                dve.wait_ge(sm["up_mm"], t + 1)
                dve.wait_ge(sm["mag_done"], t + 1)
                V.tensor_tensor(prod[t % 2], prod[t % 2], up_ps[:, 0:I], ALU.mult).then_inc(sm["prod_done"], 1)

            def x_lo(t):
                dve.wait_ge(sm["xT_done"], t + 1)
                V.tensor_tensor(xT2[t % 2][1], M0.rearrange("p (c t) -> p c t", c=KC), xT2[t % 2][0].bitcast(F32),
                                ALU.subtract).then_inc(sm["xT_lo"], 1)

            def apply_mask(t):
                dve.wait_ge(sm["flag_summed"], t + 1)
                bad = dve.value_load(flag_all[0:1, 0:1].bitcast(I32), min_val=0, max_val=0x7fffffff)
                with dve.If(bad != 0):
                    bisect(t)
                dve.wait_ge(sm["prod_done"], t + 1)
                V.scalar_tensor_tensor(prod[t % 2], mag[t % 2], thr[:, 0:1], prod[t % 2],
                                       ALU.is_ge, ALU.mult).then_inc(sm["masked"], 1)

            def norm_stats(y, done):
                step_(V.bn_stats(stats[:], y))
                V.bn_aggr(mv[:], stats[:]).then_inc(sm[done], 1)

            def sum1(t):
                dve.wait_ge(sm["down_mm"], t + 1)
                if t >= 1:
                    dve.wait_ge(sm["x1_done"], t)
                V.tensor_tensor(y1, M0[:, :], xs[:, t, :], ALU.add).then_inc(sm["y1_done"], 1)
                dve.wait_ge(sm["y1_done"], t + 1)
                norm_stats(y1, "v1_done")

            def norm1(t):
                dve.wait_ge(sm["r1_done"], t + 1)
                dve.wait_ge(sm["v1_done"], t + 1)
                V.tensor_scalar(xs[:, t, :], y1, mv[:, 0:1], rstd[:, 0:1], ALU.subtract, ALU.mult).then_inc(sm["x1_done"], 1)

            x_lo(0)
            units_lo(dve, GATE_UP)
            interference()
            search(0)
            apply_mask(0)
            biases()
            for t in range(NT):
                if t + 1 < NT:
                    search(t + 1)
                    sum1(t)
                    apply_mask(t + 1)
                    norm1(t)

            def lo_part(dst2, bank, hi_sem, done, n):
                dve.wait_ge(sm[hi_sem], n)
                V.tensor_tensor(dst2[1], bank.rearrange("p (c t) -> p c t", c=KC), dst2[0].bitcast(F32),
                                ALU.subtract).then_inc(sm[done], 1)

            def row_max(u, g):
                n = 8 * u + g
                dve.wait_ge(sm["score_mm"], n + 1)
                if n >= 2:
                    dve.wait_ge(sm["sub_done"], n - 1)
                sc = score_ps[g % 2].rearrange("p (r k) -> p r k", k=S)
                V.tensor_reduce(smax[:, g % 2, :], sc, AX.X, ALU.max).then_inc(sm["max_done"], 1)

            def less_max(u, g):
                n = 8 * u + g
                dve.wait_ge(sm["max_done"], n + 1)
                if n >= 2:
                    dve.wait_ge(sm["exp_done"], n - 1)
                sc = score_ps[g % 2].rearrange("p (r k) -> p r k", k=S)
                mb = smax[:, g % 2, :].rearrange("p (r a) -> p r a", a=1).to_broadcast([P, 8, S])
                V.tensor_tensor(sub[g % 2].rearrange("p (r k) -> p r k", k=S), sc, mb,
                                ALU.subtract).then_inc(sm["sub_done"], 1)

            def inverse_sum(u, g):
                n = 8 * u + g
                dve.wait_ge(sm["av_mm"], n + 1)
                if n >= 1:
                    dve.wait_ge(sm["av_done"], n)
                av = av_ps[:, 0:8 * W33].rearrange("p (r w) -> p r w", w=W33)
                V.reciprocal(rden[:, :], av[:, :, W33 - 1]).then_inc(sm["rden_done"], 1)

            def normalise(u, g):
                b, c = divmod(g, KC)
                n = 8 * u + g
                dve.wait_ge(sm["rden_done"], n + 1)
                if g == 0 and u >= 1:
                    dve.wait_ge(sm["aT_mm"], u)
                for j in range(2):
                    rows = slice(S * j, S * j + S)
                    src = av_ps[rows, j:j + 2 * (4 * W33 + 2)].rearrange("p (m z) -> p m z", m=2)[:, :, 0:4 * W33]
                    src = src.rearrange("p m (r w) -> p m r w", w=W33)[:, :, :, 0:4 * DK - 3:4]
                    dst = attn_n[rows, b, c * 64:(c + 1) * 64].rearrange("p (r d m) -> p m r d", r=4, m=2)
                    rd = rden[rows, :].rearrange("p (m r a) -> p m r a", m=2, a=1).to_broadcast([S, 2, 4, DK])
                    ins = V.tensor_tensor(dst, src, rd, ALU.mult)
                ins.then_inc(sm["av_done"], 1)

            def biased(w_sem, bank, bias, dst, free, done, p, half_):
                dve.wait_ge(sm[w_sem], 2 * p + half_ + 1)
                if p >= 1:
                    dve.wait_ge(sm[free], 16 * p)
                bb = bias[:, 2 * half_:2 * half_ + 2].rearrange("p (c a) -> p c a", a=1).to_broadcast([P, 2, 2 * P])
                V.tensor_tensor(dst[:, 2 * half_:2 * half_ + 2, :], bank.rearrange("p (c t) -> p c t", c=2), bb,
                                ALU.add).then_inc(sm[done], 1)

            def values_out(k, bank=M1):
                dve.wait_ge(sm["v_mm"], k + 1)
                if k < VXN:
                    dve.wait_ge(sm["vx_zero"], 3 * k + 3)
                else:
                    dve.wait_ge(sm["av_mm"], 8 * (k - VXN + 1))
                for b in range(BT):
                    for h2 in range(2):
                        rows = slice(S * b, S * b + S)
                        fv = lambda z: z.rearrange("p (a h f) -> p a h f", h=2, f=M * DK)[:, :, h2, :]
                        V.tensor_tensor(vx[k % VXN][S * h2:S * h2 + S, b, :, h2, 0:M * DK], fv(bank[rows, :]),
                                        fv(bv_f[rows, :]), ALU.add).then_inc(sm["vx_done"], 1)

            def router_choice(t):
                n = 10 * t
                second = rt[:, 0, 1:2]
                dve.wait_ge(sm["rexp_done"], t + 1)
                V.max(rt[:, 0, :], re[:]).then_inc(sm["router_step"], 1)
                dve.wait_ge(sm["router_step"], n + 1)
                V.tensor_scalar(rt[:, 1, :], re[:], second, None, ALU.is_gt, ALU.add,
                                accum_out=rsum[:, 1:2]).then_inc(sm["router_step"], 1)
                dve.wait_ge(sm["router_step"], n + 2)
                V.tensor_scalar(rt[:, 2, :], re[:], second, None, ALU.is_equal)
                V.tensor_scalar(rsum[:, 1:2], rsum[:, 1:2], -1.0, 2.0, ALU.mult, ALU.add).then_inc(sm["router_step"], 1)
                dve.wait_ge(sm["router_step"], n + 3)
                V.tensor_tensor_scan(rt[:, 3, :], rt[:, 2, :], rt[:, 2, :], 0.0, ALU.add,
                                     ALU.bypass).then_inc(sm["router_step"], 1)
                dve.wait_ge(sm["router_step"], n + 4)
                V.scalar_tensor_tensor(rt[:, 4, :], rt[:, 3, :], rsum[:, 1:2], rt[:, 2, :], ALU.is_le,
                                       ALU.mult).then_inc(sm["router_step"], 1)

            def router_weights(t):
                n = 10 * t
                dve.wait_ge(sm["router_step"], n + 5)
                V.tensor_tensor(rt[:, 5, :], rt[:, 4, :], rt[:, 1, :], ALU.add).then_inc(sm["router_step"], 1)
                dve.wait_ge(sm["router_step"], n + 6)
                V.tensor_tensor(rt[:, 6, :], rt[:, 5, :], re[:], ALU.mult).then_inc(sm["router_step"], 1)
                dve.wait_ge(sm["router_step"], n + 7)
                V.tensor_reduce(rsum[:, 2:3], rt[:, 6, :], AX.X, ALU.add).then_inc(sm["router_step"], 1)
                dve.wait_ge(sm["router_step"], n + 8)
                V.reciprocal(rsum[:, 3:4], rsum[:, 2:3]).then_inc(sm["router_step"], 1)
                dve.wait_ge(sm["router_step"], n + 9)
                V.tensor_scalar(rt[:, 7, :], rt[:, 6, :], rsum[:, 3:4], LORA_SCALING, ALU.mult,
                                ALU.mult).then_inc(sm["router_step"], 1)
                dve.wait_ge(sm["router_step"], n + 10)
                if t >= 1:
                    dve.wait_ge(sm["hwT_mm"], t)
                wb = rt[:, 7, :].rearrange("p (e a) -> p e a", a=1).to_broadcast([P, E, R])
                V.tensor_tensor(hw.rearrange("p (e r) -> p e r", e=E), M1[:, 0:ER].rearrange("p (e r) -> p e r", e=E),
                                wb, ALU.mult).then_inc(sm["hw_done"], 1)

            def pair_lo(k, bank, hi_sem, done, dst2=pairT2):
                dve.wait_ge(sm[hi_sem], k + 1)
                cols = slice((k % 2) * P, (k % 2 + 1) * P)
                V.tensor_tensor(dst2[1][:, :, cols], bank.rearrange("p (c t) -> p c t", c=KC),
                                dst2[0][:, :, cols].bitcast(F32), ALU.subtract).then_inc(sm[done], 1)

            units_lo(dve, REST[0:R0])
            for c in range(IC):
                units_lo(dve, REST[R0 + c:R0 + c + 1])
                if c in (8, 10):
                    pair_lo((c - 8) // 2, M1, "x1T_done", "x1T_lo", firstT2)
            sum1(NT - 1)
            norm1(NT - 1)
            r = R1
            for part in FIRST_PAIR:
                if part == "unit":
                    units_lo(dve, REST[r:r + 1])
                    r += 1
                elif part in ("q_0", "q_1"):
                    biased("q_mm", M1, bq_f, qb, "qx_done", "qb_done", 0, int(part[2]))
                elif part in ("ctx_a", "ctx_b"):
                    pair_lo(int(part == "ctx_b"), M0, "cT_done", "cT_lo")
                elif part in ("k_0", "k_1"):
                    biased("k_mm", (M1, M0)[int(part[2])], bk_f, kb, "kx_done", "kb_done", 0, int(part[2]))
                elif part == "v_a":
                    values_out(0, M1)
                else:
                    values_out(1, M0)
            for u in range(NT + 2):
                t, w = u - 1, u - 2
                attn, rest, last = u < NT, 0 <= t < NT, w >= 0
                p = u // 2 + 1
                even, odd = (attn and p < NT // 2 and u % 2 == j for j in range(2))
                y, yw = yb[:, t % 2, :], yb[:, w % 2, :]
                for g in range(8):
                    n = 8 * u + g
                    if g == 1 and odd:
                        biased("k_mm", M1, bk_f, kb, "kx_done", "kb_done", p, 0)
                    if g == 1 and last:
                        dve.wait_ge(sm["lora_mm"], w + 1)
                        dve.wait_ge(sm["xb2_done"], w + 1)
                        dve.wait_ge(sm["x2_done"], w + 1)
                        V.tensor_tensor(yw, base_ps, xbias[:, 1, :], ALU.add).then_inc(sm["y3_done"], 1)
                    if g == 3 and even:
                        values_out(2 * p)
                    if g == 5 and even:
                        values_out(2 * p + 1)
                    if g == 5 and odd:
                        biased("q_mm", M0, bq_f, qb, "qx_done", "qb_done", p, 0)
                    if g == 6 and odd:
                        biased("q_mm", M0, bq_f, qb, "qx_done", "qb_done", p, 1)
                    if g == 7 and rest:
                        dve.wait_ge(sm["ar_mm"], t + 1)
                        V.tensor_reduce(rsum[:, 0:1], M1[:, ER:ER + E], AX.X, ALU.max, negate=True).then_inc(sm["rmax_done"], 1)
                    if attn:
                        row_max(u, g)
                        less_max(u, g)
                    if g == 1 and even:
                        pair_lo(2 * p, M1, "cT_done", "cT_lo")
                    if g == 2 and odd:
                        pair_lo(2 * p, M1, "x1T_done", "x1T_lo")
                    if g == 3 and odd:
                        pair_lo(2 * p + 1, M1, "x1T_done", "x1T_lo")
                    if g == 4 and rest:
                        dve.wait_ge(sm["r2_done"], t + 1)
                        dve.wait_ge(sm["v2_done"], t + 1)
                        if t >= 1:
                            dve.wait_ge(sm["x2T_mm"], t)
                            dve.wait_ge(sm["xb2_done"], t)
                        V.tensor_scalar(x2, y, mv[:, 0:1], rstd[:, 0:1], ALU.subtract, ALU.mult).then_inc(sm["x2_done"], 1)
                    if g == 7 and rest:
                        router_choice(t)
                    if 2 <= n <= 8 * NT + 1:
                        inverse_sum(*divmod(n - 2, 8))
                        normalise(*divmod(n - 2, 8))
                    if g == 1 and odd:
                        biased("k_mm", M0, bk_f, kb, "kx_done", "kb_done", p, 1)
                    if g == 1 and even:
                        pair_lo(2 * p + 1, M0, "cT_done", "cT_lo")
                    if g == 1 and last:
                        dve.wait_ge(sm["y3_done"], w + 1)
                        norm_stats(yw, "v3_done")
                    if g == 2 and last:
                        dve.wait_ge(sm["r3_done"], w + 1)
                        dve.wait_ge(sm["v3_done"], w + 1)
                        V.tensor_scalar(yw, yw, mv[:, 0:1], rstd[:, 0:1], ALU.subtract, ALU.mult).then_inc(sm["x3_done"], 1)
                    if g == 2 and rest:
                        dve.wait_ge(sm["aT_done"], BT * (t + 1))
                        src = M0.rearrange("p (b a j q) -> p b a j q", b=BT, a=2, j=2)
                        for b in range(BT):
                            qs = slice(b * S, (b + 1) * S)
                            ins = V.tensor_tensor(aT2[1][:, :, :, qs], src[:, b], aT2[0][:, :, :, qs].bitcast(F32), ALU.subtract)
                        ins.then_inc(sm["aT_lo"], 1)
                    if g == 3 and rest:
                        dve.wait_ge(sm["o_mm"], t + 1)
                        dve.wait_ge(sm["xb1_done"], t + 1)
                        if t >= 2:
                            dve.wait_ge(sm[f"out_stored{t % 2}"], 16 * (t // 2))
                        V.tensor_tensor(y, M0[:, :], xbias[:, 0, :], ALU.add).then_inc(sm["y2_done"], 1)
                        dve.wait_ge(sm["y2_done"], t + 1)
                        norm_stats(y, "v2_done")
                    if g == 5 and rest:
                        dve.wait_ge(sm["x2Tf_done"], t + 1)
                        lo_part(x2T2, x2T_bank(t), "x2T_done", "x2T_lo", t + 1)
                    if g == 7 and rest:
                        router_weights(t)


_INS = ['x', 'ctx_4096', 'L0_attn_w_gate', 'L0_attn_w_up', 'L0_attn_w_down', 'L0_xattn_Wq', 'L0_xattn_bq',
        'L0_xattn_Wk', 'L0_xattn_bk', 'L0_xattn_Wv', 'L0_xattn_bv', 'L0_xattn_interference', 'L0_xattn_amp',
        'L0_xattn_Wo', 'L0_xattn_bo', 'L0_ffn_W_base', 'L0_ffn_b_base', 'L0_ffn_W_router', 'L0_ffn_lora_A',
        'L0_ffn_lora_B']


def kernel(**inputs):
    import numpy as _np
    import concourse.bacc as _bacc
    from concourse import mybir as _mybir
    from concourse.bass_utils import run_bass_kernel_spmd as _run

    nc = _bacc.Bacc("TRN2", target_bir_lowering=False, num_devices=1)
    arrays, args = {}, []
    for name in _INS:
        a = _np.ascontiguousarray(inputs[name])
        arrays[f"in_{name}"] = a
        args.append(nc.dram_tensor(f"in_{name}", a.shape, _mybir.dt.from_np(a.dtype), kind="ExternalInput").ap())
    shape = inputs['x'].shape
    args.append(nc.dram_tensor("out", tuple(shape), _mybir.dt.float32, kind="ExternalOutput").ap())
    decoder_kernel(nc, *args)
    r = _run(nc, [arrays], core_ids=[0])
    return r.results[0]["out"]
```
